# Optimizing a Trainium2 kernel written in Bass

```python
import numpy as np
import jax
import jax.numpy as jnp

def _softmax(x, axis=-1):
    return jax.nn.softmax(x, axis=axis)

def _gelu(x):
    return jax.nn.gelu(x, approximate=True)

def _silu(x):
    return jax.nn.silu(x)

def _sigmoid(x):
    return jax.nn.sigmoid(x)

def _layernorm(x, axis=-1, eps=1e-05):
    m = jnp.mean(x, axis=axis, keepdims=True)
    v = jnp.var(x, axis=axis, keepdims=True)
    return (x - m) / jnp.sqrt(v + eps)

def _scatter_add(tgt, idx, src, axis=0):
    return tgt.at[idx].add(src)

def _segment_sum(src, seg, n):
    return jax.ops.segment_sum(src, seg, n)
kernel_name = 'mk_conv_attn_hybrid_d2_conv_nhwc256_r4_6891e7'

def setup_inputs(seed: int=0):
    np.random.seed(seed)
    _w = jnp.asarray

    def _rec_inputs():
        import jax
        import jax.numpy as jnp
        _gk = jax.random.key(seed)
        x = -0.000125 + 0.9999 * jax.random.normal(jax.random.fold_in(_gk, 1), (32, 16, 16, 64), jnp.float32)
        return x
    x = _rec_inputs()

    def _L0_conv_setup():
        import jax, jax.numpy as jnp
        import numpy as np
        from jax import lax
        HEADS, DK, DV, WSZ = (8, 32, 32, 8)
        SCALE = DK ** (-0.5)

        def _conv(t, w):
            return lax.conv_general_dilated(t, w, (1, 1), 'SAME', dimension_numbers=('NHWC', 'HWIO', 'NHWC'))
        key = jax.random.key(seed)
        ks = jax.random.split(key, 8)
        B, H, W, C = (32, 16, 16, 64)
        s1 = 1.0 / np.sqrt(C)
        s3 = 1.0 / np.sqrt(9 * C)
        return {'x': jax.random.normal(ks[0], (B, H, W, C), jnp.float32), 'w_q': jax.random.normal(ks[1], (1, 1, C, DK * HEADS), jnp.float32) * s1, 'w_k': jax.random.normal(ks[2], (1, 1, C, DK * HEADS), jnp.float32) * s1, 'w_v': jax.random.normal(ks[3], (1, 1, C, DV * HEADS), jnp.float32) * s1, 'w_local': jax.random.normal(ks[4], (3, 3, DV * HEADS, DV * HEADS), jnp.float32) * s3, 'b_local': jnp.zeros((DV * HEADS,), jnp.float32), 'w_out': jax.random.normal(ks[5], (1, 1, DV * HEADS, C), jnp.float32) * s1, 'b_out': jnp.zeros((C,), jnp.float32)}
    _L0_conv_all = _L0_conv_setup()
    _L0_conv_in = {k: v for k, v in _L0_conv_all.items() if k in ('w_q', 'w_k', 'w_v', 'w_local', 'b_local', 'w_out', 'b_out')}
    del _L0_conv_all

    def _L1_attn_setup():
        import jax, jax.numpy as jnp
        import numpy as np
        import math
        N_SEQ, L_RES, D_MODEL = (128, 96, 64)
        N_HEAD, C_HEAD = (8, 32)
        EPS = 1e-05
        key = jax.random.key(seed)
        ks = jax.random.split(key, 8)
        s = 1.0 / math.sqrt(D_MODEL)
        return {'m': jax.random.normal(ks[0], (N_SEQ, L_RES, D_MODEL), jnp.float32), 'gamma': jnp.ones((D_MODEL,), jnp.float32), 'beta': jnp.zeros((D_MODEL,), jnp.float32), 'Wq': jax.random.normal(ks[1], (D_MODEL, N_HEAD * C_HEAD), jnp.float32) * s, 'Wk': jax.random.normal(ks[2], (D_MODEL, N_HEAD * C_HEAD), jnp.float32) * s, 'Wv': jax.random.normal(ks[3], (D_MODEL, N_HEAD * C_HEAD), jnp.float32) * s, 'Wg': jax.random.normal(ks[4], (D_MODEL, N_HEAD * C_HEAD), jnp.float32) * s, 'bg': jnp.zeros((N_HEAD * C_HEAD,), jnp.float32), 'Wo': jax.random.normal(ks[5], (N_HEAD * C_HEAD, D_MODEL), jnp.float32) * s, 'bo': jnp.zeros((D_MODEL,), jnp.float32)}
    _L1_attn_all = _L1_attn_setup()
    _L1_attn_in = {k: v for k, v in _L1_attn_all.items() if k in ('gamma', 'beta', 'Wq', 'Wk', 'Wv', 'Wg', 'bg', 'Wo', 'bo')}
    del _L1_attn_all

    def _L1_ffn_setup():
        import jax, jax.numpy as jnp
        import numpy as np
        N_EXPERTS = 8
        TOP_K = 2
        key = jax.random.key(seed)
        ks = jax.random.split(key, 5)
        B, T, C, E, H = (8, 512, 64, 8, 682)
        scale = 1.0 / np.sqrt(C)
        return {'x': jax.random.normal(ks[0], (B, T, C), dtype=jnp.float32), 'router_w': jax.random.normal(ks[1], (E, C), dtype=jnp.float32) * scale, 'w1': jax.random.normal(ks[2], (E, H, C), dtype=jnp.float32) * scale, 'w2': jax.random.normal(ks[3], (E, C, H), dtype=jnp.float32) * (1.0 / np.sqrt(H)), 'w3': jax.random.normal(ks[4], (E, H, C), dtype=jnp.float32) * scale}
    _L1_ffn_all = _L1_ffn_setup()
    _L1_ffn_in = {k: v for k, v in _L1_ffn_all.items() if k in ('router_w', 'w1', 'w2', 'w3')}
    del _L1_ffn_all
    return {'x': x, 'L0_conv_w_q': _L0_conv_in['w_q'], 'L0_conv_w_k': _L0_conv_in['w_k'], 'L0_conv_w_v': _L0_conv_in['w_v'], 'L0_conv_w_local': _L0_conv_in['w_local'], 'L0_conv_b_local': _L0_conv_in['b_local'], 'L0_conv_w_out': _L0_conv_in['w_out'], 'L0_conv_b_out': _L0_conv_in['b_out'], 'L1_attn_gamma': _L1_attn_in['gamma'], 'L1_attn_beta': _L1_attn_in['beta'], 'L1_attn_Wq': _L1_attn_in['Wq'], 'L1_attn_Wk': _L1_attn_in['Wk'], 'L1_attn_Wv': _L1_attn_in['Wv'], 'L1_attn_Wg': _L1_attn_in['Wg'], 'L1_attn_bg': _L1_attn_in['bg'], 'L1_attn_Wo': _L1_attn_in['Wo'], 'L1_attn_bo': _L1_attn_in['bo'], 'L1_ffn_router_w': _L1_ffn_in['router_w'], 'L1_ffn_w1': _L1_ffn_in['w1'], 'L1_ffn_w2': _L1_ffn_in['w2'], 'L1_ffn_w3': _L1_ffn_in['w3']}

def reference(x, L0_conv_w_q, L0_conv_w_k, L0_conv_w_v, L0_conv_w_local, L0_conv_b_local, L0_conv_w_out, L0_conv_b_out, L1_attn_gamma, L1_attn_beta, L1_attn_Wq, L1_attn_Wk, L1_attn_Wv, L1_attn_Wg, L1_attn_bg, L1_attn_Wo, L1_attn_bo, L1_ffn_router_w, L1_ffn_w1, L1_ffn_w2, L1_ffn_w3):
    import jax
    import jax.numpy as jnp

    def _L0_conv_ref(x, w_q, w_k, w_v, w_local, b_local, w_out, b_out):
        import jax, jax.numpy as jnp
        import numpy as np
        from jax import lax
        HEADS, DK, DV, WSZ = (8, 32, 32, 8)
        SCALE = DK ** (-0.5)

        def _conv(t, w):
            return lax.conv_general_dilated(t, w, (1, 1), 'SAME', dimension_numbers=('NHWC', 'HWIO', 'NHWC'))
        B, H, W, C = x.shape
        nx, ny = (H // WSZ, W // WSZ)
        q = _conv(x, w_q)
        k = _conv(x, w_k)
        v = _conv(x, w_v)
        local_out = _conv(v, w_local) + b_local

        def to_windows(t, d):
            t = t.reshape(B, nx, WSZ, ny, WSZ, HEADS, d)
            return t.transpose(0, 1, 3, 5, 2, 4, 6).reshape(B * nx * ny, HEADS, WSZ * WSZ, d)
        qw, kw, vw = (to_windows(q, DK), to_windows(k, DK), to_windows(v, DV))
        dots = jnp.einsum('bhid,bhjd->bhij', qw, kw) * SCALE
        attn = jax.nn.softmax(dots, axis=-1)
        out = jnp.einsum('bhij,bhjd->bhid', attn, vw)
        out = out.reshape(B, nx, ny, HEADS, WSZ, WSZ, DV)
        out = out.transpose(0, 1, 4, 2, 5, 3, 6).reshape(B, H, W, HEADS * DV)
        out = out + local_out
        out = _conv(out, w_out) + b_out
        return out

    def _L1_attn_ref(m, gamma, beta, Wq, Wk, Wv, Wg, bg, Wo, bo):
        import jax, jax.numpy as jnp
        import numpy as np
        import math
        N_SEQ, L_RES, D_MODEL = (128, 96, 64)
        N_HEAD, C_HEAD = (8, 32)
        EPS = 1e-05
        N, L, D = m.shape
        H, C = (N_HEAD, C_HEAD)
        mu = jnp.mean(m, axis=-1, keepdims=True)
        var = jnp.mean(jnp.square(m - mu), axis=-1, keepdims=True)
        mn = (m - mu) * jax.lax.rsqrt(var + EPS) * gamma + beta
        q = (mn @ Wq).reshape(N, L, H, C)
        k = (mn @ Wk).reshape(N, L, H, C)
        v = (mn @ Wv).reshape(N, L, H, C)
        g = jax.nn.sigmoid(mn @ Wg + bg).reshape(N, L, H, C)
        scale = 1.0 / math.sqrt(C) / math.sqrt(L)
        att = jnp.einsum('slhc,tlhc->sth', q, k) * scale
        att = jax.nn.softmax(att, axis=1)
        o = jnp.einsum('sth,tlhc->slhc', att, v) * g
        return o.reshape(N, L, H * C) @ Wo + bo

    def _L1_ffn_ref(x, router_w, w1, w2, w3):
        import jax, jax.numpy as jnp
        import numpy as np
        N_EXPERTS = 8
        TOP_K = 2
        B, T, C = x.shape
        flat = x.reshape(-1, C)
        logits = flat @ router_w.T
        probs = jax.nn.softmax(logits, axis=-1)
        topk_probs, topk_idx = jax.lax.top_k(probs, TOP_K)
        topk_probs = topk_probs / (jnp.sum(topk_probs, axis=-1, keepdims=True) + 1e-09)
        onehot = jax.nn.one_hot(topk_idx, N_EXPERTS, dtype=flat.dtype)
        gates = jnp.einsum('nk,nke->ne', topk_probs, onehot)
        h1 = jnp.einsum('nc,ehc->neh', flat, w1)
        h3 = jnp.einsum('nc,ehc->neh', flat, w3)
        h = jax.nn.silu(h1) * h3
        y = jnp.einsum('neh,ech->nec', h, w2)
        out = jnp.einsum('ne,nec->nc', gates, y)
        return out.reshape(B, T, C)

    def _gn(v, G=32, eps=1e-05):
        B_, H_, W_, C_ = v.shape
        g = v.reshape(B_, H_, W_, G, C_ // G)
        m = jnp.mean(g, axis=(1, 2, 4), keepdims=True)
        s = jnp.var(g, axis=(1, 2, 4), keepdims=True)
        return ((g - m) / jnp.sqrt(s + eps)).reshape(v.shape)

    def _ln_c(v, eps=1e-06):
        m = jnp.mean(v, axis=-1, keepdims=True)
        s = jnp.var(v, axis=-1, keepdims=True)
        return (v - m) / jnp.sqrt(s + eps)

    def _ln_t(v, eps=1e-05):
        m = jnp.mean(v, axis=-1, keepdims=True)
        s = jnp.var(v, axis=-1, keepdims=True)
        return (v - m) / jnp.sqrt(s + eps)

    def _to_tokens(v):
        B_, H_, W_, C_ = v.shape
        return v.reshape(B_, H_ * W_, C_)

    def _from_tokens(t, like):
        return t.reshape(like.shape)
    x = x + _L0_conv_ref(_gn(x), L0_conv_w_q, L0_conv_w_k, L0_conv_w_v, L0_conv_w_local, L0_conv_b_local, L0_conv_w_out, L0_conv_b_out)
    t = _to_tokens(x)
    t = t + _L1_attn_ref(_ln_t(t), L1_attn_gamma, L1_attn_beta, L1_attn_Wq, L1_attn_Wk, L1_attn_Wv, L1_attn_Wg, L1_attn_bg, L1_attn_Wo, L1_attn_bo)
    t = t + _L1_ffn_ref(_ln_t(t), L1_ffn_router_w, L1_ffn_w1, L1_ffn_w2, L1_ffn_w3)
    x = _from_tokens(t, x)
    return x

_drawn_inputs = setup_inputs


def setup_inputs(seed=0):
    import zlib

    import numpy as np

    out = dict(_drawn_inputs(seed))
    spreads = {'L0_conv_b_local': (0.0, 0.1),
     'L0_conv_b_out': (0.0, 0.293),
     'L1_attn_gamma': (1.0, 0.2),
     'L1_attn_beta': (0.0, 0.1),
     'L1_attn_bg': (0.0, 0.8),
     'L1_attn_bo': (0.0, 0.317)}
    factors = {}
    for name, (base, spread) in spreads.items():
        noise = np.random.default_rng([zlib.crc32(name.encode()), seed]).standard_normal(out[name].shape)
        drawn = base * np.exp(spread * noise) if base else spread * noise
        out[name] = jnp.asarray(drawn.astype(out[name].dtype))
    for name, factor in factors.items():
        out[name] = (out[name] * factor).astype(out[name].dtype)
    return out
```

```python
from contextlib import ExitStack

import concourse.bass as bass
from concourse import mybir

F32 = mybir.dt.float32
F32R = mybir.dt.float32r
ALU = mybir.AluOpType
ACT = mybir.ActivationFunctionType
AX = mybir.AxisListType

P = 128
BATCH, SIDE, C = 32, 16, 64
L = SIDE * SIDE
TOK = BATCH * L
TILES = TOK // P
HEADS, D = 8, 32
HC = HEADS * D
WIN = 8
WTOK = WIN * WIN
TAPS = 9
PADDED = SIDE + 2


class Steps:

    def __init__(self, engine, sem, per=0):
        self.engine, self.sem, self.per = engine, sem, per
        self.base, self.n = 0, 0

    def round(self, i):
        assert self.per == 0 or self.n in (0, self.per), (self.n, self.per)
        self.base, self.n = i * self.per, 0

    def did(self, ins):
        ins.then_inc(self.sem, 1)
        self.n += 1

    def settle(self):
        self.engine.wait_ge(self.sem, self.base + self.n)

    def then(self, ins):
        self.did(ins)
        self.settle()


class Shared:
    pass


def allocate(nc, ctx):
    def sb(name, shape, dt=F32):
        return ctx.enter_context(nc.sbuf_tensor(name, shape, dt))

    s = Shared()
    s.ident = sb("ident", [P, P])
    s.x1 = sb("residual", [P, TILES, C])
    s.mean_of_group = sb("mean_of_group", [P, P])
    return s


def constants(nc, s, sem):
    done, filled = sem("constants_done"), sem("constants_filled")
    with nc.Block() as block:
        @block.gpsimd
        def _(eng):
            eng.memset(s.ident[:, :], 0.0).then_inc(filled, 1)
            eng.wait_ge(filled, 1)
            eng.affine_select(out=s.ident[:, :], in_=s.ident[:, :], compare_op=ALU.not_equal, fill=1.0,
                              base=0, pattern=[[-1, P]], channel_multiplier=1).then_inc(done, 1)
            eng.memset(s.mean_of_group[:, :], 1.0 / (2 * L)).then_inc(done, 1)
            eng.wait_ge(done, 2)


def conv_weights(nc, ctx, s, a, sem):
    def sb(name, shape, dt=F32):
        return ctx.enter_context(nc.sbuf_tensor(name, shape, dt))

    s.score_w = [sb(f"score_w{k}", [P, HEADS, P], F32R) for k in range(2)]
    s.value_w = [sb(f"value_w{k}", [P, HEADS * C], F32R) for k in range(2)]
    s.tap_w = sb("tap_w", [P, TAPS, 2, C], F32R)
    s.conv_bias = sb("conv_bias", [P, 1])
    with ExitStack() as own:
        def tmp(name, shape, dt=F32):
            return own.enter_context(nc.sbuf_tensor(name, shape, dt))

        wq, wk, wv = (tmp(f"w{n}_in", [C, HC]) for n in "qkv")
        wout = tmp("wout_in", [P, 2, C])
        wlocal = tmp("wlocal_in", [P, 2, TAPS, HC])
        b_local = tmp("b_local_in", [P, 2])
        b_out = tmp("b_out_in", [C, 1])
        wT = tmp("wT", [P, 3, 2, 2, C])
        folded = tmp("folded", [P, HEADS, P])
        folded_v = tmp("folded_v", [P, HEADS, C])
        tapT = tmp("tapT", [P, TAPS, 2, P])
        tap = tmp("tap", [P, TAPS, C])
        psT = own.enter_context(nc.psum_tensor("psT_w", [P, 6, C], F32))
        psA = [own.enter_context(nc.psum_tensor(f"psA_w{r}", [P, 512], F32)) for r in range(4)]
        psB = own.enter_context(nc.psum_tensor("psB_w", [P, 2, 512], F32))
        loads, w_turned, wT_ready = sem("conv_w_loads"), sem("conv_w_turned"), sem("conv_wT_ready")
        heads_done, taps_done, tap_free = sem("head_products_done"), sem("taps_done"), sem("tap_free")
        tapT_ready, weff_done, weff_copied = sem("tapT_ready"), sem("weff_done"), sem("weff_copied")
        act_did, dve_did = sem("conv_w_act"), sem("conv_w_dve")
        n_loads = 9

        with nc.Block() as block:
            @block.sync
            def _(eng):
                for dst, src in ((wq, a["L0_conv_w_q"]), (wk, a["L0_conv_w_k"]), (wv, a["L0_conv_w_v"])):
                    eng.dma_start(dst[:, :], src.rearrange("a b c n -> (a b c) n")).then_inc(loads, 16)
                eng.dma_start(wout[:, :, :], a["L0_conv_w_out"].rearrange("a b (k p) n -> p (a b k) n", p=P)).then_inc(loads, 16)
                for k in range(2):
                    eng.dma_start(b_local[:, k:k + 1], a["L0_conv_b_local"][k * P:(k + 1) * P].rearrange("(p o) -> p o", o=1)).then_inc(loads, 16)
                eng.dma_start(b_out[:, :], a["L0_conv_b_out"].rearrange("(p o) -> p o", o=1)).then_inc(loads, 16)
                local = a["L0_conv_w_local"].rearrange("u v (k p) n -> k p (u v) n", p=P)
                for k in range(2):
                    eng.dma_start(wlocal[:, k], local[k]).then_inc(loads, 16)

            @block.tensor
            def _(eng):
                eng.wait_ge(loads, 16 * n_loads)
                for i, w in enumerate((wq, wk, wv)):
                    for k in range(2):
                        last = eng.transpose(psT[:, 2 * i + k, :], w[:, k * P:(k + 1) * P], s.ident[0:C, 0:C])
                last.then_inc(w_turned, 1)
                eng.wait_ge(wT_ready, 2)
                for h in range(HEADS):
                    k, r = divmod(h, 4)
                    rows = slice(D * r, D * r + D)
                    q, kk, v = (wT[rows, i, k].rearrange("p a c -> p (a c)") for i in range(3))
                    eng.matmul(psA[r][:, k * P:(k + 1) * P], kk, q, start=True, stop=True)
                    last = eng.matmul(psA[r][:, 2 * P + k * C:2 * P + (k + 1) * C], v, wout[rows, k, :],
                                      start=True, stop=True)
                last.then_inc(heads_done, 1)
                for t in range(TAPS):
                    if t >= 2:
                        eng.wait_ge(tap_free, t - 1)
                    for blk in range(2):
                        for k in range(2):
                            last = eng.matmul(psB[:, t % 2, blk * P:(blk + 1) * P], wlocal[:, k, t, blk * P:(blk + 1) * P],
                                              wT[:, 2, k].rearrange("p a c -> p (a c)"),
                                              start=(k == 0), stop=(k == 1))
                    last.then_inc(taps_done, 1)
                eng.wait_ge(tap_free, TAPS)
                for t in range(TAPS):
                    for blk in range(2):
                        last = eng.matmul(psB[:, t // 8, (t % 8) * C:(t % 8 + 1) * C], tapT[:, t, blk, :], wout[:, blk, :],
                                          start=(blk == 0), stop=(blk == 1))
                last.then_inc(weff_done, 1)
                for k in range(2):
                    last = eng.matmul(psB[0:C, 1, 256:257], wout[:, k, :], b_local[:, k:k + 1], start=(k == 0), stop=(k == 1))
                last.then_inc(weff_done, 1)

            @block.scalar
            def _(eng):
                eng.wait_ge(w_turned, 1)
                turned = psT[:, :, :].rearrange("p (i k) c -> p i k c", k=2)
                for twice in range(2):
                    eng.activation(wT[:, :, :, twice, :], turned, ACT.Copy).then_inc(wT_ready, 1)
                mine = Steps(eng, act_did)
                eng.wait_ge(heads_done, 1)
                for h in range(HEADS):
                    k, r = divmod(h, 4)
                    mine.did(eng.activation(folded[:, h, :], psA[r][:, k * P:(k + 1) * P], ACT.Copy, scale=D ** -0.5))
                    mine.did(eng.activation(folded_v[:, h, :], psA[r][:, 2 * P + k * C:2 * P + (k + 1) * C], ACT.Copy))
                mine.settle()
                mine.did(eng.activation(s.score_w[0][:, :, :], folded[:, :, :], ACT.Copy))
                mine.did(eng.activation(s.value_w[0][:, :], folded_v[:, :, :].rearrange("p h c -> p (h c)"), ACT.Copy))
                eng.wait_ge(weff_copied, 2)
                mine.did(eng.activation(s.tap_w[:, :, 0, :], tap[:, :, :], ACT.Copy))

            @block.vector
            def _(eng):
                for t in range(TAPS):
                    eng.wait_ge(taps_done, t + 1)
                    eng.tensor_copy(tapT[:, t], psB[:, t % 2, 0:2 * P].rearrange("p (b e) -> p b e", b=2)).then_inc(tap_free, 1)
                eng.memset(s.conv_bias[:, :], 0.0).then_inc(dve_did, 1)
                eng.wait_ge(act_did, 2 * HEADS + 2)
                eng.tensor_tensor(s.score_w[1][:, :, :], folded[:, :, :], s.score_w[0][:, :, :].bitcast(F32), ALU.subtract).then_inc(dve_did, 1)
                eng.tensor_tensor(s.value_w[1][:, :], folded_v[:, :, :].rearrange("p h c -> p (h c)"), s.value_w[0][:, :].bitcast(F32), ALU.subtract).then_inc(dve_did, 1)
                eng.wait_ge(weff_done, 2)
                eng.wait_ge(dve_did, 3)
                eng.tensor_tensor(s.conv_bias[0:C, :], psB[0:C, 1, 256:257], b_out[:, :], ALU.add).then_inc(dve_did, 1)
                eng.tensor_copy(tap[:, 0:8, :], psB[:, 0, :].rearrange("p (t c) -> p t c", c=C)).then_inc(weff_copied, 1)
                eng.tensor_copy(tap[:, 8, :], psB[:, 1, 0:C]).then_inc(weff_copied, 1)
                eng.wait_ge(act_did, 2 * HEADS + 3)
                eng.tensor_tensor(s.tap_w[:, :, 1, :], tap[:, :, :], s.tap_w[:, :, 0, :].bitcast(F32), ALU.subtract).then_inc(dve_did, 1)


def group_norm(nc, s, a, sem):
    with ExitStack() as own:
        def tmp(name, shape, dt=F32):
            return own.enter_context(nc.sbuf_tensor(name, shape, dt))

        x = tmp("gn_x", [P, TILES, C])
        sq = tmp("gn_sq", [P, TILES, C])
        groups = C // 2
        mean = tmp("gn_mean", [P, BATCH, groups])
        var = tmp("gn_var", [P, BATCH, groups])
        rstd = tmp("gn_rstd", [P, BATCH, groups])
        fix = tmp("gn_fix", [P, BATCH, groups])
        PARTS = 4
        per = BATCH // PARTS
        ps = own.enter_context(nc.psum_tensor("gn_ps", [P, 2, PARTS, 512], F32))
        x_in, sums, squares, roots = sem("gn_x_in"), sem("gn_sums"), sem("gn_squares"), sem("gn_roots")
        centered, var_ready, normed, hi_ready, dve_did = (sem("gn_centered"), sem("gn_var_ready"), sem("gn_normed"),
                                                          sem("gn_hi_ready"), sem("gn_dve"))
        lo_ready = sem("gn_lo_ready")

        def half(t, h):
            return t[:, h::2, :].rearrange("p b (g e) -> p b g e", e=2)

        def spread(t):
            return t[:, :, :].unsqueeze(3).to_broadcast([P, BATCH, groups, 2])

        with nc.Block() as block:
            def load(eng, ny):
                src = a["x"].rearrange("b (nx r) (ny c) e -> ny r c (b nx) e", nx=2, ny=2)
                for r in range(WIN):
                    p0 = ny * WTOK + r * WIN
                    eng.dma_start(x[p0:p0 + WIN, :, :], src[ny, r]).then_inc(x_in, 16)

            @block.sync
            def _(eng):
                load(eng, 0)

            @block.tensor
            def _(eng):
                eng.wait_ge(x_in, 16 * 2 * WIN)
                for k, t in enumerate((x, sq)):
                    for q in range(PARTS):
                        if k == 1:
                            eng.wait_ge(squares, 1)
                        for h in range(2):
                            first = 2 * q * per + h
                            last = eng.matmul(ps[:, k, q, :], s.mean_of_group[:, :], t[:, first:2 * (q + 1) * per:2, :],
                                              start=(h == 0), stop=(h == 1))
                        last.then_inc(sums, 1)

            @block.scalar
            def _(eng):
                load(eng, 1)
                eng.wait_ge(centered, 2)
                eng.activation(sq[:, :, :], x[:, :, :], ACT.Square).then_inc(squares, 1)
                eng.wait_ge(var_ready, 1)
                eng.activation(fix[:, :, :], var[:, :, :], ACT.Sqrt).then_inc(roots, 1)
                eng.wait_ge(normed, 2)
                eng.activation(s.xhl[:, :, 0:C].bitcast(F32R), sq[:, :, :], ACT.Copy).then_inc(hi_ready, 1)

            @block.vector
            def _(eng):
                mine = Steps(eng, dve_did)
                for q in range(PARTS):
                    eng.wait_ge(sums, q + 1)
                    mine.did(eng.tensor_reduce(mean[:, q * per:(q + 1) * per, :],
                                               ps[:, 0, q, :].rearrange("p (b g e) -> p b g e", g=groups, e=2), AX.X, ALU.add))
                eng.wait_ge(sums, PARTS)
                mine.settle()
                for h in range(2):
                    eng.tensor_tensor(half(x, h), half(x, h), spread(mean), ALU.subtract).then_inc(centered, 1)
                for q in range(PARTS):
                    eng.wait_ge(sums, PARTS + q + 1)
                    mine.did(eng.tensor_reduce(var[:, q * per:(q + 1) * per, :],
                                               ps[:, 1, q, :].rearrange("p (b g e) -> p b g e", g=groups, e=2), AX.X, ALU.add))
                mine.settle()
                eng.tensor_scalar(var[:, :, :], var[:, :, :], 1e-5, None, ALU.add).then_inc(var_ready, 1)
                eng.wait_ge(roots, 1)
                mine.then(eng.reciprocal(rstd[:, :, :], fix[:, :, :]))
                newton(eng, mine, rstd[:, :, :], var[:, :, :], fix[:, :, :])
                for h in range(2):
                    eng.tensor_tensor(half(sq, h), half(x, h), spread(rstd), ALU.mult).then_inc(normed, 1)
                eng.wait_ge(hi_ready, 1)
                eng.wait_ge(normed, 2)
                eng.tensor_tensor(s.xhl[:, :, C:2 * C], sq[:, :, :], s.xhl[:, :, 0:C], ALU.subtract).then_inc(lo_ready, 1)


def newton(eng, mine, y, v, t):
    mine.then(eng.tensor_tensor(t, y, y, ALU.mult))
    mine.then(eng.tensor_tensor(t, t, v, ALU.mult))
    mine.then(eng.tensor_scalar(t, t, -0.5, 1.5, ALU.mult, ALU.add))
    mine.then(eng.tensor_tensor(y, y, t, ALU.mult))


def conv_attention(nc, s, sem):
    with ExitStack() as own:
        def tmp(name, shape, dt=F32):
            return own.enter_context(nc.sbuf_tensor(name, shape, dt))

        W2 = 2
        staged = [tmp(f"staged{i}", [P, 2, P]) for i in range(W2)]
        xw = [tmp(f"xw{i}", [P, 4, 2, WTOK], F32R) for i in range(W2)]
        xp = [tmp(f"xp{i}", [P, PADDED, PADDED], F32R) for i in range(W2)]
        y = tmp("score_side", [P, HEADS, L])
        v = [tmp(f"values{i}", [P, 2, 4, 2, C]) for i in range(W2)]
        shifted = [tmp(f"shifted{i}", [P, HEADS, WTOK]) for i in range(W2)]
        probs = [tmp(f"probs{i}", [P, HEADS, WTOK]) for i in range(W2)]
        probsT = [tmp(f"probsT{i}", [P, 4, P]) for i in range(W2)]
        mx = [tmp(f"win_max{i}", [P, HEADS]) for i in range(W2)]
        den = [tmp(f"win_den{i}", [P, HEADS]) for i in range(W2)]
        rden = [tmp(f"win_rden{i}", [P, HEADS]) for i in range(W2)]

        def bank(name):
            return own.enter_context(nc.psum_tensor(name, [P, 512], F32))

        ps_x, ps_v, ps_t, ps_o = bank("ps_x"), bank("ps_v"), bank("ps_t"), bank("ps_o")
        ps_y = [bank("ps_y0"), bank("ps_y1")]
        ps_s = [bank("ps_s0"), bank("ps_s1")]

        staged_n, turned_n, xw_n, xp_n = sem("staged_n"), sem("turned_n"), sem("xw_n"), sem("xp_n")
        conv_n, convc_n = sem("conv_done_n"), sem("conv_copied_n")
        y_n, ya_n, yd_n = sem("y_done_n"), sem("y_copied_act_n"), sem("y_copied_dve_n")
        v_n, va_n, vd_n = sem("v_done_n"), sem("v_copied_act_n"), sem("v_copied_dve_n")
        s_n, sub_n, exp_n, rden_n, prob_n = sem("scores_n"), sem("shifted_n"), sem("exp_n"), sem("rden_n"), sem("prob_n")
        pt_n, ptc_n, o_n, added_n = sem("probs_turned_n"), sem("probsT_n"), sem("out_n"), sem("added_n")
        dve_n, zero_n = sem("win_dve_n"), sem("border_zero")
        DVE_STEPS = 4

        ROUNDS = BATCH // 2

        with nc.Block() as block:
            @block.gpsimd
            def _(eng):
                for i in range(W2):
                    eng.memset(xp[i][:, :, :].bitcast(F32), 0.0).then_inc(zero_n, 1)

                def front(n, par):
                    if not isinstance(n, int) or n >= 2:
                        eng.wait_ge(turned_n, n - 1)
                    eng.tensor_copy(staged[par][:, :, :], s.xhl[:, bass.ds(2 * n, 2), :]).then_inc(staged_n, 1)

                def back(n, par, more):
                    if more:
                        front(n + 1, 1 - par)
                    for t in range(2):
                        eng.wait_ge(rden_n, 2 * n + t + 1)
                        if not isinstance(n, int) or n >= 1:
                            eng.wait_ge(pt_n, 2 * n + t - 1)
                        eng.tensor_tensor(probs[t][:, :, :], shifted[t][:, :, :],
                                          rden[t][:, :].unsqueeze(2).to_broadcast([P, HEADS, WTOK]), ALU.mult).then_inc(prob_n, 1)

                front(0, 0)
                back(0, 0, True)
                back(1, 1, True)
                with eng.Fori(1, ROUNDS - 1) as i:
                    for par in range(2):
                        back(2 * i + par, par, True)
                for par in range(2):
                    back(BATCH - 2 + par, par, par == 0)

            @block.tensor
            def _(eng):
                def front(n, par):
                    eng.wait_ge(staged_n, n + 1)
                    if not isinstance(n, int) or n >= 1:
                        eng.wait_ge(convc_n, n)
                    for t in range(2):
                        last = eng.transpose(ps_x[:, t * P:(t + 1) * P], staged[par][:, t, :], s.ident[:, :])
                    last.then_inc(turned_n, 1)
                    eng.wait_ge(xw_n, n + 1)
                    for g in range(4):
                        if not isinstance(n, int) or n >= 1 or g >= 2:
                            if g % 2 == 0:
                                eng.wait_ge(ya_n, 2 * n + g // 2)
                            else:
                                eng.wait_ge(yd_n, 2 * n + g // 2)
                        for e in range(2):
                            for k in range(2):
                                last = eng.matmul(ps_y[g % 2][:, e * L:(e + 1) * L], s.score_w[k][:, 2 * g + e, :],
                                                  xw[par][:, :, 0, :], start=(k == 0), stop=(k == 1))
                        last.then_inc(y_n, 1)
                    for w in range(4):
                        if not isinstance(n, int) or n >= 1 or w >= 1:
                            eng.wait_ge(va_n, 4 * n + w)
                            eng.wait_ge(vd_n, 4 * n + w)
                        both = xw[par][:, w].rearrange("p a j -> p (a j)")
                        for k in range(2):
                            last = eng.matmul(ps_v[:, :], both, s.value_w[k][:, :], start=(k == 0), stop=(k == 1))
                        last.then_inc(v_n, 1)
                    eng.wait_ge(xp_n, n + 1)
                    for tap in range(TAPS):
                        u, w = divmod(tap, 3)
                        last = eng.matmul(ps_x[:, 0:L].rearrange("p (r c) -> p r c", r=SIDE),
                                          s.tap_w[:, tap].rearrange("p k c -> p (k c)"),
                                          xp[par][:, u:u + SIDE, w:w + SIDE], start=(tap == 0), stop=(tap == TAPS - 1))
                    last.then_inc(conv_n, 1)

                def back(n, par, more):
                    eng.wait_ge(ya_n, 2 * n + 2)
                    eng.wait_ge(yd_n, 2 * n + 2)
                    for t in range(2):
                        if not isinstance(n, int) or n >= 1:
                            eng.wait_ge(sub_n, 2 * n + t - 1)
                        for w in range(2):
                            cols = slice((2 * t + w) * WTOK, (2 * t + w + 1) * WTOK)
                            last = eng.matmul(ps_s[t][w * WTOK:(w + 1) * WTOK, :], xw[par][:, 2 * t + w, 0, :].bitcast(F32),
                                              y[:, :, cols], start=True, stop=True)
                        last.then_inc(s_n, 1)
                    if more:
                        front(n + 1, 1 - par)
                    for t in range(2):
                        eng.wait_ge(prob_n, 2 * n + t + 1)
                        if not isinstance(n, int) or n >= 1 or t >= 1:
                            eng.wait_ge(ptc_n, 2 * n + t)
                        for g in range(4):
                            last = eng.transpose(ps_t[:, g * P:(g + 1) * P],
                                                 probs[t][:, 2 * g:2 * g + 2, :].rearrange("p h j -> p (h j)"), s.ident[:, :])
                        last.then_inc(pt_n, 1)
                    for t in range(2):
                        eng.wait_ge(ptc_n, 2 * n + t + 1)
                        eng.wait_ge(va_n, 4 * n + 4)
                        eng.wait_ge(vd_n, 4 * n + 4)
                        if not isinstance(n, int) or n >= 1:
                            eng.wait_ge(added_n, 2 * n)
                        for g in range(4):
                            last = eng.matmul(ps_o[:, t * P:(t + 1) * P], v[par][:, t, g].rearrange("p w c -> p (w c)"),
                                              probsT[t][:, g, :], start=(g == 0), stop=(g == 3))
                        last.then_inc(o_n, 1)

                eng.wait_ge(zero_n, W2)
                front(0, 0)
                back(0, 0, True)
                back(1, 1, True)
                with eng.Fori(1, ROUNDS - 1) as i:
                    for par in range(2):
                        back(2 * i + par, par, True)
                for par in range(2):
                    back(BATCH - 2 + par, par, par == 0)

            @block.scalar
            def _(eng):
                def front(n, par):
                    eng.wait_ge(turned_n, n + 1)
                    if not isinstance(n, int) or n >= 2:
                        eng.wait_ge(o_n, 2 * (n - 1))
                    eng.activation(xw[par][:, :, :, :], ps_x[:, 0:L].rearrange("p (w j) -> p w j", w=4).unsqueeze(2).to_broadcast([P, 4, 2, WTOK]),
                                   ACT.Copy).then_inc(xw_n, 1)
                    if not isinstance(n, int) or n >= 1:
                        eng.wait_ge(s_n, 2 * n)
                    for g in (0, 2):
                        eng.wait_ge(y_n, 4 * n + g + 1)
                        eng.activation(y[:, 2 * g:2 * g + 2, :], ps_y[0][:, :].rearrange("p (e l) -> p e l", e=2),
                                       ACT.Copy).then_inc(ya_n, 1)
                    for w in range(4):
                        eng.wait_ge(v_n, 4 * n + w + 1)
                        eng.activation(v[par][0:WTOK, w // 2, :, w % 2, :], ps_v[0:WTOK, :].rearrange("p (g e c) -> p g e c", e=2, c=C)[:, :, 0, :],
                                       ACT.Copy).then_inc(va_n, 1)
                    eng.wait_ge(conv_n, n + 1)
                    eng.activation(s.conv[:, bass.ds(n * L, L)], ps_x[:, 0:L], ACT.Identity, bias=s.conv_bias[:, 0:1]).then_inc(convc_n, 1)

                def back(n, par, more):
                    for t in range(2):
                        eng.wait_ge(sub_n, 2 * n + t + 1)
                        eng.activation(shifted[t][:, :, :], shifted[t][:, :, :], ACT.Exp).then_inc(exp_n, 1)
                    if more:
                        front(n + 1, 1 - par)
                    for t in range(2):
                        eng.wait_ge(pt_n, 2 * n + t + 1)
                        if not isinstance(n, int) or n >= 1:
                            eng.wait_ge(o_n, 2 * n + t - 1)
                        eng.activation(probsT[t][:, :, :], ps_t[:, :].rearrange("p (g i) -> p g i", g=4), ACT.Copy).then_inc(ptc_n, 1)

                front(0, 0)
                back(0, 0, True)
                back(1, 1, True)
                with eng.Fori(1, ROUNDS - 1) as i:
                    for par in range(2):
                        back(2 * i + par, par, True)
                for par in range(2):
                    back(BATCH - 2 + par, par, par == 0)

            @block.vector
            def _(eng):
                def front(n, par):
                    eng.wait_ge(xw_n, n + 1)
                    if not isinstance(n, int) or n >= 2:
                        eng.wait_ge(conv_n, n - 1)
                    for nx in range(2):
                        for ny in range(2):
                            w = 2 * nx + ny
                            last = eng.tensor_copy(xp[par][:, 1 + nx * WIN:1 + (nx + 1) * WIN, 1 + ny * WIN:1 + (ny + 1) * WIN],
                                                   xw[par][:, w, 0, :].bitcast(F32).rearrange("p (r c) -> p r c", r=WIN))
                    last.then_inc(xp_n, 1)
                    if not isinstance(n, int) or n >= 1:
                        eng.wait_ge(s_n, 2 * n)
                    for g in (1, 3):
                        eng.wait_ge(y_n, 4 * n + g + 1)
                        eng.tensor_copy(y[:, 2 * g:2 * g + 2, :], ps_y[1][:, :].rearrange("p (e l) -> p e l", e=2)).then_inc(yd_n, 1)
                    if not isinstance(n, int) or n >= 2:
                        eng.wait_ge(o_n, 2 * (n - 1))
                    for w in range(4):
                        eng.wait_ge(v_n, 4 * n + w + 1)
                        eng.tensor_copy(v[par][WTOK:P, w // 2, :, w % 2, :], ps_v[WTOK:P, :].rearrange("p (g e c) -> p g e c", e=2, c=C)[:, :, 1, :]).then_inc(vd_n, 1)

                def back(n, par, more):
                    for t in range(2):
                        k = 2 * n + t
                        scores = ps_s[t][:, :].rearrange("p (h j) -> p h j", h=HEADS)
                        eng.wait_ge(s_n, k + 1)
                        eng.tensor_reduce(mx[t][:, :], scores, AX.X, ALU.max).then_inc(dve_n, 1)
                        eng.wait_ge(dve_n, 3 * n + t + 1)
                        if not isinstance(n, int) or n >= 1:
                            eng.wait_ge(prob_n, k - 1)
                        eng.tensor_tensor(shifted[t][:, :, :], scores,
                                          mx[t][:, :].unsqueeze(2).to_broadcast([P, HEADS, WTOK]), ALU.subtract).then_inc(sub_n, 1)
                    for t in range(2):
                        k = 2 * n + t
                        eng.wait_ge(exp_n, k + 1)
                        ins = eng.tensor_reduce(den[t][:, :], shifted[t][:, :, :], AX.X, ALU.add)
                        if t == 1:
                            ins.then_inc(dve_n, 1)
                    eng.wait_ge(dve_n, 3 * n + 3)
                    for t in range(2):
                        eng.reciprocal(rden[t][:, :], den[t][:, :]).then_inc(rden_n, 1)
                    if more:
                        front(n + 1, 1 - par)
                    eng.wait_ge(convc_n, n + 1)
                    for t in range(2):
                        eng.wait_ge(o_n, 2 * n + 2)
                        for w in range(2):
                            rows = slice(w * C, (w + 1) * C)
                            at = n * L + t * WIN * SIDE + w * WIN
                            own_part = s.conv[rows, bass.ds(n * L + t * WIN * SIDE, WIN * SIDE)].rearrange(
                                "p (r c) -> p r c", c=SIDE)[:, :, w * WIN:(w + 1) * WIN]
                            last = eng.tensor_tensor(own_part, own_part,
                                                     ps_o[rows, t * P + w * WTOK:t * P + (w + 1) * WTOK].rearrange("p (r c) -> p r c", r=WIN),
                                                     ALU.add)
                        last.then_inc(added_n, 1)

                front(0, 0)
                back(0, 0, True)
                back(1, 1, True)
                with eng.Fori(1, ROUNDS - 1) as i:
                    for par in range(2):
                        back(2 * i + par, par, True)
                for par in range(2):
                    back(BATCH - 2 + par, par, par == 0)


def axial_weights(nc, s, a, sem):
    with ExitStack() as own:
        def tmp(name, shape, dt=F32):
            return own.enter_context(nc.sbuf_tensor(name, shape, dt))

        raw = tmp("proj_raw", [P, 4, HC])
        padded = sem("wo_padded")
        loads, kept, scaled, split_n = sem("proj_loads"), sem("kept_loads"), sem("proj_scaled"), sem("proj_split")
        with nc.Block() as block:
            @block.sync
            def _(eng):
                for i, n in enumerate(("q", "k", "g", "v")):
                    for half in range(2):
                        eng.dma_start(raw[half * C:(half + 1) * C, i, :], a[f"L1_attn_W{n}"]).then_inc(loads, 16)
                x = a["x"].rearrange("b (h4 r) c e -> b (h4 r c) e", r=1).rearrange("b (g q) e -> q b g e", q=4)
                for q in range(4):
                    eng.dma_start(s.x1[q * BATCH:(q + 1) * BATCH, :, :], x[q]).then_inc(kept, 16)
                eng.wait_ge(padded, 2)
                eng.dma_start(s.wo[:, :, 0:C], a["L1_attn_Wo"].rearrange("(k p) n -> p k n", p=P)).then_inc(kept, 16)
                eng.dma_start(s.bo[0:C, :], a["L1_attn_bo"].rearrange("(p o) -> p o", o=1)).then_inc(kept, 16)
                for k in range(2):
                    eng.dma_start(s.bg[:, k:k + 1], a["L1_attn_bg"][k * P:(k + 1) * P].rearrange("(p o) -> p o", o=1)).then_inc(kept, 16)
                eng.dma_start(s.gamma[:, :], a["L1_attn_gamma"].partition_broadcast(P)).then_inc(kept, 16)
                eng.dma_start(s.beta[:, :], a["L1_attn_beta"].partition_broadcast(P)).then_inc(kept, 16)
                eng.wait_ge(kept, 16 * 10)

            @block.gpsimd
            def _(eng):
                eng.memset(s.wo[:, :, :], 0.0).then_inc(padded, 1)
                eng.memset(s.bo[:, :], 0.0).then_inc(padded, 1)

            @block.scalar
            def _(eng):
                eng.wait_ge(scaled, 1)
                eng.activation(s.proj[0][:, :, :], raw[:, :, :], ACT.Copy).then_inc(split_n, 1)

            @block.vector
            def _(eng):
                eng.wait_ge(loads, 16 * 8)
                eng.tensor_scalar(raw[:, 0, :], raw[:, 0, :], D ** -0.5 * L ** -0.5, None, ALU.mult).then_inc(scaled, 1)
                eng.wait_ge(split_n, 1)
                eng.tensor_tensor(s.proj[1][:, :, :], raw[:, :, :], s.proj[0][:, :, :].bitcast(F32), ALU.subtract).then_inc(split_n, 1)


GROUP = 4
GTOK = GROUP * P
GROUPS = TILES // GROUP


def sym(n):
    return not isinstance(n, int)


def layer_norm(eng, mine, x, b, roots_n, root_wait, sq_n, sq_wait, var_n, center_n, twice):
    wide = [P, GROUP, C]
    mine.then(eng.tensor_reduce(b.sum[:, :], x, AX.X, ALU.add))
    mine.then(eng.tensor_scalar(b.sum[:, :], b.sum[:, :], 1.0 / C, None, ALU.mult))
    eng.tensor_tensor(b.xc[:, :, :], x, b.sum[:, :].unsqueeze(2).to_broadcast(wide), ALU.subtract).then_inc(center_n, 1)
    eng.wait_ge(sq_n, sq_wait)
    mine.then(eng.tensor_reduce(b.var[:, :], b.sq[:, :, :], AX.X, ALU.add))
    eps = 1e-5
    if twice:
        ins = eng.tensor_scalar(b.var[:, :], b.var[:, :], (1 + eps) / C, eps * eps, ALU.mult, ALU.add)
    else:
        ins = eng.tensor_scalar(b.var[:, :], b.var[:, :], 1.0 / C, eps, ALU.mult, ALU.add)
    ins.then_inc(var_n, 1)
    eng.wait_ge(roots_n, root_wait)
    mine.then(eng.reciprocal(b.rstd[:, :], b.root[:, :]))
    newton(eng, mine, b.rstd[:, :], b.var[:, :], b.root[:, :])
    eng.wait_ge(center_n, sq_wait)
    mine.then(eng.tensor_tensor(b.xc[:, :, :], b.xc[:, :, :], b.rstd[:, :].unsqueeze(2).to_broadcast(wide), ALU.mult))


LN_STEPS = 9


class NormBuffers:

    def __init__(self, tmp, name):
        self.x = tmp(f"{name}_x", [P, GROUP, C])
        self.sum, self.var = tmp(f"{name}_sum", [P, GROUP]), tmp(f"{name}_var", [P, GROUP])
        self.rstd, self.root = tmp(f"{name}_rstd", [P, GROUP]), tmp(f"{name}_root", [P, GROUP])
        self.xc, self.sq = tmp(f"{name}_xc", [P, GROUP, C]), tmp(f"{name}_sq", [P, GROUP, C])
        self.hl = tmp(f"{name}_hl", [P, GROUP, P])


def axial_scores(nc, s, sem):
    with ExitStack() as own:
        def tmp(name, shape, dt=F32):
            return own.enter_context(nc.sbuf_tensor(name, shape, dt))

        b = NormBuffers(tmp, "ax")
        staged = [tmp(f"ax_staged{i}", [P, 16, BATCH]) for i in range(2)]
        qk = [tmp(f"ax_qk{i}", [P, 4, GROUP, BATCH, 4]) for i in range(2)]
        qkl = [tmp(f"ax_qkl{i}", [P, 4, 4, BATCH, 4]) for i in range(2)]
        zero = tmp("ax_zero", [P, 2 * P])
        att = tmp("ax_att", [P, 2, BATCH])
        attT = tmp("ax_attT", [P, 2, BATCH])
        top = tmp("ax_top", [P, 2])
        den = tmp("ax_den", [P, 2])

        def bank(name):
            return own.enter_context(nc.psum_tensor(name, [P, 512], F32))

        ps_f, ps_x, ps_a = bank("ax_ps_f"), bank("ax_ps_x"), bank("ax_ps_a")
        ps_qk = [bank(f"ax_ps_qk{i}") for i in range(4)]
        staged_n, f_n, res_n, center_n, sq_n, var_n, root_n = (sem("ax_staged_n"), sem("ax_f_n"), sem("ax_res_n"), sem("ax_center_n"),
                                                               sem("ax_sq_n"), sem("ax_var_n"), sem("ax_root_n"))
        z_n, hi_n, lo_n, x_n, xt_n, dve_n = sem("ax_z_n"), sem("ax_hi_n"), sem("ax_lo_n"), sem("ax_x_n"), sem("ax_xt_n"), sem("ax_dve_n")
        qk_n, q_c, k_c, moved_n, att_n, zero_n = (sem("ax_qk_n"), sem("ax_q_copied"), sem("ax_k_copied"),
                                                  [sem(f"ax_moved{i}") for i in range(2)], sem("ax_att_n"), sem("ax_zero_n"))
        top_n, exp_n, kept_n = sem("ax_top_n"), sem("ax_exp_n"), sem("ax_kept_n")
        MOVES = 16

        def run(eng, body):
            with eng.Fori(0, GROUPS // 2) as i:
                for par in range(2):
                    body(2 * i + par, par)

        with nc.Block() as block:
            @block.gpsimd
            def _(eng):
                eng.memset(zero[:, :], 0.0).then_inc(zero_n, 1)
                eng.memset(s.att_w[:, :, :], 0.0).then_inc(zero_n, 1)
                eng.wait_ge(zero_n, 2)
                by_position = s.conv[:, :].rearrange("p (s l) -> p l s", l=L)

                def body(g, par):
                    eng.wait_ge(f_n, g)
                    eng.tensor_copy(staged[par][:, :, :], by_position[:, bass.ds(16 * g, 16), :]).then_inc(staged_n, 1)
                    eng.wait_ge(res_n, g + 1)
                    eng.tensor_copy(s.x1[:, bass.ds(g * GROUP, GROUP), :], b.x[:, :, :]).then_inc(kept_n, 1)
                run(eng, body)
                eng.wait_ge(kept_n, GROUPS)

            @block.sync
            def _(eng):
                def body(g, par):
                    eng.wait_ge(q_c, 2 * g + 2)
                    eng.wait_ge(k_c, 2 * g + 2)
                    eng.wait_ge(att_n, g - par)
                    for h in range(4):
                        for t in range(GROUP):
                            eng.dma_start(qkl[par][t * D:(t + 1) * D, :, h, :, :].rearrange("p k s l -> p k (s l)"),
                                          qk[par][h * D:(h + 1) * D, :, t, :, :].rearrange("p k s l -> p k (s l)")).then_inc(moved_n[par], 16)
                run(eng, body)

            @block.tensor
            def _(eng):
                eng.wait_ge(zero_n, 2)
                eng.matmul(ps_a[:, 0:2 * P], zero[:, 0:P], zero[:, :], start=True, stop=False, skip_group_check=True)

                def body(g, par):
                    eng.wait_ge(staged_n, g + 1)
                    eng.wait_ge(res_n, g)
                    for t in range(GROUP):
                        last = eng.transpose(ps_f[:, t * P:(t + 1) * P],
                                             staged[par][:, 4 * t:4 * t + 4, :].rearrange("p l s -> p (l s)"), s.ident[:, :])
                    last.then_inc(f_n, 1)
                    eng.wait_ge(lo_n, g + 1)
                    eng.wait_ge(hi_n, g + 1)
                    for t in range(GROUP):
                        last = eng.transpose(ps_x[:, t * P:(t + 1) * P], b.hl[:, t, :], s.ident[:, :])
                    last.then_inc(x_n, 1)
                    eng.wait_ge(xt_n, g + 1)
                    eng.wait_ge(q_c, 2 * g)
                    eng.wait_ge(k_c, 2 * g)
                    for m in range(4):
                        for k in range(2):
                            last = eng.matmul(ps_qk[m][:, :], s.proj[k][:, m // 2, (m % 2) * P:(m % 2 + 1) * P],
                                              s.xt[:, bass.ds(g * GTOK, GTOK)], start=(k == 0), stop=(k == 1))
                        last.then_inc(qk_n, 1)

                def scores(half_round, par):
                    eng.wait_ge(moved_n[par], 16 * MOVES * (half_round + 1))
                    for l in range(4):
                        for k in range(2):
                            last = eng.matmul(ps_a[:, k * P:(k + 1) * P], qkl[par][:, k].rearrange("p h s l -> p (h s) l")[:, :, l],
                                              qkl[par][:, 2 + k].rearrange("p h s l -> p (h s) l")[:, :, l],
                                              start=False, stop=False, skip_group_check=True)
                    last.then_inc(att_n, 1)

                with eng.Fori(0, GROUPS // 2) as i:
                    for par in range(2):
                        body(2 * i + par, par)
                        if par == 1:
                            scores(i, 0)
                            scores(i, 1)
                eng.matmul(ps_a[:, 0:2 * P], zero[:, 0:P], zero[:, :], start=False, stop=True, skip_group_check=True).then_inc(att_n, 1)

            @block.scalar
            def _(eng):
                def body(g, par):
                    eng.wait_ge(center_n, g + 1)
                    eng.activation(b.sq[:, :, :], b.xc[:, :, :], ACT.Square).then_inc(sq_n, 1)
                    eng.wait_ge(var_n, g + 1)
                    eng.activation(b.root[:, :], b.var[:, :], ACT.Sqrt).then_inc(root_n, 1)
                    eng.wait_ge(z_n, g + 1)
                    eng.wait_ge(x_n, g)
                    eng.activation(b.hl[:, :, 0:C].bitcast(F32R), b.xc[:, :, :], ACT.Copy).then_inc(hi_n, 1)
                    eng.wait_ge(x_n, g + 1)
                    eng.activation(s.xt[:, bass.ds(g * GTOK, GTOK)], ps_x[:, :], ACT.Copy).then_inc(xt_n, 1)
                    for m in range(2):
                        eng.wait_ge(qk_n, 4 * g + m + 1)
                        if m == 0:
                            eng.wait_ge(att_n, g - par)
                        eng.activation(qk[par][:, m].rearrange("p t s l -> p t l s"),
                                       ps_qk[m][:, :].rearrange("p (t l s) -> p t l s", t=GROUP, l=4), ACT.Copy).then_inc(q_c, 1)
                run(eng, body)
                eng.wait_ge(top_n, 1)
                eng.activation(att[:, :, :], att[:, :, :], ACT.Exp).then_inc(exp_n, 1)

            @block.vector
            def _(eng):
                mine = Steps(eng, dve_n, 1 + LN_STEPS + 1)

                def body(g, par):
                    mine.round(g)
                    tiles = s.x1[:, bass.ds(g * GROUP, GROUP), :]
                    folded = ps_f[:, :].rearrange("p (t k c) -> p t k c", t=GROUP, k=2)
                    eng.wait_ge(f_n, g + 1)
                    mine.then(eng.tensor_tensor(tiles, tiles, folded[:, :, 0, :], ALU.add))
                    eng.wait_ge(kept_n, g)
                    eng.tensor_tensor(b.x[:, :, :], tiles, folded[:, :, 1, :], ALU.add).then_inc(res_n, 1)
                    eng.wait_ge(lo_n, g)
                    eng.wait_ge(res_n, g + 1)
                    layer_norm(eng, mine, b.x[:, :, :], b, root_n, g + 1, sq_n, g + 1, var_n, center_n, True)
                    wide = [P, GROUP, C]
                    mine.then(eng.tensor_tensor(b.xc[:, :, :], b.xc[:, :, :], s.gamma[:, :].unsqueeze(1).to_broadcast(wide), ALU.mult))
                    eng.tensor_tensor(b.xc[:, :, :], b.xc[:, :, :], s.beta[:, :].unsqueeze(1).to_broadcast(wide), ALU.add).then_inc(z_n, 1)
                    eng.wait_ge(hi_n, g + 1)
                    eng.wait_ge(z_n, g + 1)
                    eng.tensor_tensor(b.hl[:, :, C:2 * C], b.xc[:, :, :], b.hl[:, :, 0:C], ALU.subtract).then_inc(lo_n, 1)
                    for m in range(2):
                        eng.wait_ge(qk_n, 4 * g + m + 3)
                        if m == 0:
                            eng.wait_ge(att_n, g - par)
                        eng.tensor_copy(qk[par][:, 2 + m].rearrange("p t s l -> p t l s"),
                                        ps_qk[2 + m][:, :].rearrange("p (t l s) -> p t l s", t=GROUP, l=4)).then_inc(k_c, 1)
                run(eng, body)
                mine = Steps(eng, sem("ax_softmax_dve"))
                eng.wait_ge(att_n, GROUPS + 1)
                for h in range(4):
                    rows = slice(h * BATCH, (h + 1) * BATCH)
                    mine.did(eng.tensor_copy(att[rows, :, :], ps_a[rows, 0:2 * P].rearrange("p (k n) -> p k n", k=2)[:, :, rows]))
                mine.settle()
                mine.then(eng.tensor_reduce(top[:, :], att[:, :, :], AX.X, ALU.max))
                eng.tensor_tensor(att[:, :, :], att[:, :, :], top[:, :].unsqueeze(2).to_broadcast([P, 2, BATCH]), ALU.subtract).then_inc(top_n, 1)
                eng.wait_ge(exp_n, 1)
                mine.then(eng.tensor_reduce(den[:, :], att[:, :, :], AX.X, ALU.add))
                mine.then(eng.reciprocal(top[:, :], den[:, :]))
                mine.then(eng.tensor_tensor(att[:, :, :], att[:, :, :], top[:, :].unsqueeze(2).to_broadcast([P, 2, BATCH]), ALU.mult))
                mine.then(eng.transpose(attT[:, :, :].rearrange("p k s -> p (k s)"), att[:, :, :].rearrange("p k s -> p (k s)")))
                for h in range(4):
                    for q in range(4):
                        rows = slice(q * BATCH, (q + 1) * BATCH)
                        mine.did(eng.tensor_copy(s.att_w[rows, h::4, rows], attT[h * BATCH:(h + 1) * BATCH, :, :]))
                mine.settle()


def axial_values(nc, s, sem):
    with ExitStack() as own:
        def tmp(name, shape, dt=F32):
            return own.enter_context(nc.sbuf_tensor(name, shape, dt))

        xs = [tmp(f"av_x{i}", [P, GTOK], F32R) for i in range(2)]
        v = [tmp(f"av_v{i}", [P, GROUP, HC]) for i in range(2)]
        gate = [tmp(f"av_gate{i}", [P, 2, GTOK]) for i in range(2)]
        o = [tmp(f"av_o{i}", [P, GROUP, HC]) for i in range(2)]
        og = [tmp(f"av_og{i}", [P, 2, GTOK]) for i in range(2)]
        ao = [tmp(f"av_ao{i}", [P, GTOK]) for i in range(2)]

        def bank(name):
            return own.enter_context(nc.psum_tensor(name, [P, 512], F32))

        ps_v, ps_o, ps_t = ([bank(f"av_ps_{n}{i}") for i in range(2)] for n in "vot")
        ps_w, ps_r = bank("av_ps_w"), bank("av_ps_r")
        xs_n, v_n, v_c, g_n, g_c, o_n, o_c = (sem(f"av_{n}") for n in ("x_staged", "v_done", "v_copied", "g_done", "g_copied", "o_done", "o_copied"))
        t_n, og_n, w_n, ao_n, r_n, res_n = (sem(f"av_{n}") for n in ("turned", "gated", "projected", "ao_copied", "ao_turned", "residual"))

        def run(eng, body):
            with eng.Fori(0, GROUPS // 2) as i:
                for par in range(2):
                    body(2 * i + par, par)

        with nc.Block() as block:
            @block.gpsimd
            def _(eng):
                def body(g, par):
                    eng.wait_ge(g_n, 2 * (g - par))
                    eng.tensor_copy(xs[par][:, :], s.xt[:, bass.ds(g * GTOK, GTOK)].bitcast(F32)).then_inc(xs_n, 1)
                run(eng, body)

            @block.tensor
            def _(eng):
                def body(g, par):
                    eng.wait_ge(xs_n, g + 1)
                    eng.wait_ge(g_c, 2 * g)
                    for t in range(GROUP):
                        for k in range(2):
                            last = eng.matmul(ps_v[t // 2][:, (t % 2) * HC:(t % 2 + 1) * HC], xs[par][:, t * P:(t + 1) * P],
                                              s.proj[k][:, 3, :], start=(k == 0), stop=(k == 1))
                        if t % 2:
                            last.then_inc(v_n, 1)
                    for m in range(2):
                        eng.wait_ge(v_c, 2 * g + m + 1)
                        for k in range(2):
                            last = eng.matmul(ps_v[m][:, :], s.proj[k][:, 2, m * P:(m + 1) * P], xs[par][:, :],
                                              start=(k == 0), stop=(k == 1))
                        last.then_inc(g_n, 1)
                    eng.wait_ge(v_c, 2 * g + 2)
                    eng.wait_ge(o_c, 2 * g)
                    for h in range(HEADS):
                        last = eng.matmul(ps_o[h // 4][:, (h % 4) * P:(h % 4 + 1) * P].rearrange("p (t c) -> p t c", t=GROUP),
                                          s.att_w[:, h, :], v[par][:, :, h * D:(h + 1) * D], start=True, stop=True)
                        if h % 4 == 3:
                            last.then_inc(o_n, 1)
                    eng.wait_ge(o_c, 2 * g + 2)
                    eng.wait_ge(og_n, 2 * g)
                    for m in range(2):
                        for t in range(GROUP):
                            last = eng.transpose(ps_t[m][:, t * P:(t + 1) * P], o[par][:, t, m * P:(m + 1) * P], s.ident[:, :])
                        last.then_inc(t_n, 1)
                    eng.wait_ge(og_n, 2 * g + 2)
                    eng.wait_ge(ao_n, g)
                    for m in range(2):
                        last = eng.matmul(ps_w[:, :], s.wo[:, m, :], og[par][:, m, :], start=(m == 0), stop=(m == 1))
                    last.then_inc(w_n, 1)
                    eng.wait_ge(ao_n, g + 1)
                    eng.wait_ge(res_n, g)
                    for t in range(GROUP):
                        last = eng.transpose(ps_r[:, t * P:(t + 1) * P], ao[par][:, t * P:(t + 1) * P], s.ident[:, :])
                    last.then_inc(r_n, 1)
                run(eng, body)

            @block.scalar
            def _(eng):
                def body(g, par):
                    eng.wait_ge(t_n, 2 * (g - par))
                    eng.wait_ge(og_n, 2 * (g - par))
                    for m in range(2):
                        eng.wait_ge(g_n, 2 * g + m + 1)
                        eng.activation(gate[par][:, m, :], ps_v[m][:, :], ACT.Sigmoid, bias=s.bg[:, m:m + 1]).then_inc(g_c, 1)
                    for m in range(2):
                        eng.wait_ge(o_n, 2 * g + m + 1)
                        eng.activation(o[par][:, :, m * P:(m + 1) * P].rearrange("p t (h c) -> p h t c", c=D),
                                       ps_o[m][:, :].rearrange("p (h t c) -> p h t c", h=4, t=GROUP), ACT.Copy).then_inc(o_c, 1)
                    eng.wait_ge(w_n, g + 1)
                    eng.activation(ao[par][:, :], ps_w[:, :], ACT.Identity, bias=s.bo[:, 0:1]).then_inc(ao_n, 1)
                run(eng, body)

            @block.vector
            def _(eng):
                def body(g, par):
                    for m in range(2):
                        eng.wait_ge(v_n, 2 * g + m + 1)
                        if m == 0:
                            eng.wait_ge(o_n, 2 * (g - par))
                        eng.tensor_copy(v[par][:, 2 * m:2 * m + 2, :], ps_v[m][:, :].rearrange("p (t n) -> p t n", t=2)).then_inc(v_c, 1)
                    for m in range(2):
                        eng.wait_ge(t_n, 2 * g + m + 1)
                        eng.wait_ge(g_c, 2 * g + m + 1)
                        if m == 0:
                            eng.wait_ge(w_n, g - par)
                        eng.tensor_tensor(og[par][:, m, :], ps_t[m][:, :], gate[par][:, m, :], ALU.mult).then_inc(og_n, 1)
                    eng.wait_ge(r_n, g + 1)
                    tiles = s.x1[:, bass.ds(g * GROUP, GROUP), :]
                    eng.tensor_tensor(tiles, tiles, ps_r[:, :].rearrange("p (t c) -> p t c", c=P)[:, :, 0:C], ALU.add).then_inc(res_n, 1)
                run(eng, body)


EXPERTS, HID = 8, 682
HCHUNK, HCHUNKS = 114, 6
HPAD = HCHUNK * HCHUNKS
SLOT = 256
FTILES = 2 * TOK // SLOT + EXPERTS - 1
SLOTS = FTILES * SLOT
EXPERT_ROWS = TOK // SLOT


def expert_weights(nc, s, a, sem):
    with ExitStack() as own:
        def tmp(name, shape, dt=F32):
            return own.enter_context(nc.sbuf_tensor(name, shape, dt))

        w13 = [tmp(f"w13_in{i}", [HCHUNK, 2, HCHUNKS, 2, C]) for i in range(2)]
        w2 = [tmp(f"w2_in{i}", [C, HPAD]) for i in range(2)]
        ps = [own.enter_context(nc.psum_tensor(f"ew_ps{i}", [P, 512], F32)) for i in range(6)]
        zeroed, in_n, turned, hi_n, lo_n, w2_n, rw_n = (sem(f"ew_{n}") for n in ("zeroed", "loads", "turned", "hi", "lo", "w2", "router"))
        in_n = [in_n, sem("ew_loads_odd")]
        LOADS = 2 * 2 * 2 + 1
        HALF = HCHUNKS // 2

        with nc.Block() as block:
            @block.gpsimd
            def _(eng):
                for i in range(2):
                    eng.memset(w13[i][:, :, HCHUNKS - 1], 0.0).then_inc(zeroed, 1)
                    eng.memset(w2[i][:, HID:HPAD], 0.0).then_inc(zeroed, 1)
                eng.memset(s.w2[:, :, :, C:P], 0.0).then_inc(zeroed, 1)

            @block.sync
            def _(eng):
                eng.wait_ge(zeroed, 4)
                whole = (HCHUNKS - 1) * HCHUNK
                for e in range(EXPERTS):
                    i = e % 2
                    if e >= 2:
                        eng.wait_ge(turned, 5 * (e - 1))
                    for m, name in enumerate(("w1", "w3")):
                        w = a[f"L1_ffn_{name}"][e]
                        for twice in range(2):
                            eng.dma_start(w13[i][:, m, 0:HCHUNKS - 1, twice, :],
                                          w[0:whole, :].rearrange("(k p) c -> p k c", p=HCHUNK)).then_inc(in_n[i], 16)
                            eng.dma_start(w13[i][0:HID - whole, m, HCHUNKS - 1, twice, :], w[whole:HID, :]).then_inc(in_n[i], 16)
                    eng.dma_start(w2[i][:, 0:HID], a["L1_ffn_w2"][e]).then_inc(in_n[i], 16)
                for half in range(2):
                    eng.dma_start(s.router[half * C:(half + 1) * C, :], a["L1_ffn_router_w"].rearrange("e c -> c e"),
                                  allow_slow_non_contiguous=True).then_inc(rw_n, 16)
                eng.wait_ge(rw_n, 32)

            @block.tensor
            def _(eng):
                for e in range(EXPERTS):
                    i = e % 2
                    eng.wait_ge(in_n[i], 16 * LOADS * (e // 2 + 1))
                    for part in range(4):
                        m, half = divmod(part, 2)
                        if e >= 1:
                            eng.wait_ge(lo_n, 4 * (e - 1) + part + 1)
                        for k in range(HALF):
                            last = eng.transpose(ps[part][:, k * HCHUNK:(k + 1) * HCHUNK],
                                                 w13[i][:, m, half * HALF + k].rearrange("p a c -> p (a c)"), s.ident[0:HCHUNK, 0:HCHUNK])
                        last.then_inc(turned, 1)
                    if e >= 2:
                        eng.wait_ge(w2_n, e - 1)
                    for k in range(HCHUNKS):
                        last = eng.transpose(ps[4 + i][0:HCHUNK, k * C:(k + 1) * C], w2[i][:, k * HCHUNK:(k + 1) * HCHUNK], s.ident[0:C, 0:C])
                    last.then_inc(turned, 1)

            def halves(w, e, m, half):
                return w[:, e, m, half * HALF * HCHUNK:(half + 1) * HALF * HCHUNK]

            @block.scalar
            def _(eng):
                for e in range(EXPERTS):
                    for part in range(4):
                        eng.wait_ge(turned, 5 * e + part + 1)
                        eng.activation(halves(s.w13[0], e, *divmod(part, 2)), ps[part][:, 0:HALF * HCHUNK], ACT.Copy).then_inc(hi_n, 1)

            @block.vector
            def _(eng):
                for e in range(EXPERTS):
                    for part in range(4):
                        eng.wait_ge(hi_n, 4 * e + part + 1)
                        eng.tensor_tensor(halves(s.w13[1], e, *divmod(part, 2)), ps[part][:, 0:HALF * HCHUNK],
                                          halves(s.w13[0], e, *divmod(part, 2)).bitcast(F32), ALU.subtract).then_inc(lo_n, 1)
                    eng.wait_ge(turned, 5 * e + 5)
                    if e == 0:
                        eng.wait_ge(zeroed, 5)
                    eng.tensor_copy(s.w2[:, e, :, 0:C], ps[4 + e % 2][0:HCHUNK, 0:HCHUNKS * C].rearrange("p (k c) -> p k c", c=C)).then_inc(w2_n, 1)


def route(nc, s, sem):
    with ExitStack() as own:
        def tmp(name, shape, dt=F32):
            return own.enter_context(nc.sbuf_tensor(name, shape, dt))

        b = NormBuffers(tmp, "rt")
        z = tmp("rt_z", [P, TILES, C])
        xt = [tmp(f"rt_xt{i}", [P, GTOK]) for i in range(2)]
        logits = tmp("rt_logits", [P, TILES, EXPERTS])
        probs, work = tmp("rt_probs", [P, TILES, EXPERTS]), tmp("rt_work", [P, TILES, EXPERTS])
        pick = [tmp(f"rt_pick{k}", [P, TILES, EXPERTS]) for k in range(2)]
        number = tmp("rt_number", [P, EXPERTS])
        best = [tmp(f"rt_best{k}", [P, TILES]) for k in range(2)]
        small = tmp("rt_small", [P, TILES])
        before, ones = tmp("rt_before", [P, P]), tmp("rt_ones", [P, P])
        total, ahead = tmp("rt_total", [P, EXPERTS, TILES]), tmp("rt_ahead", [P, EXPERTS, TILES])
        one_row = tmp("rt_one_row", [P, TILES])
        step = tmp("rt_step", [P, EXPERT_ROWS])
        over = tmp("rt_over", [P, EXPERTS, EXPERT_ROWS])
        count, end, start = tmp("rt_count", [P, EXPERTS]), tmp("rt_end", [P, EXPERTS]), tmp("rt_start", [P, EXPERTS])
        slot_f = tmp("rt_slot_f", [P, TILES])
        tile_no = tmp("rt_tile_no", [P, FTILES])
        past = tmp("rt_past", [P, FTILES, EXPERTS])
        owner = tmp("rt_owner", [P, FTILES])

        def bank(name):
            return own.enter_context(nc.psum_tensor(name, [P, 512], F32))

        ps_x, ps_l, ps_p, ps_c = bank("rt_ps_x"), bank("rt_ps_l"), bank("rt_ps_p"), bank("rt_ps_c")
        center_n, sq_n, var_n, root_n, z_n, hi_n, lo_n, x_n, xt_n, l_n, lc_n, dve_n = (
            sem(f"rt_{n}") for n in ("center", "sq", "var", "root", "z", "hi", "lo", "x", "xt", "logit", "logit_copied", "dve"))
        const_n, max_n, exp_n, picked_n, ranked_n, slots_n, zero_n, out_n = (
            sem(f"rt_{n}") for n in ("const", "max", "exp", "picked", "ranked", "slots", "zero_slots", "scattered"))
        filled_n, staged_n = sem("rt_filled"), sem("rt_staged")
        ZPARTS = 2
        zero = tmp("rt_zero", [P, SLOTS * C // P // ZPARTS])

        def run(eng, body):
            with eng.Fori(0, GROUPS // 2) as i:
                for par in range(2):
                    body(2 * i + par, par)

        with nc.Block() as block:
            @block.sync
            def _(eng):
                eng.wait_ge(filled_n, 1)
                blank = s.slot_x[:, :].rearrange("(k p r) c -> k p (r c)", k=ZPARTS, p=P)
                for k in range(ZPARTS):
                    eng.dma_start(blank[k], zero[:, :]).then_inc(zero_n, 16)
                eng.wait_ge(zero_n, 16 * ZPARTS)

            @block.gpsimd
            def _(eng):
                eng.memset(zero[:, :], 0.0).then_inc(filled_n, 1)
                eng.memset(ones[:, :], 1.0).then_inc(const_n, 1)
                eng.memset(one_row[:, :], 1.0).then_inc(const_n, 1)
                eng.wait_ge(const_n, 2)
                eng.affine_select(out=before[:, :], in_=ones[:, :], compare_op=ALU.is_gt, fill=0.0, base=0,
                                  pattern=[[1, P]], channel_multiplier=-1).then_inc(const_n, 1)
                for t, n, by in ((number, EXPERTS, 1), (step, EXPERT_ROWS, SLOT), (tile_no, FTILES, 1)):
                    eng.iota(t[:, :], pattern=[[by, n]], base=0, channel_multiplier=0,
                             allow_small_or_imprecise_dtypes=True).then_inc(const_n, 1)

                def body(g, par):
                    eng.wait_ge(center_n, g)
                    eng.tensor_copy(b.x[:, :, :], s.x1[:, bass.ds(g * GROUP, GROUP), :]).then_inc(staged_n, 1)
                run(eng, body)
                eng.wait_ge(zero_n, 16 * ZPARTS)
                eng.wait_ge(slots_n, 2)
                for t in range(TILES):
                    for k in range(2):
                        eng.indirect_dma_start(s.slot_x[:, :], bass.IndirectOffsetOnAxis(s.slot[k][:, t:t + 1], 0),
                                               z[:, t, :], None).then_inc(out_n, 16)
                eng.wait_ge(out_n, 16 * 2 * TILES)

            @block.tensor
            def _(eng):
                def body(g, par):
                    eng.wait_ge(hi_n, g + 1)
                    eng.wait_ge(lo_n, g + 1)
                    for t in range(GROUP):
                        last = eng.transpose(ps_x[:, t * P:(t + 1) * P], b.hl[:, t, :], s.ident[:, :])
                    last.then_inc(x_n, 1)
                    eng.wait_ge(xt_n, g + 1)
                    eng.wait_ge(lc_n, g)
                    for t in range(GROUP):
                        last = eng.matmul(ps_l[:, t * EXPERTS:(t + 1) * EXPERTS], xt[par][:, t * P:(t + 1) * P], s.router[:, :],
                                          start=True, stop=True)
                    last.then_inc(l_n, 1)
                run(eng, body)
                eng.wait_ge(const_n, 3)
                eng.wait_ge(picked_n, 1)
                chosen = work[:, :, :].rearrange("p t e -> p (t e)")
                eng.matmul(ps_p[:, :], before[:, :], chosen, start=True, stop=True)
                eng.matmul(ps_c[:, :], ones[:, :], chosen, start=True, stop=True).then_inc(ranked_n, 1)

            @block.scalar
            def _(eng):
                def body(g, par):
                    eng.wait_ge(center_n, g + 1)
                    eng.activation(b.sq[:, :, :], b.xc[:, :, :], ACT.Square).then_inc(sq_n, 1)
                    eng.wait_ge(var_n, g + 1)
                    eng.activation(b.root[:, :], b.var[:, :], ACT.Sqrt).then_inc(root_n, 1)
                    eng.wait_ge(z_n, g + 1)
                    eng.wait_ge(x_n, g)
                    eng.activation(b.hl[:, :, 0:C].bitcast(F32R), b.xc[:, :, :], ACT.Copy).then_inc(hi_n, 1)
                    eng.wait_ge(x_n, g + 1)
                    eng.activation(xt[par][:, :], ps_x[:, :], ACT.Copy).then_inc(xt_n, 1)
                run(eng, body)
                eng.wait_ge(max_n, 1)
                eng.activation(work[:, :, :], work[:, :, :], ACT.Exp).then_inc(exp_n, 1)

            @block.vector
            def _(eng):
                mine = Steps(eng, dve_n, LN_STEPS)

                def body(g, par):
                    mine.round(g)
                    eng.wait_ge(lo_n, g)
                    eng.wait_ge(staged_n, g + 1)
                    layer_norm(eng, mine, b.x[:, :, :], b, root_n, g + 1, sq_n, g + 1, var_n, center_n, False)
                    eng.tensor_copy(z[:, bass.ds(g * GROUP, GROUP), :], b.xc[:, :, :]).then_inc(z_n, 1)
                    eng.wait_ge(hi_n, g + 1)
                    eng.tensor_tensor(b.hl[:, :, C:2 * C], b.xc[:, :, :], b.hl[:, :, 0:C], ALU.subtract).then_inc(lo_n, 1)
                    eng.wait_ge(l_n, g + 1)
                    eng.tensor_copy(logits[:, bass.ds(g * GROUP, GROUP), :],
                                    ps_l[:, 0:GROUP * EXPERTS].rearrange("p (t e) -> p t e", e=EXPERTS)).then_inc(lc_n, 1)
                run(eng, body)
                wide = [P, TILES, EXPERTS]
                mine = Steps(eng, sem("rt_pick_dve"))

                def over_experts(t):
                    return t[:, :].unsqueeze(2).to_broadcast(wide)

                def over_tokens(t):
                    return t[:, :].unsqueeze(1).to_broadcast(wide)

                eng.wait_ge(lc_n, GROUPS)
                eng.wait_ge(const_n, 6)
                mine.then(eng.tensor_reduce(small[:, :], logits[:, :, :], AX.X, ALU.max))
                eng.tensor_tensor(work[:, :, :], logits[:, :, :], over_experts(small), ALU.subtract).then_inc(max_n, 1)
                eng.wait_ge(exp_n, 1)
                mine.then(eng.tensor_reduce(small[:, :], work[:, :, :], AX.X, ALU.add))
                mine.then(eng.reciprocal(small[:, :], small[:, :]))
                mine.then(eng.tensor_tensor(probs[:, :, :], work[:, :, :], over_experts(small), ALU.mult))
                for k in range(2):
                    mine.then(eng.tensor_reduce(best[k][:, :], probs[:, :, :], AX.X, ALU.max))
                    mine.then(eng.tensor_tensor(work[:, :, :], probs[:, :, :], over_experts(best[k]), ALU.is_lt))
                    mine.then(eng.tensor_scalar(work[:, :, :], work[:, :, :], float(EXPERTS), None, ALU.mult))
                    mine.then(eng.tensor_tensor(work[:, :, :], work[:, :, :], over_tokens(number), ALU.add))
                    mine.then(eng.tensor_reduce(small[:, :], work[:, :, :], AX.X, ALU.min))
                    mine.then(eng.tensor_tensor(pick[k][:, :, :], over_tokens(number), over_experts(small), ALU.is_equal))
                    if k == 0:
                        mine.then(eng.tensor_scalar(work[:, :, :], pick[0][:, :, :], 2.0, None, ALU.mult))
                        mine.then(eng.tensor_tensor(probs[:, :, :], probs[:, :, :], work[:, :, :], ALU.subtract))
                eng.tensor_tensor(work[:, :, :], pick[0][:, :, :], pick[1][:, :, :], ALU.add).then_inc(picked_n, 1)
                mine.then(eng.tensor_tensor(small[:, :], best[0][:, :], best[1][:, :], ALU.add))
                mine.then(eng.tensor_scalar(small[:, :], small[:, :], 1e-9, None, ALU.add))
                mine.then(eng.reciprocal(small[:, :], small[:, :]))
                for k in range(2):
                    mine.did(eng.tensor_tensor(s.gate[k][:, :], best[k][:, :], small[:, :], ALU.mult))
                eng.wait_ge(ranked_n, 1)
                mine.then(eng.tensor_copy(total[:, :, :], ps_c[:, :].rearrange("p (t e) -> p e t", e=EXPERTS)))
                for e in range(EXPERTS):
                    mine.did(eng.tensor_tensor_scan(ahead[:, e, :], one_row[:, :], total[:, e, :], 0.0, ALU.mult, ALU.add))
                mine.settle()
                mine.then(eng.tensor_tensor(over[:, :, :], ahead[:, :, TILES - 1:TILES].to_broadcast([P, EXPERTS, EXPERT_ROWS]),
                                            step[:, :].unsqueeze(1).to_broadcast([P, EXPERTS, EXPERT_ROWS]), ALU.is_gt))
                mine.then(eng.tensor_reduce(count[:, :], over[:, :, :], AX.X, ALU.add))
                mine.then(eng.tensor_tensor_scan(end[:, :], one_row[:, 0:EXPERTS], count[:, :], 0.0, ALU.mult, ALU.add))
                mine.then(eng.tensor_tensor(start[:, :], end[:, :], count[:, :], ALU.subtract))
                mine.then(eng.tensor_scalar(start[:, :], start[:, :], float(SLOT), None, ALU.mult))
                mine.then(eng.tensor_tensor(ahead[:, :, :], ahead[:, :, :], total[:, :, :], ALU.subtract))
                mine.then(eng.tensor_tensor(ahead[:, :, :], ahead[:, :, :], start[:, :].unsqueeze(2).to_broadcast([P, EXPERTS, TILES]), ALU.add))
                mine.then(eng.tensor_tensor(probs[:, :, :], ps_p[:, :].rearrange("p (t e) -> p t e", e=EXPERTS),
                                            ahead[:, :, :].rearrange("p e t -> p t e"), ALU.add))
                for k in range(2):
                    mine.then(eng.tensor_tensor(work[:, :, :], probs[:, :, :], pick[k][:, :, :], ALU.mult))
                    mine.then(eng.tensor_reduce(slot_f[:, :], work[:, :, :], AX.X, ALU.add))
                    eng.tensor_copy(s.slot[k][:, :], slot_f[:, :]).then_inc(slots_n, 1)
                    eng.wait_ge(slots_n, k + 1)
                mine.then(eng.tensor_tensor(past[:, :, :], tile_no[:, :].unsqueeze(2).to_broadcast([P, FTILES, EXPERTS]),
                                            end[:, :].unsqueeze(1).to_broadcast([P, FTILES, EXPERTS]), ALU.is_ge))
                mine.then(eng.tensor_reduce(owner[:, :], past[:, :, :], AX.X, ALU.add))
                mine.then(eng.tensor_scalar(owner[:, :], owner[:, :], float(EXPERTS - 1), None, ALU.min))
                mine.then(eng.tensor_copy(s.owner[:, :], owner[:, :]))


def experts(nc, s, sem):
    with ExitStack() as own:
        def tmp(name, shape, dt=F32):
            return own.enter_context(nc.sbuf_tensor(name, shape, dt))

        R = SLOT // P
        x = [tmp(f"ex_x{i}", [P, R, C]) for i in range(2)]
        hl = [tmp(f"ex_hl{i}", [P, R, P]) for i in range(2)]
        xt = [tmp(f"ex_xt{i}", [P, SLOT], F32R) for i in range(2)]
        w13 = [[tmp(f"ex_w13_{i}{k}", [P, 2, HPAD], F32R) for k in range(2)] for i in range(2)]
        w2 = [tmp(f"ex_w2_{i}", [HCHUNK, HCHUNKS, P]) for i in range(2)]
        act = [tmp(f"ex_act{i}", [HCHUNK, SLOT]) for i in range(3)]
        h = [tmp(f"ex_h{i}", [HCHUNK, HCHUNKS, SLOT]) for i in range(2)]
        y = [tmp(f"ex_y{i}", [P, SLOT]) for i in range(2)]
        out = [tmp(f"ex_out{i}", [P, R, C]) for i in range(2)]

        def bank(name):
            return own.enter_context(nc.psum_tensor(name, [P, 512], F32))

        ps_x, ps_y, ps_o = bank("ex_ps_x"), bank("ex_ps_y"), bank("ex_ps_o")
        ps_1, ps_3 = [bank(f"ex_ps_1{i}") for i in range(2)], [bank(f"ex_ps_3{i}") for i in range(2)]
        x_in = [sem(f"ex_x_in{i}") for i in range(2)]
        hi_n, lo_n, x_n, xt_n, w_n, h1_n, h3_n, act_n, h_n, y_n, yc_n, o_n, oc_n = (
            sem(f"ex_{n}") for n in ("hi", "lo", "x", "xt", "weights", "h1", "h3", "act", "h", "y", "y_copied", "o", "o_copied"))
        stored = [sem(f"ex_stored{i}") for i in range(2)]
        slot_x = s.slot_x[:, :].rearrange("(k p r) c -> k p r c", p=P, r=R)
        slot_y = s.slot_y[:, :].rearrange("(k p r) c -> k p r c", p=P, r=R)

        def run(eng, body):
            with eng.Fori(0, FTILES // 2) as i:
                for par in range(2):
                    body(2 * i + par, par, i)
            if FTILES % 2:
                body(FTILES - 1, 0, FTILES // 2)

        with nc.Block() as block:
            @block.sync
            def _(eng):
                def load(k, par):
                    eng.dma_start(x[par][:, :, :], slot_x[bass.ds(k, 1)].rearrange("o p r c -> (o p) r c")).then_inc(x_in[par], 16)

                def body(k, par, half):
                    if sym(k):
                        eng.wait_ge(lo_n, k)
                        eng.wait_ge(hi_n, k)
                        load(k + 1, 1 - par)
                    eng.wait_ge(oc_n, k + 1)
                    eng.dma_start(slot_y[bass.ds(k, 1)].rearrange("o p r c -> (o p) r c"), out[par][:, :, :]).then_inc(stored[par], 16)
                load(0, 0)
                run(eng, body)
                eng.wait_ge(stored[0], 16 * (FTILES - FTILES // 2))
                eng.wait_ge(stored[1], 16 * (FTILES // 2))

            @block.gpsimd
            def _(eng):
                def body(k, par, half):
                    e = eng.value_load(s.owner[0:1, bass.ds(k, 1)], min_val=0, max_val=EXPERTS - 1)
                    eng.wait_ge(y_n, k - par)
                    for j in range(2):
                        eng.tensor_copy(w13[par][j][:, :, :], s.w13[j][:, bass.ds(e, 1), :, :].rearrange("p o m n -> p (o m) n").bitcast(F32)).then_inc(w_n, 1)
                    eng.tensor_copy(w2[par][:, :, :], s.w2[:, bass.ds(e, 1), :, :].rearrange("p o k n -> p (o k) n")).then_inc(w_n, 1)
                run(eng, body)

            @block.tensor
            def _(eng):
                def body(k, par, half):
                    eng.wait_ge(hi_n, k + 1)
                    eng.wait_ge(lo_n, k + 1)
                    for r in range(R):
                        last = eng.transpose(ps_x[:, r * P:(r + 1) * P], hl[par][:, r, :], s.ident[:, :])
                    last.then_inc(x_n, 1)
                    eng.wait_ge(xt_n, k + 1)
                    eng.wait_ge(w_n, 3 * k + 3)
                    for c in range(HCHUNKS):
                        for m, (ps, done, free) in enumerate(((ps_1, h1_n, act_n), (ps_3, h3_n, h_n))):
                            for j in range(2):
                                if j == 0 and (c >= 2 or sym(k) or k > 0):
                                    eng.wait_ge(free, HCHUNKS * k + c - 1 if c >= 1 else HCHUNKS * k)
                                last = eng.matmul(ps[c % 2][0:HCHUNK, 0:SLOT], w13[par][j][:, m, c * HCHUNK:(c + 1) * HCHUNK], xt[par][:, :],
                                                  start=(j == 0), stop=(j == 1))
                            last.then_inc(done, 1)
                    eng.wait_ge(yc_n, k)
                    for c in range(HCHUNKS):
                        eng.wait_ge(h_n, HCHUNKS * k + c + 1)
                        last = eng.matmul(ps_y[:, 0:SLOT], w2[par][:, c, :], h[par][:, c, :], start=(c == 0), stop=(c == HCHUNKS - 1))
                    last.then_inc(y_n, 1)
                    eng.wait_ge(yc_n, k + 1)
                    eng.wait_ge(oc_n, k)
                    for r in range(R):
                        last = eng.transpose(ps_o[:, r * P:(r + 1) * P], y[par][:, r * P:(r + 1) * P], s.ident[:, :])
                    last.then_inc(o_n, 1)
                run(eng, body)

            @block.scalar
            def _(eng):
                def body(k, par, half):
                    eng.wait_ge(x_in[par], 16 * (half + 1))
                    eng.wait_ge(x_n, k - par)
                    eng.activation(hl[par][:, :, 0:C].bitcast(F32R), x[par][:, :, :], ACT.Copy).then_inc(hi_n, 1)
                    eng.wait_ge(x_n, k + 1)
                    eng.wait_ge(h3_n, HCHUNKS * (k - par))
                    eng.activation(xt[par][:, :], ps_x[:, 0:SLOT], ACT.Copy).then_inc(xt_n, 1)
                    for c in range(HCHUNKS):
                        eng.wait_ge(h1_n, HCHUNKS * k + c + 1)
                        if c >= 3 or sym(k) or k > 0:
                            eng.wait_ge(h_n, HCHUNKS * k + max(c - 2, 0))
                        eng.activation(act[c % 3][:, :], ps_1[c % 2][0:HCHUNK, 0:SLOT], ACT.Silu).then_inc(act_n, 1)
                    eng.wait_ge(y_n, k + 1)
                    eng.wait_ge(o_n, k - par)
                    eng.activation(y[par][:, :], ps_y[:, 0:SLOT], ACT.Copy).then_inc(yc_n, 1)
                run(eng, body)

            @block.vector
            def _(eng):
                def body(k, par, half):
                    eng.wait_ge(hi_n, k + 1)
                    eng.wait_ge(x_n, k - par)
                    eng.tensor_tensor(hl[par][:, :, C:2 * C], x[par][:, :, :], hl[par][:, :, 0:C], ALU.subtract).then_inc(lo_n, 1)
                    eng.wait_ge(y_n, k - par)
                    for c in range(HCHUNKS):
                        eng.wait_ge(act_n, HCHUNKS * k + c + 1)
                        eng.wait_ge(h3_n, HCHUNKS * k + c + 1)
                        eng.tensor_tensor(h[par][:, c, :], act[c % 3][:, :], ps_3[c % 2][0:HCHUNK, 0:SLOT], ALU.mult).then_inc(h_n, 1)
                    eng.wait_ge(o_n, k + 1)
                    eng.wait_ge(stored[par], 16 * half)
                    eng.tensor_copy(out[par][:, :, :], ps_o[:, 0:R * P].rearrange("p (r c) -> p r c", c=P)[:, :, 0:C]).then_inc(oc_n, 1)
                run(eng, body)



def combine(nc, s, out, sem):
    with ExitStack() as own:
        def tmp(name, shape, dt=F32):
            return own.enter_context(nc.sbuf_tensor(name, shape, dt))

        got = [tmp(f"cb_got{k}", [P, TILES, C]) for k in range(2)]
        in_n, sum_n, out_n, dve_n = [sem(f"cb_in{q}") for q in range(4)], sem("cb_sum"), sem("cb_out"), sem("cb_dve")
        QT = TILES // 4
        with nc.Block() as block:
            @block.gpsimd
            def _(eng):
                for t in range(TILES):
                    for k in range(2):
                        eng.indirect_dma_start(got[k][:, t, :], None, s.slot_y[:, :],
                                               bass.IndirectOffsetOnAxis(s.slot[k][:, t:t + 1], 0)).then_inc(in_n[t // QT], 16)

            @block.vector
            def _(eng):
                mine = Steps(eng, dve_n)
                wide = [P, QT, C]
                for q in range(4):
                    tiles = slice(q * QT, (q + 1) * QT)
                    eng.wait_ge(in_n[q], 16 * 2 * QT)
                    for k in range(2):
                        mine.did(eng.tensor_tensor(got[k][:, tiles, :], got[k][:, tiles, :], s.gate[k][:, tiles].unsqueeze(2).to_broadcast(wide), ALU.mult))
                    mine.settle()
                    mine.then(eng.tensor_tensor(got[0][:, tiles, :], got[0][:, tiles, :], got[1][:, tiles, :], ALU.add))
                    eng.tensor_tensor(s.x1[:, tiles, :], s.x1[:, tiles, :], got[0][:, tiles, :], ALU.add).then_inc(sum_n, 1)

            @block.sync
            def _(eng):
                dst = out.rearrange("b r c e -> b (r c) e").rearrange("b (g q) e -> q b g e", q=4)
                for part in range(4):
                    eng.wait_ge(sum_n, part + 1)
                    tiles = slice(part * QT, (part + 1) * QT)
                    for q in range(4):
                        eng.dma_start(dst[q][:, tiles, :], s.x1[q * BATCH:(q + 1) * BATCH, tiles, :]).then_inc(out_n, 16)
                eng.wait_ge(out_n, 16 * 16)


def hybrid_block(nc, a, out):
    with ExitStack() as ctx:
        def sem(name):
            return ctx.enter_context(nc.semaphore(name))

        s = allocate(nc, ctx)
        constants(nc, s, sem)
        with ExitStack() as upto_layer2:
            def sb(name, shape, dt=F32):
                return upto_layer2.enter_context(nc.sbuf_tensor(name, shape, dt))

            s.conv = sb("conv_out", [P, TOK])
            with ExitStack() as layer1:
                s.xhl = layer1.enter_context(nc.sbuf_tensor("gn_hl", [P, TILES, P], F32))
                conv_weights(nc, layer1, s, a, sem)
                group_norm(nc, s, a, sem)
                conv_attention(nc, s, sem)
            s.xt = sb("norm_T", [P, TOK], F32R)
            s.proj = [sb(f"proj{k}", [P, 4, HC], F32R) for k in range(2)]
            s.wo, s.bo, s.bg = sb("wo_sb", [P, 2, P]), sb("bo_sb", [P, 1]), sb("bg_sb", [P, 2])
            s.gamma, s.beta = sb("gamma_sb", [P, C]), sb("beta_sb", [P, C])
            s.att_w = sb("att_w", [P, HEADS, P])
            axial_weights(nc, s, a, sem)
            axial_scores(nc, s, sem)
            axial_values(nc, s, sem)

        def sb(name, shape, dt=F32):
            return ctx.enter_context(nc.sbuf_tensor(name, shape, dt))

        s.w13 = [sb(f"w13_{k}", [P, EXPERTS, 2, HPAD], F32R) for k in range(2)]
        s.w2 = sb("w2_sb", [HCHUNK, EXPERTS, HCHUNKS, P])
        s.router = sb("router", [P, EXPERTS])
        s.slot = [sb(f"slot{k}", [P, TILES], mybir.dt.uint32) for k in range(2)]
        s.gate = [sb(f"gate{k}", [P, TILES]) for k in range(2)]
        s.owner = sb("owner", [P, FTILES], mybir.dt.int32)
        s.slot_x = nc.dram_tensor("slot_x", [SLOTS, C], F32, kind="Internal").ap()
        s.slot_y = nc.dram_tensor("slot_y", [SLOTS, C], F32, kind="Internal").ap()
        expert_weights(nc, s, a, sem)
        route(nc, s, sem)
        experts(nc, s, sem)
        combine(nc, s, out, sem)


_INS = ['x', 'L0_conv_w_q', 'L0_conv_w_k', 'L0_conv_w_v', 'L0_conv_w_local', 'L0_conv_b_local', 'L0_conv_w_out',
        'L0_conv_b_out', 'L1_attn_gamma', 'L1_attn_beta', 'L1_attn_Wq', 'L1_attn_Wk', 'L1_attn_Wv', 'L1_attn_Wg',
        'L1_attn_bg', 'L1_attn_Wo', 'L1_attn_bo', 'L1_ffn_router_w', 'L1_ffn_w1', 'L1_ffn_w2', 'L1_ffn_w3']
_OUTS = [((BATCH, SIDE, SIDE, C), 'float32')]


def kernel(**inputs):
    import numpy as _np
    import concourse.bacc as _bacc
    from concourse import mybir as _mybir
    from concourse.bass_utils import run_bass_kernel_spmd as _run

    nc = _bacc.Bacc("TRN2", target_bir_lowering=False, num_devices=1)
    arrays, args = {}, {}
    for name in _INS:
        arr = _np.ascontiguousarray(inputs[name])
        arrays[f"in_{name}_dram"] = arr
        args[name] = nc.dram_tensor(f"in_{name}_dram", arr.shape, _mybir.dt.from_np(arr.dtype), kind="ExternalInput").ap()
    shape, dtype = _OUTS[0]
    out = nc.dram_tensor("out_0_dram", shape, _mybir.dt.from_np(_np.dtype(dtype)), kind="ExternalOutput").ap()
    hybrid_block(nc, args, out)
    r = _run(nc, [arrays], core_ids=[0])
    return r.results[0]["out_0_dram"]
```

```python
from contextlib import ExitStack

import concourse.bass as bass
from concourse import mybir

F32 = mybir.dt.float32
F32R = mybir.dt.float32r
ALU = mybir.AluOpType
ACT = mybir.ActivationFunctionType
AX = mybir.AxisListType

P = 128
BATCH, SIDE, C = 32, 16, 64
L = SIDE * SIDE
TOK = BATCH * L
TILES = TOK // P
HEADS, D = 8, 32
HC = HEADS * D
WIN = 8
WTOK = WIN * WIN
TAPS = 9
PADDED = SIDE + 2


class Steps:

    def __init__(self, engine, sem, per=0):
        self.engine, self.sem, self.per = engine, sem, per
        self.base, self.n = 0, 0

    def round(self, i):
        assert self.per == 0 or self.n in (0, self.per), (self.n, self.per)
        self.base, self.n = i * self.per, 0

    def did(self, ins):
        ins.then_inc(self.sem, 1)
        self.n += 1

    def settle(self):
        self.engine.wait_ge(self.sem, self.base + self.n)

    def then(self, ins):
        self.did(ins)
        self.settle()


class Shared:
    pass


def allocate(nc, ctx):
    def sb(name, shape, dt=F32):
        return ctx.enter_context(nc.sbuf_tensor(name, shape, dt))

    s = Shared()
    s.ident = sb("ident", [P, P])
    s.x1 = sb("residual", [P, TILES, C])
    s.mean_of_group = sb("mean_of_group", [P, P])
    return s


def constants(nc, s, sem):
    done, filled = sem("constants_done"), sem("constants_filled")
    with nc.Block() as block:
        @block.gpsimd
        def _(eng):
            eng.memset(s.ident[:, :], 0.0).then_inc(filled, 1)
            eng.wait_ge(filled, 1)
            eng.affine_select(out=s.ident[:, :], in_=s.ident[:, :], compare_op=ALU.not_equal, fill=1.0,
                              base=0, pattern=[[-1, P]], channel_multiplier=1).then_inc(done, 1)
            eng.memset(s.mean_of_group[:, :], 1.0 / (2 * L)).then_inc(done, 1)
            eng.wait_ge(done, 2)


def conv_weights(nc, ctx, s, a, sem):
    def sb(name, shape, dt=F32):
        return ctx.enter_context(nc.sbuf_tensor(name, shape, dt))

    s.score_w = [sb(f"score_w{k}", [P, HEADS, P], F32R) for k in range(2)]
    s.value_w = [sb(f"value_w{k}", [P, HEADS * C], F32R) for k in range(2)]
    s.tap_w = sb("tap_w", [P, TAPS, 2, C], F32R)
    s.conv_bias = sb("conv_bias", [P, 1])
    with ExitStack() as own:
        def tmp(name, shape, dt=F32):
            return own.enter_context(nc.sbuf_tensor(name, shape, dt))

        wq, wk, wv = (tmp(f"w{n}_in", [C, HC]) for n in "qkv")
        wout = tmp("wout_in", [P, 2, C])
        wlocal = tmp("wlocal_in", [P, 2, TAPS, HC])
        b_local = tmp("b_local_in", [P, 2])
        b_out = tmp("b_out_in", [C, 1])
        wT = tmp("wT", [P, 3, 2, 2, C])
        folded = tmp("folded", [P, HEADS, P])
        folded_v = tmp("folded_v", [P, HEADS, C])
        tapT = tmp("tapT", [P, TAPS, 2, P])
        tap = tmp("tap", [P, TAPS, C])
        psT = own.enter_context(nc.psum_tensor("psT_w", [P, 6, C], F32))
        psA = [own.enter_context(nc.psum_tensor(f"psA_w{r}", [P, 512], F32)) for r in range(4)]
        psB = own.enter_context(nc.psum_tensor("psB_w", [P, 2, 512], F32))
        loads, w_turned, wT_ready = sem("conv_w_loads"), sem("conv_w_turned"), sem("conv_wT_ready")
        heads_done, taps_done, tap_free = sem("head_products_done"), sem("taps_done"), sem("tap_free")
        tapT_ready, weff_done, weff_copied = sem("tapT_ready"), sem("weff_done"), sem("weff_copied")
        act_did, dve_did = sem("conv_w_act"), sem("conv_w_dve")
        n_loads = 9

        with nc.Block() as block:
            @block.sync
            def _(eng):
                for dst, src in ((wq, a["L0_conv_w_q"]), (wk, a["L0_conv_w_k"]), (wv, a["L0_conv_w_v"])):
                    eng.dma_start(dst[:, :], src.rearrange("a b c n -> (a b c) n")).then_inc(loads, 16)
                eng.dma_start(wout[:, :, :], a["L0_conv_w_out"].rearrange("a b (k p) n -> p (a b k) n", p=P)).then_inc(loads, 16)
                for k in range(2):
                    eng.dma_start(b_local[:, k:k + 1], a["L0_conv_b_local"][k * P:(k + 1) * P].rearrange("(p o) -> p o", o=1)).then_inc(loads, 16)
                eng.dma_start(b_out[:, :], a["L0_conv_b_out"].rearrange("(p o) -> p o", o=1)).then_inc(loads, 16)
                local = a["L0_conv_w_local"].rearrange("u v (k p) n -> k p (u v) n", p=P)
                for k in range(2):
                    eng.dma_start(wlocal[:, k], local[k]).then_inc(loads, 16)

            @block.tensor
            def _(eng):
                eng.wait_ge(loads, 16 * n_loads)
                for i, w in enumerate((wq, wk, wv)):
                    for k in range(2):
                        last = eng.transpose(psT[:, 2 * i + k, :], w[:, k * P:(k + 1) * P], s.ident[0:C, 0:C])
                last.then_inc(w_turned, 1)
                eng.wait_ge(wT_ready, 2)
                for h in range(HEADS):
                    k, r = divmod(h, 4)
                    rows = slice(D * r, D * r + D)
                    q, kk, v = (wT[rows, i, k].rearrange("p a c -> p (a c)") for i in range(3))
                    eng.matmul(psA[r][:, k * P:(k + 1) * P], kk, q, start=True, stop=True)
                    last = eng.matmul(psA[r][:, 2 * P + k * C:2 * P + (k + 1) * C], v, wout[rows, k, :],
                                      start=True, stop=True)
                last.then_inc(heads_done, 1)
                for t in range(TAPS):
                    if t >= 2:
                        eng.wait_ge(tap_free, t - 1)
                    for blk in range(2):
                        for k in range(2):
                            last = eng.matmul(psB[:, t % 2, blk * P:(blk + 1) * P], wlocal[:, k, t, blk * P:(blk + 1) * P],
                                              wT[:, 2, k].rearrange("p a c -> p (a c)"),
                                              start=(k == 0), stop=(k == 1))
                    last.then_inc(taps_done, 1)
                eng.wait_ge(tap_free, TAPS)
                for t in range(TAPS):
                    for blk in range(2):
                        last = eng.matmul(psB[:, t // 8, (t % 8) * C:(t % 8 + 1) * C], tapT[:, t, blk, :], wout[:, blk, :],
                                          start=(blk == 0), stop=(blk == 1))
                last.then_inc(weff_done, 1)
                for k in range(2):
                    last = eng.matmul(psB[0:C, 1, 256:257], wout[:, k, :], b_local[:, k:k + 1], start=(k == 0), stop=(k == 1))
                last.then_inc(weff_done, 1)

            @block.scalar
            def _(eng):
                eng.wait_ge(w_turned, 1)
                turned = psT[:, :, :].rearrange("p (i k) c -> p i k c", k=2)
                for twice in range(2):
                    eng.activation(wT[:, :, :, twice, :], turned, ACT.Copy).then_inc(wT_ready, 1)
                mine = Steps(eng, act_did)
                eng.wait_ge(heads_done, 1)
                for h in range(HEADS):
                    k, r = divmod(h, 4)
                    mine.did(eng.activation(folded[:, h, :], psA[r][:, k * P:(k + 1) * P], ACT.Copy, scale=D ** -0.5))
                    mine.did(eng.activation(folded_v[:, h, :], psA[r][:, 2 * P + k * C:2 * P + (k + 1) * C], ACT.Copy))
                mine.settle()
                mine.did(eng.activation(s.score_w[0][:, :, :], folded[:, :, :], ACT.Copy))
                mine.did(eng.activation(s.value_w[0][:, :], folded_v[:, :, :].rearrange("p h c -> p (h c)"), ACT.Copy))
                eng.wait_ge(weff_copied, 2)
                mine.did(eng.activation(s.tap_w[:, :, 0, :], tap[:, :, :], ACT.Copy))

            @block.vector
            def _(eng):
                for t in range(TAPS):
                    eng.wait_ge(taps_done, t + 1)
                    eng.tensor_copy(tapT[:, t], psB[:, t % 2, 0:2 * P].rearrange("p (b e) -> p b e", b=2)).then_inc(tap_free, 1)
                eng.memset(s.conv_bias[:, :], 0.0).then_inc(dve_did, 1)
                eng.wait_ge(act_did, 2 * HEADS + 2)
                eng.tensor_tensor(s.score_w[1][:, :, :], folded[:, :, :], s.score_w[0][:, :, :].bitcast(F32), ALU.subtract).then_inc(dve_did, 1)
                eng.tensor_tensor(s.value_w[1][:, :], folded_v[:, :, :].rearrange("p h c -> p (h c)"), s.value_w[0][:, :].bitcast(F32), ALU.subtract).then_inc(dve_did, 1)
                eng.wait_ge(weff_done, 2)
                eng.wait_ge(dve_did, 3)
                eng.tensor_tensor(s.conv_bias[0:C, :], psB[0:C, 1, 256:257], b_out[:, :], ALU.add).then_inc(dve_did, 1)
                eng.tensor_copy(tap[:, 0:8, :], psB[:, 0, :].rearrange("p (t c) -> p t c", c=C)).then_inc(weff_copied, 1)
                eng.tensor_copy(tap[:, 8, :], psB[:, 1, 0:C]).then_inc(weff_copied, 1)
                eng.wait_ge(act_did, 2 * HEADS + 3)
                eng.tensor_tensor(s.tap_w[:, :, 1, :], tap[:, :, :], s.tap_w[:, :, 0, :].bitcast(F32), ALU.subtract).then_inc(dve_did, 1)


def group_norm(nc, s, a, sem):
    with ExitStack() as own:
        def tmp(name, shape, dt=F32):
            return own.enter_context(nc.sbuf_tensor(name, shape, dt))

        x = tmp("gn_x", [P, TILES, C])
        sq = tmp("gn_sq", [P, TILES, C])
        groups = C // 2
        mean = tmp("gn_mean", [P, BATCH, groups])
        var = tmp("gn_var", [P, BATCH, groups])
        rstd = tmp("gn_rstd", [P, BATCH, groups])
        fix = tmp("gn_fix", [P, BATCH, groups])
        PARTS = 4
        per = BATCH // PARTS
        ps = own.enter_context(nc.psum_tensor("gn_ps", [P, 2, PARTS, 512], F32))
        x_in, sums, squares, roots = sem("gn_x_in"), sem("gn_sums"), sem("gn_squares"), sem("gn_roots")
        centered, var_ready, normed, hi_ready, dve_did = (sem("gn_centered"), sem("gn_var_ready"), sem("gn_normed"),
                                                          sem("gn_hi_ready"), sem("gn_dve"))
        lo_ready = sem("gn_lo_ready")

        def half(t, h):
            return t[:, h::2, :].rearrange("p b (g e) -> p b g e", e=2)

        def spread(t):
            return t[:, :, :].unsqueeze(3).to_broadcast([P, BATCH, groups, 2])

        with nc.Block() as block:
            def load(eng, ny):
                src = a["x"].rearrange("b (nx r) (ny c) e -> ny r c (b nx) e", nx=2, ny=2)
                for r in range(WIN):
                    p0 = ny * WTOK + r * WIN
                    eng.dma_start(x[p0:p0 + WIN, :, :], src[ny, r]).then_inc(x_in, 16)

            @block.sync
            def _(eng):
                load(eng, 0)

            @block.tensor
            def _(eng):
                eng.wait_ge(x_in, 16 * 2 * WIN)
                for k, t in enumerate((x, sq)):
                    for q in range(PARTS):
                        if k == 1:
                            eng.wait_ge(squares, 1)
                        for h in range(2):
                            first = 2 * q * per + h
                            last = eng.matmul(ps[:, k, q, :], s.mean_of_group[:, :], t[:, first:2 * (q + 1) * per:2, :],
                                              start=(h == 0), stop=(h == 1))
                        last.then_inc(sums, 1)

            @block.scalar
            def _(eng):
                load(eng, 1)
                eng.wait_ge(centered, 2)
                eng.activation(sq[:, :, :], x[:, :, :], ACT.Square).then_inc(squares, 1)
                eng.wait_ge(var_ready, 1)
                eng.activation(fix[:, :, :], var[:, :, :], ACT.Sqrt).then_inc(roots, 1)
                eng.wait_ge(normed, 2)
                eng.activation(s.xhl[:, :, 0:C].bitcast(F32R), sq[:, :, :], ACT.Copy).then_inc(hi_ready, 1)

            @block.vector
            def _(eng):
                mine = Steps(eng, dve_did)
                for q in range(PARTS):
                    eng.wait_ge(sums, q + 1)
                    mine.did(eng.tensor_reduce(mean[:, q * per:(q + 1) * per, :],
                                               ps[:, 0, q, :].rearrange("p (b g e) -> p b g e", g=groups, e=2), AX.X, ALU.add))
                eng.wait_ge(sums, PARTS)
                mine.settle()
                for h in range(2):
                    eng.tensor_tensor(half(x, h), half(x, h), spread(mean), ALU.subtract).then_inc(centered, 1)
                for q in range(PARTS):
                    eng.wait_ge(sums, PARTS + q + 1)
                    mine.did(eng.tensor_reduce(var[:, q * per:(q + 1) * per, :],
                                               ps[:, 1, q, :].rearrange("p (b g e) -> p b g e", g=groups, e=2), AX.X, ALU.add))
                mine.settle()
                eng.tensor_scalar(var[:, :, :], var[:, :, :], 1e-5, None, ALU.add).then_inc(var_ready, 1)
                eng.wait_ge(roots, 1)
                mine.then(eng.reciprocal(rstd[:, :, :], fix[:, :, :]))
                newton(eng, mine, rstd[:, :, :], var[:, :, :], fix[:, :, :])
                for h in range(2):
                    eng.tensor_tensor(half(sq, h), half(x, h), spread(rstd), ALU.mult).then_inc(normed, 1)
                eng.wait_ge(hi_ready, 1)
                eng.wait_ge(normed, 2)
                eng.tensor_tensor(s.xhl[:, :, C:2 * C], sq[:, :, :], s.xhl[:, :, 0:C], ALU.subtract).then_inc(lo_ready, 1)


def newton(eng, mine, y, v, t):
    mine.then(eng.tensor_tensor(t, y, y, ALU.mult))
    mine.then(eng.tensor_tensor(t, t, v, ALU.mult))
    mine.then(eng.tensor_scalar(t, t, -0.5, 1.5, ALU.mult, ALU.add))
    mine.then(eng.tensor_tensor(y, y, t, ALU.mult))


def conv_attention(nc, s, sem):
    with ExitStack() as own:
        def tmp(name, shape, dt=F32):
            return own.enter_context(nc.sbuf_tensor(name, shape, dt))

        W2 = 2
        staged = [tmp(f"staged{i}", [P, 2, P]) for i in range(W2)]
        xw = [tmp(f"xw{i}", [P, 4, 2, WTOK], F32R) for i in range(W2)]
        xp = [tmp(f"xp{i}", [P, PADDED, PADDED], F32R) for i in range(W2)]
        y = tmp("score_side", [P, HEADS, L])
        v = [tmp(f"values{i}", [P, 2, 4, 2, C]) for i in range(W2)]
        shifted = [tmp(f"shifted{i}", [P, HEADS, WTOK]) for i in range(W2)]
        probs = [tmp(f"probs{i}", [P, HEADS, WTOK]) for i in range(W2)]
        probsT = [tmp(f"probsT{i}", [P, 4, P]) for i in range(W2)]
        mx = [tmp(f"win_max{i}", [P, HEADS]) for i in range(W2)]
        den = [tmp(f"win_den{i}", [P, HEADS]) for i in range(W2)]
        rden = [tmp(f"win_rden{i}", [P, HEADS]) for i in range(W2)]

        def bank(name):
            return own.enter_context(nc.psum_tensor(name, [P, 512], F32))

        ps_x, ps_t, ps_o = bank("ps_x"), bank("ps_t"), bank("ps_o")
        ps_a = [bank(f"ps_a{i}") for i in range(3)]
        ps_s = [bank("ps_s0"), bank("ps_s1")]

        staged_n, turned_n, xw_n, xp_n = sem("staged_n"), sem("turned_n"), sem("xw_n"), sem("xp_n")
        conv_n, convc_n = sem("conv_done_n"), sem("conv_copied_n")
        y_n, ya_n, yd_n = sem("y_done_n"), sem("y_copied_act_n"), sem("y_copied_dve_n")
        v_n, va_n, vd_n = sem("v_done_n"), sem("v_copied_act_n"), sem("v_copied_dve_n")
        s_n, sub_n, exp_n, rden_n, prob_n = sem("scores_n"), sem("shifted_n"), sem("exp_n"), sem("rden_n"), sem("prob_n")
        pt_n, ptc_n, o_n, added_n = sem("probs_turned_n"), sem("probsT_n"), sem("out_n"), sem("added_n")
        max_n, den_n, zero_n = sem("win_max_n"), sem("win_den_n"), sem("border_zero")

        def images(eng, body):
            body(0, 0)
            body(1, 1)
            with eng.Fori(1, BATCH // 2 - 1) as i:
                for par in range(2):
                    body(2 * i + par, par)
            body(BATCH - 2, 0)
            body(BATCH - 1, 1)

        def there(n):
            return sym(n) or n < BATCH

        with nc.Block() as block:
            @block.gpsimd
            def _(eng):
                for i in range(W2):
                    eng.memset(xp[i][:, :, :].bitcast(F32), 0.0).then_inc(zero_n, 1)

                def stage(n, par):
                    wait(eng, turned_n, n - 1)
                    eng.tensor_copy(staged[par][:, :, :], s.xhl[:, bass.ds(2 * n, 2), :]).then_inc(staged_n, 1)

                def body(n, par):
                    if there(n + 2):
                        stage(n + 2, par)
                    for t in range(2):
                        eng.wait_ge(rden_n, 2 * n + t + 1)
                        wait(eng, pt_n, 2 * n + t - 1)
                        eng.tensor_tensor(probs[t][:, :, :], shifted[t][:, :, :],
                                          rden[t][:, :].unsqueeze(2).to_broadcast([P, HEADS, WTOK]), ALU.mult).then_inc(prob_n, 1)

                stage(0, 0)
                stage(1, 1)
                images(eng, body)

            @block.tensor
            def _(eng):
                def turn(n, par):
                    eng.wait_ge(staged_n, n + 1)
                    wait(eng, convc_n, n)
                    for t in range(2):
                        last = eng.transpose(ps_x[:, t * P:(t + 1) * P], staged[par][:, t, :], s.ident[:, :])
                    last.then_inc(turned_n, 1)

                def right_side(n, par):
                    eng.wait_ge(xw_n, n + 1)
                    for g in range(4):
                        if g < 2:
                            wait(eng, va_n, 4 * n - 1 + g)
                            wait(eng, vd_n, 4 * n - 1 + g)
                        elif g == 3:
                            eng.wait_ge(ya_n, 2 * n + 1)
                        for e in range(2):
                            for k in range(2):
                                last = eng.matmul(ps_a[g % 3][:, e * L:(e + 1) * L], s.score_w[k][:, 2 * g + e, :],
                                                  xw[par][:, :, 0, :], start=(k == 0), stop=(k == 1))
                        last.then_inc(y_n, 1)

                def values(n, par):
                    for w in range(4):
                        if w == 0:
                            eng.wait_ge(yd_n, 2 * n + 1)
                        elif w == 1:
                            eng.wait_ge(ya_n, 2 * n + 2)
                        elif w == 2:
                            eng.wait_ge(yd_n, 2 * n + 2)
                        else:
                            eng.wait_ge(va_n, 4 * n + 1)
                            eng.wait_ge(vd_n, 4 * n + 1)
                        both = xw[par][:, w].rearrange("p a j -> p (a j)")
                        for k in range(2):
                            last = eng.matmul(ps_a[(w + 1) % 3][:, :], both, s.value_w[k][:, :], start=(k == 0), stop=(k == 1))
                        last.then_inc(v_n, 1)

                def convolution(n, par):
                    eng.wait_ge(xp_n, n + 1)
                    for tap in range(TAPS):
                        u, w = divmod(tap, 3)
                        last = eng.matmul(ps_x[:, 0:L].rearrange("p (r c) -> p r c", r=SIDE),
                                          s.tap_w[:, tap].rearrange("p k c -> p (k c)"),
                                          xp[par][:, u:u + SIDE, w:w + SIDE], start=(tap == 0), stop=(tap == TAPS - 1))
                    last.then_inc(conv_n, 1)

                def scores(n, par):
                    eng.wait_ge(ya_n, 2 * n + 2)
                    eng.wait_ge(yd_n, 2 * n + 2)
                    for t in range(2):
                        wait(eng, sub_n, 2 * n + t - 1)
                        for w in range(2):
                            cols = slice((2 * t + w) * WTOK, (2 * t + w + 1) * WTOK)
                            last = eng.matmul(ps_s[t][w * WTOK:(w + 1) * WTOK, :], xw[par][:, 2 * t + w, 0, :].bitcast(F32),
                                              y[:, :, cols], start=True, stop=True)
                        last.then_inc(s_n, 1)

                def turn_probs(n, t):
                    eng.wait_ge(prob_n, 2 * n + t + 1)
                    wait(eng, ptc_n, 2 * n + t)
                    for g in range(4):
                        last = eng.transpose(ps_t[:, g * P:(g + 1) * P],
                                             probs[t][:, 2 * g:2 * g + 2, :].rearrange("p h j -> p (h j)"), s.ident[:, :])
                    last.then_inc(pt_n, 1)

                def output(n, par, t):
                    eng.wait_ge(ptc_n, 2 * n + t + 1)
                    if t == 0:
                        eng.wait_ge(va_n, 4 * n + 4)
                        eng.wait_ge(vd_n, 4 * n + 4)
                        wait(eng, added_n, n)
                    for g in range(4):
                        last = eng.matmul(ps_o[:, t * P:(t + 1) * P], v[par][:, t, g].rearrange("p w c -> p (w c)"),
                                          probsT[t][:, g, :], start=(g == 0), stop=(g == 3))
                    last.then_inc(o_n, 1)

                def body(n, par):
                    scores(n, par)
                    if there(n + 1):
                        right_side(n + 1, 1 - par)
                        values(n + 1, 1 - par)
                    turn_probs(n, 0)
                    if there(n + 1):
                        convolution(n + 1, 1 - par)
                    turn_probs(n, 1)
                    output(n, par, 0)
                    if there(n + 2):
                        turn(n + 2, par)
                    output(n, par, 1)

                eng.wait_ge(zero_n, W2)
                turn(0, 0)
                right_side(0, 0)
                values(0, 0)
                convolution(0, 0)
                turn(1, 1)
                images(eng, body)

            @block.scalar
            def _(eng):
                def windows(n, par):
                    eng.wait_ge(turned_n, n + 1)
                    eng.activation(xw[par][:, :, :, :], ps_x[:, 0:L].rearrange("p (w j) -> p w j", w=4).unsqueeze(2).to_broadcast([P, 4, 2, WTOK]),
                                   ACT.Copy).then_inc(xw_n, 1)

                def right_side(n):
                    wait(eng, s_n, 2 * n)
                    for g in (0, 2):
                        eng.wait_ge(y_n, 4 * n + g + 1)
                        eng.activation(y[:, 2 * g:2 * g + 2, :], ps_a[g][:, :].rearrange("p (e l) -> p e l", e=2),
                                       ACT.Copy).then_inc(ya_n, 1)

                def values(n, par):
                    wait(eng, o_n, 2 * (n - 1))
                    for w in range(4):
                        eng.wait_ge(v_n, 4 * n + w + 1)
                        eng.activation(v[par][0:WTOK, w // 2, :, w % 2, :],
                                       ps_a[(w + 1) % 3][0:WTOK, :].rearrange("p (g e c) -> p g e c", e=2, c=C)[:, :, 0, :],
                                       ACT.Copy).then_inc(va_n, 1)

                def convolution(n):
                    eng.wait_ge(conv_n, n + 1)
                    eng.activation(s.conv[:, bass.ds(n * L, L)], ps_x[:, 0:L], ACT.Identity, bias=s.conv_bias[:, 0:1]).then_inc(convc_n, 1)

                def turned_probs(n, t):
                    eng.wait_ge(pt_n, 2 * n + t + 1)
                    wait(eng, o_n, 2 * n + t - 1)
                    eng.activation(probsT[t][:, :, :], ps_t[:, :].rearrange("p (g i) -> p g i", g=4), ACT.Copy).then_inc(ptc_n, 1)

                def body(n, par):
                    for t in range(2):
                        eng.wait_ge(sub_n, 2 * n + t + 1)
                        eng.activation(shifted[t][:, :, :], shifted[t][:, :, :], ACT.Exp).then_inc(exp_n, 1)
                    if there(n + 1):
                        right_side(n + 1)
                        values(n + 1, 1 - par)
                    turned_probs(n, 0)
                    if there(n + 1):
                        convolution(n + 1)
                    turned_probs(n, 1)
                    if there(n + 2):
                        windows(n + 2, par)

                windows(0, 0)
                right_side(0)
                values(0, 0)
                convolution(0)
                windows(1, 1)
                images(eng, body)

            @block.vector
            def _(eng):
                def padded(n, par):
                    eng.wait_ge(xw_n, n + 1)
                    wait(eng, conv_n, n - 1)
                    for nx in range(2):
                        for ny in range(2):
                            w = 2 * nx + ny
                            last = eng.tensor_copy(xp[par][:, 1 + nx * WIN:1 + (nx + 1) * WIN, 1 + ny * WIN:1 + (ny + 1) * WIN],
                                                   xw[par][:, w, 0, :].bitcast(F32).rearrange("p (r c) -> p r c", r=WIN))
                    last.then_inc(xp_n, 1)

                def right_side(n, g):
                    if g == 1:
                        wait(eng, s_n, 2 * n)
                    eng.wait_ge(y_n, 4 * n + g + 1)
                    eng.tensor_copy(y[:, 2 * g:2 * g + 2, :], ps_a[g % 3][:, :].rearrange("p (e l) -> p e l", e=2)).then_inc(yd_n, 1)

                def values(n, par, w):
                    if w == 0:
                        wait(eng, o_n, 2 * (n - 1))
                    eng.wait_ge(v_n, 4 * n + w + 1)
                    eng.tensor_copy(v[par][WTOK:P, w // 2, :, w % 2, :],
                                    ps_a[(w + 1) % 3][WTOK:P, :].rearrange("p (g e c) -> p g e c", e=2, c=C)[:, :, 1, :]).then_inc(vd_n, 1)

                def shift(n, t):
                    k = 2 * n + t
                    scores = ps_s[t][:, :].rearrange("p (h j) -> p h j", h=HEADS)
                    eng.wait_ge(s_n, k + 1)
                    eng.tensor_reduce(mx[t][:, :], scores, AX.X, ALU.max).then_inc(max_n, 1)
                    eng.wait_ge(max_n, k + 1)
                    wait(eng, prob_n, k - 1)
                    eng.tensor_tensor(shifted[t][:, :, :], scores,
                                      mx[t][:, :].unsqueeze(2).to_broadcast([P, HEADS, WTOK]), ALU.subtract).then_inc(sub_n, 1)

                def sums(n, t):
                    eng.wait_ge(exp_n, 2 * n + t + 1)
                    eng.tensor_reduce(den[t][:, :], shifted[t][:, :, :], AX.X, ALU.add).then_inc(den_n, 1)

                def inverse(n, t):
                    eng.wait_ge(den_n, 2 * n + t + 1)
                    eng.reciprocal(rden[t][:, :], den[t][:, :]).then_inc(rden_n, 1)

                def add(n):
                    eng.wait_ge(convc_n, n + 1)
                    eng.wait_ge(o_n, 2 * n + 2)
                    for t in range(2):
                        for w in range(2):
                            rows = slice(w * C, (w + 1) * C)
                            own_part = s.conv[rows, bass.ds(n * L + t * WIN * SIDE, WIN * SIDE)].rearrange(
                                "p (r c) -> p r c", c=SIDE)[:, :, w * WIN:(w + 1) * WIN]
                            last = eng.tensor_tensor(own_part, own_part,
                                                     ps_o[rows, t * P + w * WTOK:t * P + (w + 1) * WTOK].rearrange("p (r c) -> p r c", r=WIN),
                                                     ALU.add)
                    last.then_inc(added_n, 1)

                def body(n, par):
                    more = there(n + 1)
                    if more:
                        padded(n + 1, 1 - par)
                    shift(n, 0)
                    shift(n, 1)
                    if more:
                        right_side(n + 1, 1)
                    sums(n, 0)
                    if more:
                        right_side(n + 1, 3)
                    inverse(n, 0)
                    sums(n, 1)
                    if more:
                        values(n + 1, 1 - par, 0)
                    inverse(n, 1)
                    if more:
                        for w in range(1, 4):
                            values(n + 1, 1 - par, w)
                    if sym(n) or n > 0:
                        add(n - 1)

                padded(0, 0)
                right_side(0, 1)
                right_side(0, 3)
                for w in range(4):
                    values(0, 0, w)
                images(eng, body)
                add(BATCH - 1)


def axial_weights(nc, s, a, sem):
    with ExitStack() as own:
        def tmp(name, shape, dt=F32):
            return own.enter_context(nc.sbuf_tensor(name, shape, dt))

        raw = tmp("proj_raw", [P, 4, HC])
        padded = sem("wo_padded")
        loads, kept, scaled, split_n = sem("proj_loads"), sem("kept_loads"), sem("proj_scaled"), sem("proj_split")
        with nc.Block() as block:
            @block.sync
            def _(eng):
                for i, n in enumerate(("q", "k", "g", "v")):
                    for half in range(2):
                        eng.dma_start(raw[half * C:(half + 1) * C, i, :], a[f"L1_attn_W{n}"]).then_inc(loads, 16)
                x = a["x"].rearrange("b (h4 r) c e -> b (h4 r c) e", r=1).rearrange("b (g q) e -> q b g e", q=4)
                for q in range(4):
                    eng.dma_start(s.x1[q * BATCH:(q + 1) * BATCH, :, :], x[q]).then_inc(kept, 16)
                eng.wait_ge(padded, 2)
                eng.dma_start(s.wo[:, :, 0:C], a["L1_attn_Wo"].rearrange("(k p) n -> p k n", p=P)).then_inc(kept, 16)
                eng.dma_start(s.bo[0:C, :], a["L1_attn_bo"].rearrange("(p o) -> p o", o=1)).then_inc(kept, 16)
                for k in range(2):
                    eng.dma_start(s.bg[:, k:k + 1], a["L1_attn_bg"][k * P:(k + 1) * P].rearrange("(p o) -> p o", o=1)).then_inc(kept, 16)
                eng.dma_start(s.gamma[:, :], a["L1_attn_gamma"].partition_broadcast(P)).then_inc(kept, 16)
                eng.dma_start(s.beta[:, :], a["L1_attn_beta"].partition_broadcast(P)).then_inc(kept, 16)
                eng.wait_ge(kept, 16 * 10)

            @block.gpsimd
            def _(eng):
                eng.memset(s.wo[:, :, :], 0.0).then_inc(padded, 1)
                eng.memset(s.bo[:, :], 0.0).then_inc(padded, 1)

            @block.scalar
            def _(eng):
                eng.wait_ge(scaled, 1)
                eng.activation(s.proj[0][:, :, :], raw[:, :, :], ACT.Copy).then_inc(split_n, 1)

            @block.vector
            def _(eng):
                eng.wait_ge(loads, 16 * 8)
                eng.tensor_scalar(raw[:, 0, :], raw[:, 0, :], D ** -0.5 * L ** -0.5, None, ALU.mult).then_inc(scaled, 1)
                eng.wait_ge(split_n, 1)
                eng.tensor_tensor(s.proj[1][:, :, :], raw[:, :, :], s.proj[0][:, :, :].bitcast(F32), ALU.subtract).then_inc(split_n, 1)


GROUP = 4
GTOK = GROUP * P
GROUPS = TILES // GROUP


def sym(n):
    return not isinstance(n, int)


def wait(eng, semaphore, n):
    if sym(n) or n > 0:
        eng.wait_ge(semaphore, n)


def by_groups(eng, body):
    for g in range(2):
        body(g, g)
    with eng.Fori(1, GROUPS // 2) as i:
        for par in range(2):
            body(2 * i + par, par)


def layer_norm(eng, mine, x, b, roots_n, root_wait, sq_n, sq_wait, var_n, center_n, twice):
    wide = [P, GROUP, C]
    mine.then(eng.tensor_reduce(b.sum[:, :], x, AX.X, ALU.add))
    mine.then(eng.tensor_scalar(b.sum[:, :], b.sum[:, :], 1.0 / C, None, ALU.mult))
    eng.tensor_tensor(b.xc[:, :, :], x, b.sum[:, :].unsqueeze(2).to_broadcast(wide), ALU.subtract).then_inc(center_n, 1)
    eng.wait_ge(sq_n, sq_wait)
    mine.then(eng.tensor_reduce(b.var[:, :], b.sq[:, :, :], AX.X, ALU.add))
    eps = 1e-5
    if twice:
        ins = eng.tensor_scalar(b.var[:, :], b.var[:, :], (1 + eps) / C, eps * eps, ALU.mult, ALU.add)
    else:
        ins = eng.tensor_scalar(b.var[:, :], b.var[:, :], 1.0 / C, eps, ALU.mult, ALU.add)
    ins.then_inc(var_n, 1)
    eng.wait_ge(roots_n, root_wait)
    mine.then(eng.reciprocal(b.rstd[:, :], b.root[:, :]))
    newton(eng, mine, b.rstd[:, :], b.var[:, :], b.root[:, :])
    eng.wait_ge(center_n, sq_wait)
    mine.then(eng.tensor_tensor(b.xc[:, :, :], b.xc[:, :, :], b.rstd[:, :].unsqueeze(2).to_broadcast(wide), ALU.mult))


LN_STEPS = 9


class NormBuffers:

    def __init__(self, tmp, name):
        self.x = tmp(f"{name}_x", [P, GROUP, C])
        self.sum, self.var = tmp(f"{name}_sum", [P, GROUP]), tmp(f"{name}_var", [P, GROUP])
        self.rstd, self.root = tmp(f"{name}_rstd", [P, GROUP]), tmp(f"{name}_root", [P, GROUP])
        self.xc, self.sq = tmp(f"{name}_xc", [P, GROUP, C]), tmp(f"{name}_sq", [P, GROUP, C])
        self.hl = tmp(f"{name}_hl", [P, GROUP, P])


def axial_scores(nc, s, sem):
    with ExitStack() as own:
        def tmp(name, shape, dt=F32):
            return own.enter_context(nc.sbuf_tensor(name, shape, dt))

        b = NormBuffers(tmp, "ax")
        staged = [tmp(f"ax_staged{i}", [P, 16, BATCH]) for i in range(2)]
        qk = [tmp(f"ax_qk{i}", [P, 4, GROUP, BATCH, 4]) for i in range(2)]
        qkl = [tmp(f"ax_qkl{i}", [P, 4, 4, BATCH, 4]) for i in range(2)]
        zero = tmp("ax_zero", [P, 2 * P])
        att = tmp("ax_att", [P, 2, BATCH])
        attT = tmp("ax_attT", [P, 2, BATCH])
        top = tmp("ax_top", [P, 2])
        den = tmp("ax_den", [P, 2])

        def bank(name):
            return own.enter_context(nc.psum_tensor(name, [P, 512], F32))

        ps_f, ps_x, ps_a = bank("ax_ps_f"), bank("ax_ps_x"), bank("ax_ps_a")
        ps_qk = [bank(f"ax_ps_qk{i}") for i in range(4)]
        staged_n, f_n, res_n, center_n, sq_n, var_n, root_n = (sem("ax_staged_n"), sem("ax_f_n"), sem("ax_res_n"), sem("ax_center_n"),
                                                               sem("ax_sq_n"), sem("ax_var_n"), sem("ax_root_n"))
        z_n, hi_n, lo_n, x_n, xt_n, dve_n = sem("ax_z_n"), sem("ax_hi_n"), sem("ax_lo_n"), sem("ax_x_n"), sem("ax_xt_n"), sem("ax_dve_n")
        qk_n, q_c, k_c, moved_n, att_n, zero_n = (sem("ax_qk_n"), sem("ax_q_copied"), sem("ax_k_copied"),
                                                  [sem(f"ax_moved{i}") for i in range(2)], sem("ax_att_n"), sem("ax_zero_n"))
        top_n, exp_n, kept_n = sem("ax_top_n"), sem("ax_exp_n"), sem("ax_kept_n")
        MOVES = 16

        with nc.Block() as block:
            @block.gpsimd
            def _(eng):
                eng.memset(zero[:, :], 0.0).then_inc(zero_n, 1)
                eng.memset(s.att_w[:, :, :], 0.0).then_inc(zero_n, 1)
                eng.wait_ge(zero_n, 2)
                by_position = s.conv[:, :].rearrange("p (s l) -> p l s", l=L)

                def body(g, par):
                    wait(eng, f_n, g)
                    eng.tensor_copy(staged[par][:, :, :], by_position[:, bass.ds(16 * g, 16), :]).then_inc(staged_n, 1)
                    eng.wait_ge(res_n, g + 1)
                    eng.tensor_copy(s.x1[:, bass.ds(g * GROUP, GROUP), :], b.x[:, :, :]).then_inc(kept_n, 1)
                by_groups(eng, body)
                eng.wait_ge(kept_n, GROUPS)

            @block.sync
            def _(eng):
                def body(g, par):
                    eng.wait_ge(q_c, 2 * g + 2)
                    eng.wait_ge(k_c, 2 * g + 2)
                    wait(eng, att_n, g - par)
                    for h in range(4):
                        for t in range(GROUP):
                            eng.dma_start(qkl[par][t * D:(t + 1) * D, :, h, :, :].rearrange("p k s l -> p k (s l)"),
                                          qk[par][h * D:(h + 1) * D, :, t, :, :].rearrange("p k s l -> p k (s l)")).then_inc(moved_n[par], 16)
                by_groups(eng, body)

            @block.tensor
            def _(eng):
                eng.wait_ge(zero_n, 2)
                eng.matmul(ps_a[:, 0:2 * P], zero[:, 0:P], zero[:, :], start=True, stop=False, skip_group_check=True)

                def body(g, par):
                    eng.wait_ge(staged_n, g + 1)
                    wait(eng, res_n, g)
                    for t in range(GROUP):
                        last = eng.transpose(ps_f[:, t * P:(t + 1) * P],
                                             staged[par][:, 4 * t:4 * t + 4, :].rearrange("p l s -> p (l s)"), s.ident[:, :])
                    last.then_inc(f_n, 1)
                    eng.wait_ge(lo_n, g + 1)
                    eng.wait_ge(hi_n, g + 1)
                    for t in range(GROUP):
                        last = eng.transpose(ps_x[:, t * P:(t + 1) * P], b.hl[:, t, :], s.ident[:, :])
                    last.then_inc(x_n, 1)
                    eng.wait_ge(xt_n, g + 1)
                    wait(eng, q_c, 2 * g)
                    wait(eng, k_c, 2 * g)
                    for m in range(4):
                        for k in range(2):
                            last = eng.matmul(ps_qk[m][:, :], s.proj[k][:, m // 2, (m % 2) * P:(m % 2 + 1) * P],
                                              s.xt[:, bass.ds(g * GTOK, GTOK)], start=(k == 0), stop=(k == 1))
                        last.then_inc(qk_n, 1)

                def scores(half_round, par):
                    eng.wait_ge(moved_n[par], 16 * MOVES * (half_round + 1))
                    for l in range(4):
                        for k in range(2):
                            last = eng.matmul(ps_a[:, k * P:(k + 1) * P], qkl[par][:, k].rearrange("p h s l -> p (h s) l")[:, :, l],
                                              qkl[par][:, 2 + k].rearrange("p h s l -> p (h s) l")[:, :, l],
                                              start=False, stop=False, skip_group_check=True)
                    last.then_inc(att_n, 1)

                def both(i):
                    for par in range(2):
                        body(2 * i + par, par)
                    for par in range(2):
                        scores(i, par)
                both(0)
                with eng.Fori(1, GROUPS // 2) as i:
                    both(i)
                eng.matmul(ps_a[:, 0:2 * P], zero[:, 0:P], zero[:, :], start=False, stop=True, skip_group_check=True).then_inc(att_n, 1)

            @block.scalar
            def _(eng):
                def body(g, par):
                    eng.wait_ge(center_n, g + 1)
                    eng.activation(b.sq[:, :, :], b.xc[:, :, :], ACT.Square).then_inc(sq_n, 1)
                    eng.wait_ge(var_n, g + 1)
                    eng.activation(b.root[:, :], b.var[:, :], ACT.Sqrt).then_inc(root_n, 1)
                    eng.wait_ge(z_n, g + 1)
                    wait(eng, x_n, g)
                    eng.activation(b.hl[:, :, 0:C].bitcast(F32R), b.xc[:, :, :], ACT.Copy).then_inc(hi_n, 1)
                    eng.wait_ge(x_n, g + 1)
                    eng.activation(s.xt[:, bass.ds(g * GTOK, GTOK)], ps_x[:, :], ACT.Copy).then_inc(xt_n, 1)
                    for m in range(2):
                        eng.wait_ge(qk_n, 4 * g + m + 1)
                        if m == 0:
                            wait(eng, att_n, g - par)
                        eng.activation(qk[par][:, m].rearrange("p t s l -> p t l s"),
                                       ps_qk[m][:, :].rearrange("p (t l s) -> p t l s", t=GROUP, l=4), ACT.Copy).then_inc(q_c, 1)
                by_groups(eng, body)
                eng.wait_ge(top_n, 1)
                eng.activation(att[:, :, :], att[:, :, :], ACT.Exp).then_inc(exp_n, 1)

            @block.vector
            def _(eng):
                mine = Steps(eng, dve_n, 1 + LN_STEPS + 1)

                def body(g, par):
                    mine.round(g)
                    tiles = s.x1[:, bass.ds(g * GROUP, GROUP), :]
                    folded = ps_f[:, :].rearrange("p (t k c) -> p t k c", t=GROUP, k=2)
                    eng.wait_ge(f_n, g + 1)
                    mine.then(eng.tensor_tensor(tiles, tiles, folded[:, :, 0, :], ALU.add))
                    wait(eng, kept_n, g)
                    eng.tensor_tensor(b.x[:, :, :], tiles, folded[:, :, 1, :], ALU.add).then_inc(res_n, 1)
                    wait(eng, lo_n, g)
                    eng.wait_ge(res_n, g + 1)
                    layer_norm(eng, mine, b.x[:, :, :], b, root_n, g + 1, sq_n, g + 1, var_n, center_n, True)
                    wide = [P, GROUP, C]
                    mine.then(eng.tensor_tensor(b.xc[:, :, :], b.xc[:, :, :], s.gamma[:, :].unsqueeze(1).to_broadcast(wide), ALU.mult))
                    eng.tensor_tensor(b.xc[:, :, :], b.xc[:, :, :], s.beta[:, :].unsqueeze(1).to_broadcast(wide), ALU.add).then_inc(z_n, 1)
                    eng.wait_ge(hi_n, g + 1)
                    eng.wait_ge(z_n, g + 1)
                    eng.tensor_tensor(b.hl[:, :, C:2 * C], b.xc[:, :, :], b.hl[:, :, 0:C], ALU.subtract).then_inc(lo_n, 1)
                    for m in range(2):
                        eng.wait_ge(qk_n, 4 * g + m + 3)
                        if m == 0:
                            wait(eng, att_n, g - par)
                        eng.tensor_copy(qk[par][:, 2 + m].rearrange("p t s l -> p t l s"),
                                        ps_qk[2 + m][:, :].rearrange("p (t l s) -> p t l s", t=GROUP, l=4)).then_inc(k_c, 1)
                by_groups(eng, body)
                mine = Steps(eng, sem("ax_softmax_dve"))
                eng.wait_ge(att_n, GROUPS + 1)
                for h in range(4):
                    rows = slice(h * BATCH, (h + 1) * BATCH)
                    mine.did(eng.tensor_copy(att[rows, :, :], ps_a[rows, 0:2 * P].rearrange("p (k n) -> p k n", k=2)[:, :, rows]))
                mine.settle()
                mine.then(eng.tensor_reduce(top[:, :], att[:, :, :], AX.X, ALU.max))
                eng.tensor_tensor(att[:, :, :], att[:, :, :], top[:, :].unsqueeze(2).to_broadcast([P, 2, BATCH]), ALU.subtract).then_inc(top_n, 1)
                eng.wait_ge(exp_n, 1)
                mine.then(eng.tensor_reduce(den[:, :], att[:, :, :], AX.X, ALU.add))
                mine.then(eng.reciprocal(top[:, :], den[:, :]))
                mine.then(eng.tensor_tensor(att[:, :, :], att[:, :, :], top[:, :].unsqueeze(2).to_broadcast([P, 2, BATCH]), ALU.mult))
                mine.then(eng.transpose(attT[:, :, :].rearrange("p k s -> p (k s)"), att[:, :, :].rearrange("p k s -> p (k s)")))
                for h in range(4):
                    for q in range(4):
                        rows = slice(q * BATCH, (q + 1) * BATCH)
                        mine.did(eng.tensor_copy(s.att_w[rows, h::4, rows], attT[h * BATCH:(h + 1) * BATCH, :, :]))
                mine.settle()


def axial_values(nc, s, sem):
    with ExitStack() as own:
        def tmp(name, shape, dt=F32):
            return own.enter_context(nc.sbuf_tensor(name, shape, dt))

        xs = [tmp(f"av_x{i}", [P, GTOK], F32R) for i in range(2)]
        v = [tmp(f"av_v{i}", [P, GROUP, HC]) for i in range(2)]
        gate = [tmp(f"av_gate{i}", [P, 2, GTOK]) for i in range(2)]
        o = [tmp(f"av_o{i}", [P, GROUP, HC]) for i in range(2)]
        og = [tmp(f"av_og{i}", [P, 2, GTOK]) for i in range(2)]
        ao = [tmp(f"av_ao{i}", [P, GTOK]) for i in range(2)]

        def bank(name):
            return own.enter_context(nc.psum_tensor(name, [P, 512], F32))

        ps_v, ps_o, ps_t = ([bank(f"av_ps_{n}{i}") for i in range(2)] for n in "vot")
        ps_w, ps_r = bank("av_ps_w"), bank("av_ps_r")
        xs_n, v_n, v_c, g_n, g_c, o_n, o_c = (sem(f"av_{n}") for n in ("x_staged", "v_done", "v_copied", "g_done", "g_copied", "o_done", "o_copied"))
        t_n, og_n, w_n, ao_n, r_n, res_n = (sem(f"av_{n}") for n in ("turned", "gated", "projected", "ao_copied", "ao_turned", "residual"))

        with nc.Block() as block:
            @block.gpsimd
            def _(eng):
                def body(g, par):
                    wait(eng, g_n, 2 * (g - par))
                    eng.tensor_copy(xs[par][:, :], s.xt[:, bass.ds(g * GTOK, GTOK)].bitcast(F32)).then_inc(xs_n, 1)
                by_groups(eng, body)

            @block.tensor
            def _(eng):
                def body(g, par):
                    eng.wait_ge(xs_n, g + 1)
                    wait(eng, g_c, 2 * g)
                    for t in range(GROUP):
                        for k in range(2):
                            last = eng.matmul(ps_v[t // 2][:, (t % 2) * HC:(t % 2 + 1) * HC], xs[par][:, t * P:(t + 1) * P],
                                              s.proj[k][:, 3, :], start=(k == 0), stop=(k == 1))
                        if t % 2:
                            last.then_inc(v_n, 1)
                    for m in range(2):
                        eng.wait_ge(v_c, 2 * g + m + 1)
                        for k in range(2):
                            last = eng.matmul(ps_v[m][:, :], s.proj[k][:, 2, m * P:(m + 1) * P], xs[par][:, :],
                                              start=(k == 0), stop=(k == 1))
                        last.then_inc(g_n, 1)
                    eng.wait_ge(v_c, 2 * g + 2)
                    wait(eng, o_c, 2 * g)
                    for h in range(HEADS):
                        last = eng.matmul(ps_o[h // 4][:, (h % 4) * P:(h % 4 + 1) * P].rearrange("p (t c) -> p t c", t=GROUP),
                                          s.att_w[:, h, :], v[par][:, :, h * D:(h + 1) * D], start=True, stop=True)
                        if h % 4 == 3:
                            last.then_inc(o_n, 1)
                    eng.wait_ge(o_c, 2 * g + 2)
                    wait(eng, og_n, 2 * g)
                    for m in range(2):
                        for t in range(GROUP):
                            last = eng.transpose(ps_t[m][:, t * P:(t + 1) * P], o[par][:, t, m * P:(m + 1) * P], s.ident[:, :])
                        last.then_inc(t_n, 1)
                    eng.wait_ge(og_n, 2 * g + 2)
                    wait(eng, ao_n, g)
                    for m in range(2):
                        last = eng.matmul(ps_w[:, :], s.wo[:, m, :], og[par][:, m, :], start=(m == 0), stop=(m == 1))
                    last.then_inc(w_n, 1)
                    eng.wait_ge(ao_n, g + 1)
                    wait(eng, res_n, g)
                    for t in range(GROUP):
                        last = eng.transpose(ps_r[:, t * P:(t + 1) * P], ao[par][:, t * P:(t + 1) * P], s.ident[:, :])
                    last.then_inc(r_n, 1)
                by_groups(eng, body)

            @block.scalar
            def _(eng):
                def body(g, par):
                    wait(eng, t_n, 2 * (g - par))
                    wait(eng, og_n, 2 * (g - par))
                    for m in range(2):
                        eng.wait_ge(g_n, 2 * g + m + 1)
                        eng.activation(gate[par][:, m, :], ps_v[m][:, :], ACT.Sigmoid, bias=s.bg[:, m:m + 1]).then_inc(g_c, 1)
                    for m in range(2):
                        eng.wait_ge(o_n, 2 * g + m + 1)
                        eng.activation(o[par][:, :, m * P:(m + 1) * P].rearrange("p t (h c) -> p h t c", c=D),
                                       ps_o[m][:, :].rearrange("p (h t c) -> p h t c", h=4, t=GROUP), ACT.Copy).then_inc(o_c, 1)
                    eng.wait_ge(w_n, g + 1)
                    eng.activation(ao[par][:, :], ps_w[:, :], ACT.Identity, bias=s.bo[:, 0:1]).then_inc(ao_n, 1)
                by_groups(eng, body)

            @block.vector
            def _(eng):
                def body(g, par):
                    for m in range(2):
                        eng.wait_ge(v_n, 2 * g + m + 1)
                        if m == 0:
                            wait(eng, o_n, 2 * (g - par))
                        eng.tensor_copy(v[par][:, 2 * m:2 * m + 2, :], ps_v[m][:, :].rearrange("p (t n) -> p t n", t=2)).then_inc(v_c, 1)
                    for m in range(2):
                        eng.wait_ge(t_n, 2 * g + m + 1)
                        eng.wait_ge(g_c, 2 * g + m + 1)
                        if m == 0:
                            wait(eng, w_n, g - par)
                        eng.tensor_tensor(og[par][:, m, :], ps_t[m][:, :], gate[par][:, m, :], ALU.mult).then_inc(og_n, 1)
                    eng.wait_ge(r_n, g + 1)
                    tiles = s.x1[:, bass.ds(g * GROUP, GROUP), :]
                    eng.tensor_tensor(tiles, tiles, ps_r[:, :].rearrange("p (t c) -> p t c", c=P)[:, :, 0:C], ALU.add).then_inc(res_n, 1)
                by_groups(eng, body)


EXPERTS, HID = 8, 682
HCHUNK, HCHUNKS = 114, 6
HPAD = HCHUNK * HCHUNKS
SLOT = 512
FTILES = 2 * TOK // SLOT + EXPERTS - 1
SLOTS = FTILES * SLOT
EXPERT_ROWS = TOK // SLOT
R = SLOT // P
ROW = C + 2


def expert_weights(nc, s, a, sem):
    with ExitStack() as own:
        def tmp(name, shape, dt=F32):
            return own.enter_context(nc.sbuf_tensor(name, shape, dt))

        w13 = [tmp(f"w13_in{i}", [HCHUNK, 2, HCHUNKS, 2, C]) for i in range(2)]
        w2 = [tmp(f"w2_in{i}", [C, HPAD]) for i in range(2)]
        ps = [own.enter_context(nc.psum_tensor(f"ew_ps{i}", [P, 512], F32)) for i in range(6)]
        zeroed, in_n, turned, hi_n, lo_n, w2_n = (sem(f"ew_{n}") for n in ("zeroed", "loads", "turned", "hi", "lo", "w2"))
        in_n, sent = [in_n, sem("ew_loads_odd")], sem("ew_tokens_sent")
        LOADS = 2 * 2 * 2 + 1
        HALF = HCHUNKS // 2

        with nc.Block() as block:
            @block.gpsimd
            def _(eng):
                for i in range(2):
                    eng.memset(w13[i][:, :, HCHUNKS - 1], 0.0).then_inc(zeroed, 1)
                    eng.memset(w2[i][:, HID:HPAD], 0.0).then_inc(zeroed, 1)
                for t in range(TILES):
                    for k in range(2):
                        eng.indirect_dma_start(s.slot_x[:, :], bass.IndirectOffsetOnAxis(s.slot[k][:, t:t + 1], 0),
                                               s.rows[k][:, t, :], None).then_inc(sent, 16)
                eng.wait_ge(sent, 16 * 2 * TILES)

            @block.sync
            def _(eng):
                eng.wait_ge(zeroed, 4)
                whole = (HCHUNKS - 1) * HCHUNK
                for e in range(EXPERTS):
                    i = e % 2
                    if e >= 2:
                        eng.wait_ge(turned, 5 * (e - 1))
                    for m, name in enumerate(("w1", "w3")):
                        w = a[f"L1_ffn_{name}"][e]
                        for twice in range(2):
                            eng.dma_start(w13[i][:, m, 0:HCHUNKS - 1, twice, :],
                                          w[0:whole, :].rearrange("(k p) c -> p k c", p=HCHUNK)).then_inc(in_n[i], 16)
                            eng.dma_start(w13[i][0:HID - whole, m, HCHUNKS - 1, twice, :], w[whole:HID, :]).then_inc(in_n[i], 16)
                    eng.dma_start(w2[i][:, 0:HID], a["L1_ffn_w2"][e]).then_inc(in_n[i], 16)

            @block.tensor
            def _(eng):
                for e in range(EXPERTS):
                    i = e % 2
                    eng.wait_ge(in_n[i], 16 * LOADS * (e // 2 + 1))
                    for part in range(4):
                        m, half = divmod(part, 2)
                        if e >= 1:
                            eng.wait_ge(lo_n, 4 * (e - 1) + part + 1)
                        for k in range(HALF):
                            last = eng.transpose(ps[part][:, k * HCHUNK:(k + 1) * HCHUNK],
                                                 w13[i][:, m, half * HALF + k].rearrange("p a c -> p (a c)"), s.ident[0:HCHUNK, 0:HCHUNK])
                        last.then_inc(turned, 1)
                    if e >= 2:
                        eng.wait_ge(w2_n, e - 1)
                    for k in range(HCHUNKS):
                        last = eng.transpose(ps[4 + i][0:HCHUNK, k * C:(k + 1) * C], w2[i][:, k * HCHUNK:(k + 1) * HCHUNK], s.ident[0:C, 0:C])
                    last.then_inc(turned, 1)

            def halves(w, e, m, half):
                return w[:, e, m, half * HALF * HCHUNK:(half + 1) * HALF * HCHUNK]

            @block.scalar
            def _(eng):
                for e in range(EXPERTS):
                    for part in range(4):
                        eng.wait_ge(turned, 5 * e + part + 1)
                        eng.activation(halves(s.w13[0], e, *divmod(part, 2)), ps[part][:, 0:HALF * HCHUNK], ACT.Copy).then_inc(hi_n, 1)

            @block.vector
            def _(eng):
                for e in range(EXPERTS):
                    for part in range(4):
                        eng.wait_ge(hi_n, 4 * e + part + 1)
                        eng.tensor_tensor(halves(s.w13[1], e, *divmod(part, 2)), ps[part][:, 0:HALF * HCHUNK],
                                          halves(s.w13[0], e, *divmod(part, 2)).bitcast(F32), ALU.subtract).then_inc(lo_n, 1)
                    eng.wait_ge(turned, 5 * e + 5)
                    eng.tensor_copy(s.w2[:, e, :], ps[4 + e % 2][0:HCHUNK, 0:HCHUNKS * C]).then_inc(w2_n, 1)


def route(nc, s, a, sem):
    with ExitStack() as own:
        def tmp(name, shape, dt=F32):
            return own.enter_context(nc.sbuf_tensor(name, shape, dt))

        b = NormBuffers(tmp, "rt")
        xt = [tmp(f"rt_xt{i}", [P, GTOK]) for i in range(2)]
        logits = tmp("rt_logits", [P, TILES, EXPERTS])
        probs, work = tmp("rt_probs", [P, TILES, EXPERTS]), tmp("rt_work", [P, TILES, EXPERTS])
        pick = [tmp(f"rt_pick{k}", [P, TILES, EXPERTS]) for k in range(2)]
        number = tmp("rt_number", [P, EXPERTS])
        best = [tmp(f"rt_best{k}", [P, TILES]) for k in range(2)]
        small = tmp("rt_small", [P, TILES])
        before, ones = tmp("rt_before", [P, P]), tmp("rt_ones", [P, P])
        total, ahead = tmp("rt_total", [P, EXPERTS, TILES]), tmp("rt_ahead", [P, EXPERTS, TILES])
        one_row = tmp("rt_one_row", [P, TILES])
        step = tmp("rt_step", [P, EXPERT_ROWS])
        over = tmp("rt_over", [P, EXPERTS, EXPERT_ROWS])
        count, end, start = tmp("rt_count", [P, EXPERTS]), tmp("rt_end", [P, EXPERTS]), tmp("rt_start", [P, EXPERTS])
        slot_f = tmp("rt_slot_f", [P, TILES])
        tile_no = tmp("rt_tile_no", [P, FTILES])
        past = tmp("rt_past", [P, FTILES, EXPERTS])
        owner = tmp("rt_owner", [P, FTILES])

        def bank(name):
            return own.enter_context(nc.psum_tensor(name, [P, 512], F32))

        ps_x, ps_l, ps_p, ps_c = bank("rt_ps_x"), bank("rt_ps_l"), bank("rt_ps_p"), bank("rt_ps_c")
        center_n, sq_n, var_n, root_n, z_n, hi_n, lo_n, x_n, xt_n, l_n, lc_n, dve_n = (
            sem(f"rt_{n}") for n in ("center", "sq", "var", "root", "z", "hi", "lo", "x", "xt", "logit", "logit_copied", "dve"))
        const_n, max_n, exp_n, picked_n, ranked_n, slots_n, zero_n = (
            sem(f"rt_{n}") for n in ("const", "max", "exp", "picked", "ranked", "slots", "zero_slots"))
        rw_n = sem("rt_router_loads")
        filled_n, staged_n, ids_n = sem("rt_filled"), sem("rt_staged"), sem("rt_ids")
        blank = tmp("rt_blank", [P, R, ROW])

        with nc.Block() as block:
            @block.sync
            def _(eng):
                for half in range(2):
                    eng.dma_start(s.router[half * C:(half + 1) * C, :], a["L1_ffn_router_w"].rearrange("e c -> c e"),
                                  allow_slow_non_contiguous=True).then_inc(rw_n, 16)
                eng.wait_ge(filled_n, 2)
                eng.dma_start(s.slot_x[:, :].rearrange("(k p r) c -> p k (r c)", p=P, r=R),
                              blank[:, :, :].rearrange("p r c -> p (r c)").unsqueeze(1).to_broadcast([P, FTILES, R * ROW])).then_inc(zero_n, 16)
                rows = s.summed[0:TOK, :].rearrange("(b g q) e -> q b g e", b=BATCH, q=4)
                for q in range(4):
                    eng.dma_start(rows[q], s.x1[q * BATCH:(q + 1) * BATCH, :, :]).then_inc(zero_n, 16)
                eng.dma_start(s.summed[TOK:TOK + SLOT, :].rearrange("(p r) c -> p r c", p=P), blank[:, :, 0:C]).then_inc(zero_n, 16)
                eng.wait_ge(zero_n, 16 * 6)

            @block.gpsimd
            def _(eng):
                eng.memset(blank[:, :, :], 0.0).then_inc(filled_n, 1)
                eng.wait_ge(filled_n, 1)
                for q in range(4):
                    wait(eng, ids_n, q)
                    eng.iota(s.rows[0][q * BATCH:(q + 1) * BATCH, :, C + 1].bitcast(mybir.dt.int32), pattern=[[4, TILES]], base=q,
                             channel_multiplier=L).then_inc(ids_n, 1)
                eng.wait_ge(ids_n, 4)
                eng.tensor_copy(s.rows[1][:, :, C + 1].bitcast(mybir.dt.int32), s.rows[0][:, :, C + 1].bitcast(mybir.dt.int32)).then_inc(ids_n, 1)
                eng.wait_ge(filled_n, 1)
                eng.iota(blank[:, :, C + 1].bitcast(mybir.dt.int32), pattern=[[1, R]], base=TOK, channel_multiplier=R).then_inc(filled_n, 1)
                eng.memset(ones[:, :], 1.0).then_inc(const_n, 1)
                eng.memset(one_row[:, :], 1.0).then_inc(const_n, 1)
                eng.wait_ge(const_n, 2)
                eng.affine_select(out=before[:, :], in_=ones[:, :], compare_op=ALU.is_gt, fill=0.0, base=0,
                                  pattern=[[1, P]], channel_multiplier=-1).then_inc(const_n, 1)
                for t, n, by in ((number, EXPERTS, 1), (step, EXPERT_ROWS, SLOT), (tile_no, FTILES, 1)):
                    eng.iota(t[:, :], pattern=[[by, n]], base=0, channel_multiplier=0,
                             allow_small_or_imprecise_dtypes=True).then_inc(const_n, 1)

                def body(g, par):
                    wait(eng, center_n, g)
                    eng.tensor_copy(b.x[:, :, :], s.x1[:, bass.ds(g * GROUP, GROUP), :]).then_inc(staged_n, 1)
                by_groups(eng, body)
                eng.wait_ge(ids_n, 5)

            @block.tensor
            def _(eng):
                eng.wait_ge(rw_n, 32)

                def body(g, par):
                    eng.wait_ge(hi_n, g + 1)
                    eng.wait_ge(lo_n, g + 1)
                    for t in range(GROUP):
                        last = eng.transpose(ps_x[:, t * P:(t + 1) * P], b.hl[:, t, :], s.ident[:, :])
                    last.then_inc(x_n, 1)
                    eng.wait_ge(xt_n, g + 1)
                    wait(eng, lc_n, g)
                    for t in range(GROUP):
                        last = eng.matmul(ps_l[:, t * EXPERTS:(t + 1) * EXPERTS], xt[par][:, t * P:(t + 1) * P], s.router[:, :],
                                          start=True, stop=True)
                    last.then_inc(l_n, 1)
                by_groups(eng, body)
                eng.wait_ge(const_n, 3)
                eng.wait_ge(picked_n, 1)
                chosen = work[:, :, :].rearrange("p t e -> p (t e)")
                eng.matmul(ps_p[:, :], before[:, :], chosen, start=True, stop=True)
                eng.matmul(ps_c[:, :], ones[:, :], chosen, start=True, stop=True).then_inc(ranked_n, 1)

            @block.scalar
            def _(eng):
                def body(g, par):
                    eng.wait_ge(center_n, g + 1)
                    eng.activation(b.sq[:, :, :], b.xc[:, :, :], ACT.Square).then_inc(sq_n, 1)
                    eng.wait_ge(var_n, g + 1)
                    eng.activation(b.root[:, :], b.var[:, :], ACT.Sqrt).then_inc(root_n, 1)
                    eng.wait_ge(z_n, 2 * g + 2)
                    wait(eng, x_n, g)
                    eng.activation(b.hl[:, :, 0:C].bitcast(F32R), b.xc[:, :, :], ACT.Copy).then_inc(hi_n, 1)
                    eng.wait_ge(x_n, g + 1)
                    eng.activation(xt[par][:, :], ps_x[:, :], ACT.Copy).then_inc(xt_n, 1)
                by_groups(eng, body)
                eng.wait_ge(max_n, 1)
                eng.activation(work[:, :, :], work[:, :, :], ACT.Exp).then_inc(exp_n, 1)

            @block.vector
            def _(eng):
                mine = Steps(eng, dve_n, LN_STEPS)

                def body(g, par):
                    mine.round(g)
                    wait(eng, lo_n, g)
                    eng.wait_ge(staged_n, g + 1)
                    layer_norm(eng, mine, b.x[:, :, :], b, root_n, g + 1, sq_n, g + 1, var_n, center_n, False)
                    for k in range(2):
                        eng.tensor_copy(s.rows[k][:, bass.ds(g * GROUP, GROUP), 0:C], b.xc[:, :, :]).then_inc(z_n, 1)
                    eng.wait_ge(hi_n, g + 1)
                    eng.tensor_tensor(b.hl[:, :, C:2 * C], b.xc[:, :, :], b.hl[:, :, 0:C], ALU.subtract).then_inc(lo_n, 1)
                    eng.wait_ge(l_n, g + 1)
                    eng.tensor_copy(logits[:, bass.ds(g * GROUP, GROUP), :],
                                    ps_l[:, 0:GROUP * EXPERTS].rearrange("p (t e) -> p t e", e=EXPERTS)).then_inc(lc_n, 1)
                by_groups(eng, body)
                wide = [P, TILES, EXPERTS]
                mine = Steps(eng, sem("rt_pick_dve"))

                def over_experts(t):
                    return t[:, :].unsqueeze(2).to_broadcast(wide)

                def over_tokens(t):
                    return t[:, :].unsqueeze(1).to_broadcast(wide)

                eng.wait_ge(lc_n, GROUPS)
                eng.wait_ge(const_n, 6)
                mine.then(eng.tensor_reduce(small[:, :], logits[:, :, :], AX.X, ALU.max))
                eng.tensor_tensor(work[:, :, :], logits[:, :, :], over_experts(small), ALU.subtract).then_inc(max_n, 1)
                eng.wait_ge(exp_n, 1)
                mine.then(eng.tensor_reduce(small[:, :], work[:, :, :], AX.X, ALU.add))
                mine.then(eng.reciprocal(small[:, :], small[:, :]))
                mine.then(eng.tensor_tensor(probs[:, :, :], work[:, :, :], over_experts(small), ALU.mult))
                for k in range(2):
                    mine.then(eng.tensor_reduce(best[k][:, :], probs[:, :, :], AX.X, ALU.max))
                    mine.then(eng.tensor_tensor(work[:, :, :], probs[:, :, :], over_experts(best[k]), ALU.is_lt))
                    mine.then(eng.tensor_scalar(work[:, :, :], work[:, :, :], float(EXPERTS), None, ALU.mult))
                    mine.then(eng.tensor_tensor(work[:, :, :], work[:, :, :], over_tokens(number), ALU.add))
                    mine.then(eng.tensor_reduce(small[:, :], work[:, :, :], AX.X, ALU.min))
                    mine.then(eng.tensor_tensor(pick[k][:, :, :], over_tokens(number), over_experts(small), ALU.is_equal))
                    if k == 0:
                        mine.then(eng.tensor_scalar(work[:, :, :], pick[0][:, :, :], 2.0, None, ALU.mult))
                        mine.then(eng.tensor_tensor(probs[:, :, :], probs[:, :, :], work[:, :, :], ALU.subtract))
                eng.tensor_tensor(work[:, :, :], pick[0][:, :, :], pick[1][:, :, :], ALU.add).then_inc(picked_n, 1)
                mine.then(eng.tensor_tensor(small[:, :], best[0][:, :], best[1][:, :], ALU.add))
                mine.then(eng.tensor_scalar(small[:, :], small[:, :], 1e-9, None, ALU.add))
                mine.then(eng.reciprocal(small[:, :], small[:, :]))
                for k in range(2):
                    mine.did(eng.tensor_tensor(s.rows[k][:, :, C], best[k][:, :], small[:, :], ALU.mult))
                eng.wait_ge(ranked_n, 1)
                mine.then(eng.tensor_copy(total[:, :, :], ps_c[:, :].rearrange("p (t e) -> p e t", e=EXPERTS)))
                for e in range(EXPERTS):
                    mine.did(eng.tensor_tensor_scan(ahead[:, e, :], one_row[:, :], total[:, e, :], 0.0, ALU.mult, ALU.add))
                mine.settle()
                mine.then(eng.tensor_tensor(over[:, :, :], ahead[:, :, TILES - 1:TILES].to_broadcast([P, EXPERTS, EXPERT_ROWS]),
                                            step[:, :].unsqueeze(1).to_broadcast([P, EXPERTS, EXPERT_ROWS]), ALU.is_gt))
                mine.then(eng.tensor_reduce(count[:, :], over[:, :, :], AX.X, ALU.add))
                mine.then(eng.tensor_tensor_scan(end[:, :], one_row[:, 0:EXPERTS], count[:, :], 0.0, ALU.mult, ALU.add))
                mine.then(eng.tensor_tensor(start[:, :], end[:, :], count[:, :], ALU.subtract))
                mine.then(eng.tensor_scalar(start[:, :], start[:, :], float(SLOT), None, ALU.mult))
                mine.then(eng.tensor_tensor(ahead[:, :, :], ahead[:, :, :], total[:, :, :], ALU.subtract))
                mine.then(eng.tensor_tensor(ahead[:, :, :], ahead[:, :, :], start[:, :].unsqueeze(2).to_broadcast([P, EXPERTS, TILES]), ALU.add))
                mine.then(eng.tensor_tensor(probs[:, :, :], ps_p[:, :].rearrange("p (t e) -> p t e", e=EXPERTS),
                                            ahead[:, :, :].rearrange("p e t -> p t e"), ALU.add))
                for k in range(2):
                    mine.then(eng.tensor_tensor(work[:, :, :], probs[:, :, :], pick[k][:, :, :], ALU.mult))
                    mine.then(eng.tensor_reduce(slot_f[:, :], work[:, :, :], AX.X, ALU.add))
                    eng.tensor_copy(s.slot[k][:, :], slot_f[:, :]).then_inc(slots_n, 1)
                    eng.wait_ge(slots_n, k + 1)
                mine.then(eng.tensor_tensor(past[:, :, :], tile_no[:, :].unsqueeze(2).to_broadcast([P, FTILES, EXPERTS]),
                                            end[:, :].unsqueeze(1).to_broadcast([P, FTILES, EXPERTS]), ALU.is_ge))
                mine.then(eng.tensor_reduce(owner[:, :], past[:, :, :], AX.X, ALU.add))
                mine.then(eng.tensor_scalar(owner[:, :], owner[:, :], float(EXPERTS - 1), None, ALU.min))
                mine.then(eng.tensor_copy(s.owner[:, :], owner[:, :]))


def experts(nc, s, sem):
    with ExitStack() as own:
        def tmp(name, shape, dt=F32):
            return own.enter_context(nc.sbuf_tensor(name, shape, dt))

        x = [tmp(f"ex_x{i}", [P, R, ROW]) for i in range(4)]
        hl = tmp("ex_hl", [P, R, P])
        xt = [tmp(f"ex_xt{i}", [P, SLOT], F32R) for i in range(2)]
        w13 = [[tmp(f"ex_w13_{i}{k}", [P, 2, HPAD], F32R) for k in range(2)] for i in range(2)]
        w2 = [tmp(f"ex_w2_{i}", [HCHUNK, HCHUNKS, P]) for i in range(2)]
        act = [tmp(f"ex_act{i}", [HCHUNK, SLOT]) for i in range(2)]
        h = tmp("ex_h", [HCHUNK, HCHUNKS, SLOT])
        y = tmp("ex_y", [P, SLOT])
        out = [tmp(f"ex_out{i}", [P, R, C]) for i in range(2)]

        def bank(name):
            return own.enter_context(nc.psum_tensor(name, [P, 512], F32))

        ps_x, ps_y, ps_o = bank("ex_ps_x"), bank("ex_ps_y"), bank("ex_ps_o")
        ps_1, ps_3 = [bank(f"ex_ps_1{i}") for i in range(2)], [bank(f"ex_ps_3{i}") for i in range(2)]
        x_in = [sem(f"ex_x_in{i}") for i in range(4)]
        hi_n, lo_n, x_n, xt_n, w13_n, w2_n, h1_n, h3_n, act_n, h_n, y_n, yc_n, o_n, oc_n, padded = (
            sem(f"ex_{n}") for n in ("hi", "lo", "x", "xt", "w13", "w2", "h1", "h3", "act", "h", "y", "y_copied", "o", "o_copied", "padded"))
        added = sem("ex_added")
        slot_x = s.slot_x[:, :].rearrange("(k p r) c -> k p r c", p=P, r=R)
        LAST = FTILES - 1
        FIRST = 3
        ROUNDS = (FTILES - FIRST - 1) // 4

        def run(eng, body):
            for k in range(FIRST):
                body(k, k % 4, k // 4)
            with eng.Fori(0, ROUNDS) as i:
                for u in range(4):
                    k = FIRST + u
                    body(4 * i + k, k % 4, i + k // 4)
            for k in range(FIRST + 4 * ROUNDS, FTILES):
                body(k, k % 4, k // 4)

        with nc.Block() as block:
            @block.sync
            def _(eng):
                def load(k, buf):
                    eng.dma_start(x[buf][:, :, :], slot_x[bass.ds(k, 1)].rearrange("o p r c -> (o p) r c")).then_inc(x_in[buf], 16)

                def body(k, buf, quarter):
                    if sym(k) or k + 4 <= LAST:
                        eng.wait_ge(added, 16 * R * (k + 1))
                        load(k + 4, buf)
                for k in range(4):
                    load(k, k)
                for k in range(FIRST):
                    body(k, k % 4, 0)
                with eng.Fori(0, ROUNDS - 1) as i:
                    for u in range(4):
                        body(4 * i + FIRST + u, (FIRST + u) % 4, 0)
                for k in range(FIRST + 4 * (ROUNDS - 1), FTILES):
                    body(k, k % 4, 0)

            @block.gpsimd
            def _(eng):
                for i in range(2):
                    eng.memset(w2[i][:, :, :], 0.0).then_inc(padded, 1)
                eng.wait_ge(padded, 2)

                def weights(k, par):
                    e = eng.value_load(s.owner[0:1, bass.ds(k, 1)], min_val=0, max_val=EXPERTS - 1)
                    eng.tensor_copy(w2[par][:, :, 0:C], s.w2[:, bass.ds(e, 1), :].rearrange("p o (k c) -> p (o k) c", c=C)).then_inc(w2_n, 1)

                def body(k, buf, quarter):
                    wait(eng, added, 16 * R * k)
                    eng.wait_ge(oc_n, k + 1)
                    if sym(k) or k + 2 <= LAST:
                        weights(k + 2, buf % 2)
                    for j in range(R):
                        eng.indirect_dma_start(s.summed[:, :], bass.IndirectOffsetOnAxis(x[buf][:, j, C + 1:C + 2].bitcast(mybir.dt.uint32), 0),
                                               out[buf % 2][:, j, :], None, compute_op=ALU.add).then_inc(added, 16)
                weights(0, 0)
                weights(1, 1)
                run(eng, body)
                eng.wait_ge(added, 16 * R * FTILES)

            @block.tensor
            def _(eng):
                def turn_in(k):
                    eng.wait_ge(hi_n, k + 1)
                    eng.wait_ge(lo_n, k + 1)
                    wait(eng, xt_n, k)
                    for r in range(R):
                        last = eng.transpose(ps_x[:, r * P:(r + 1) * P], hl[:, r, :], s.ident[:, :])
                    last.then_inc(x_n, 1)

                def turn_out(k):
                    eng.wait_ge(yc_n, k + 1)
                    wait(eng, oc_n, k)
                    for r in range(R):
                        last = eng.transpose(ps_o[:, r * P:(r + 1) * P], y[:, r * P:(r + 1) * P], s.ident[:, :])
                    last.then_inc(o_n, 1)

                def body(k, buf, quarter):
                    par = buf % 2
                    eng.wait_ge(xt_n, k + 1)
                    eng.wait_ge(w13_n, 4 * k + 4)
                    for c in range(HCHUNKS):
                        for m, (ps, done, free) in enumerate(((ps_1, h1_n, act_n), (ps_3, h3_n, h_n))):
                            wait(eng, free, HCHUNKS * k + c - 1)
                            for j in range(2):
                                last = eng.matmul(ps[c % 2][0:HCHUNK, :], w13[par][j][:, m, c * HCHUNK:(c + 1) * HCHUNK], xt[par][:, :],
                                                  start=(j == 0), stop=(j == 1))
                            last.then_inc(done, 1)
                    if sym(k) or k > 0:
                        turn_out(k - 1)
                    if sym(k) or k < LAST:
                        turn_in(k + 1)
                    eng.wait_ge(w2_n, k + 1)
                    wait(eng, yc_n, k)
                    for c in range(HCHUNKS):
                        eng.wait_ge(h_n, HCHUNKS * k + c + 1)
                        last = eng.matmul(ps_y[:, :], w2[par][:, c, :], h[:, c, :], start=(c == 0), stop=(c == HCHUNKS - 1))
                    last.then_inc(y_n, 1)
                turn_in(0)
                run(eng, body)
                turn_out(LAST)

            @block.scalar
            def _(eng):
                def upper(k, buf, quarter):
                    eng.wait_ge(x_in[buf], 16 * (quarter + 1))
                    wait(eng, x_n, k)
                    eng.activation(hl[:, :, 0:C].bitcast(F32R), x[buf][:, :, 0:C], ACT.Copy).then_inc(hi_n, 1)

                def across(k, par):
                    eng.wait_ge(x_n, k + 1)
                    eng.activation(xt[par][:, :], ps_x[:, :], ACT.Copy).then_inc(xt_n, 1)

                def body(k, buf, quarter):
                    more = sym(k) or k < LAST
                    for c in range(HCHUNKS):
                        eng.wait_ge(h1_n, HCHUNKS * k + c + 1)
                        wait(eng, h_n, HCHUNKS * k + c - 1)
                        eng.activation(act[c % 2][:, :], ps_1[c % 2][0:HCHUNK, :], ACT.Silu).then_inc(act_n, 1)
                        if c == 1 and more:
                            upper(k + 1, (buf + 1) % 4, quarter + (buf + 1) // 4)
                    if more:
                        across(k + 1, (buf + 1) % 2)
                    eng.wait_ge(y_n, k + 1)
                    wait(eng, o_n, k)
                    eng.activation(y[:, :], ps_y[:, :], ACT.Copy).then_inc(yc_n, 1)
                upper(0, 0, 0)
                across(0, 0)
                run(eng, body)

            @block.vector
            def _(eng):
                def weights(k, par, parts):
                    for j, m in parts:
                        eng.tensor_scalar(w13[par][j][:, m, :], s.w13[j][:, bass.ds(e_of[0], 1), m, :].rearrange("p o n -> p (o n)").bitcast(F32),
                                          1.0, None, ALU.mult).then_inc(w13_n, 1)

                def lower(k, buf):
                    eng.wait_ge(hi_n, k + 1)
                    wait(eng, x_n, k)
                    eng.tensor_tensor(hl[:, :, C:2 * C], x[buf][:, :, 0:C], hl[:, :, 0:C], ALU.subtract).then_inc(lo_n, 1)

                def result(k, buf):
                    eng.wait_ge(o_n, k + 1)
                    wait(eng, added, 16 * R * (k - 1))
                    eng.tensor_tensor(out[buf % 2][:, :, :], ps_o[:, :].rearrange("p (r c) -> p r c", c=P)[:, :, 0:C],
                                      x[buf][:, :, C:C + 1].to_broadcast([P, R, C]), ALU.mult).then_inc(oc_n, 1)

                PARTS = [(j, m) for j in range(2) for m in range(2)]
                e_of = [eng.value_load(s.owner[0:1, 0:1], min_val=0, max_val=EXPERTS - 1)]
                weights(0, 0, PARTS)
                eng.wait_ge(x_in[0], 16)
                lower(0, 0)

                def body(k, buf, quarter):
                    more = sym(k) or k < LAST
                    if more:
                        e_of[0] = eng.value_load(s.owner[0:1, bass.ds(k + 1, 1)], min_val=0, max_val=EXPERTS - 1)
                    for c in range(HCHUNKS):
                        eng.wait_ge(act_n, HCHUNKS * k + c + 1)
                        eng.wait_ge(h3_n, HCHUNKS * k + c + 1)
                        eng.tensor_tensor(h[:, c, :], act[c % 2][:, :], ps_3[c % 2][0:HCHUNK, :], ALU.mult).then_inc(h_n, 1)
                        if more and c < 4:
                            weights(k + 1, (buf + 1) % 2, PARTS[c:c + 1])
                        if more and c == 4:
                            lower(k + 1, (buf + 1) % 4)
                    if sym(k) or k > 0:
                        result(k - 1, (buf - 1) % 4)
                run(eng, body)
                result(LAST, LAST % 4)


def finish(nc, s, out, sem):
    copied = sem("output_copied")
    with nc.Block() as block:
        @block.sync
        def _(eng):
            eng.dma_start(out.rearrange("b r c e -> (b r c) e"), s.summed[0:TOK, :]).then_inc(copied, 16)
            eng.wait_ge(copied, 16)


def hybrid_block(nc, a, out):
    with ExitStack() as ctx:
        def sem(name):
            return ctx.enter_context(nc.semaphore(name))

        s = allocate(nc, ctx)
        constants(nc, s, sem)
        with ExitStack() as upto_layer2:
            def sb(name, shape, dt=F32):
                return upto_layer2.enter_context(nc.sbuf_tensor(name, shape, dt))

            s.conv = sb("conv_out", [P, TOK])
            with ExitStack() as layer1:
                s.xhl = layer1.enter_context(nc.sbuf_tensor("gn_hl", [P, TILES, P], F32))
                conv_weights(nc, layer1, s, a, sem)
                group_norm(nc, s, a, sem)
                conv_attention(nc, s, sem)
            s.xt = sb("norm_T", [P, TOK], F32R)
            s.proj = [sb(f"proj{k}", [P, 4, HC], F32R) for k in range(2)]
            s.wo, s.bo, s.bg = sb("wo_sb", [P, 2, P]), sb("bo_sb", [P, 1]), sb("bg_sb", [P, 2])
            s.gamma, s.beta = sb("gamma_sb", [P, C]), sb("beta_sb", [P, C])
            s.att_w = sb("att_w", [P, HEADS, P])
            axial_weights(nc, s, a, sem)
            axial_scores(nc, s, sem)
            axial_values(nc, s, sem)

        def sb(name, shape, dt=F32):
            return ctx.enter_context(nc.sbuf_tensor(name, shape, dt))

        s.slot = [sb(f"slot{k}", [P, TILES], mybir.dt.uint32) for k in range(2)]
        s.owner = sb("owner", [P, FTILES], mybir.dt.int32)
        s.router = sb("router", [P, EXPERTS])
        s.w13 = [sb(f"w13_{k}", [P, EXPERTS, 2, HPAD], F32R) for k in range(2)]
        s.w2 = sb("w2_sb", [HCHUNK, EXPERTS, HCHUNKS * C])
        s.slot_x = nc.dram_tensor("slot_x", [SLOTS, ROW], F32, kind="Internal").ap()
        s.summed = nc.dram_tensor("summed", [TOK + SLOT, C], F32, kind="Internal").ap()
        with ExitStack() as dispatch:
            s.rows = [dispatch.enter_context(nc.sbuf_tensor(f"rows{k}", [P, TILES, ROW], F32)) for k in range(2)]
            route(nc, s, a, sem)
            expert_weights(nc, s, a, sem)
        experts(nc, s, sem)
        finish(nc, s, out, sem)


_INS = ['x', 'L0_conv_w_q', 'L0_conv_w_k', 'L0_conv_w_v', 'L0_conv_w_local', 'L0_conv_b_local', 'L0_conv_w_out',
        'L0_conv_b_out', 'L1_attn_gamma', 'L1_attn_beta', 'L1_attn_Wq', 'L1_attn_Wk', 'L1_attn_Wv', 'L1_attn_Wg',
        'L1_attn_bg', 'L1_attn_Wo', 'L1_attn_bo', 'L1_ffn_router_w', 'L1_ffn_w1', 'L1_ffn_w2', 'L1_ffn_w3']
_OUTS = [((BATCH, SIDE, SIDE, C), 'float32')]


def kernel(**inputs):
    import numpy as _np
    import concourse.bacc as _bacc
    from concourse import mybir as _mybir
    from concourse.bass_utils import run_bass_kernel_spmd as _run

    nc = _bacc.Bacc("TRN2", target_bir_lowering=False, num_devices=1)
    arrays, args = {}, {}
    for name in _INS:
        arr = _np.ascontiguousarray(inputs[name])
        arrays[f"in_{name}_dram"] = arr
        args[name] = nc.dram_tensor(f"in_{name}_dram", arr.shape, _mybir.dt.from_np(arr.dtype), kind="ExternalInput").ap()
    shape, dtype = _OUTS[0]
    out = nc.dram_tensor("out_0_dram", shape, _mybir.dt.from_np(_np.dtype(dtype)), kind="ExternalOutput").ap()
    hybrid_block(nc, args, out)
    r = _run(nc, [arrays], core_ids=[0])
    return r.results[0]["out_0_dram"]
```

```python
from contextlib import ExitStack

import concourse.bass as bass
from concourse import mybir

F32 = mybir.dt.float32
F32R = mybir.dt.float32r
ALU = mybir.AluOpType
ACT = mybir.ActivationFunctionType
AX = mybir.AxisListType

P = 128
BATCH, SIDE, C = 32, 16, 64
L = SIDE * SIDE
TOK = BATCH * L
TILES = TOK // P
HEADS, D = 8, 32
HC = HEADS * D
WIN = 8
WTOK = WIN * WIN
TAPS = 9
PADDED = SIDE + 2


class Steps:

    def __init__(self, engine, sem, per=0):
        self.engine, self.sem, self.per = engine, sem, per
        self.base, self.n = 0, 0

    def round(self, i):
        assert self.per == 0 or self.n in (0, self.per), (self.n, self.per)
        self.base, self.n = i * self.per, 0

    def did(self, ins):
        ins.then_inc(self.sem, 1)
        self.n += 1

    def settle(self):
        self.engine.wait_ge(self.sem, self.base + self.n)

    def then(self, ins):
        self.did(ins)
        self.settle()


class Shared:
    pass


def allocate(nc, ctx):
    def sb(name, shape, dt=F32):
        return ctx.enter_context(nc.sbuf_tensor(name, shape, dt))

    s = Shared()
    s.ident = sb("ident", [P, P])
    s.x1 = sb("residual", [P, TILES, C])
    s.mean_of_group = sb("mean_of_group", [P, P])
    s.fold = sb("fold", [P, C])
    return s


def constants(nc, s, sem):
    done, filled = sem("constants_done"), sem("constants_filled")
    with nc.Block() as block:
        @block.gpsimd
        def _(eng):
            eng.memset(s.ident[:, :], 0.0).then_inc(filled, 1)
            eng.wait_ge(filled, 1)
            eng.affine_select(out=s.ident[:, :], in_=s.ident[:, :], compare_op=ALU.not_equal, fill=1.0,
                              base=0, pattern=[[-1, P]], channel_multiplier=1).then_inc(done, 1)
            eng.memset(s.mean_of_group[:, :], 1.0 / (2 * L)).then_inc(done, 1)
            eng.memset(s.fold[:, :], 0.0).then_inc(filled, 1)
            for half in range(2):
                eng.wait_ge(filled, 2 + half)
                eng.affine_select(out=s.fold[:, :], in_=s.fold[:, :], compare_op=ALU.not_equal, fill=1.0,
                                  base=-half * C, pattern=[[-1, C]], channel_multiplier=1).then_inc(filled, 1)
            eng.wait_ge(filled, 4)
            eng.wait_ge(done, 2)


def conv_weights(nc, ctx, s, a, sem):
    def sb(name, shape, dt=F32):
        return ctx.enter_context(nc.sbuf_tensor(name, shape, dt))

    s.score_w = [sb(f"score_w{k}", [P, HEADS, P], F32R) for k in range(2)]
    s.value_w = [sb(f"value_w{k}", [P, HEADS * C], F32R) for k in range(2)]
    s.tap_w = sb("tap_w", [P, TAPS, 2, C], F32R)
    s.conv_bias = sb("conv_bias", [P, 1])
    with ExitStack() as own:
        def tmp(name, shape, dt=F32):
            return own.enter_context(nc.sbuf_tensor(name, shape, dt))

        wq, wk, wv = (tmp(f"w{n}_in", [C, HC]) for n in "qkv")
        wout = tmp("wout_in", [P, 2, C])
        wlocal = tmp("wlocal_in", [P, 2, TAPS, HC])
        b_local = tmp("b_local_in", [P, 2])
        b_out = tmp("b_out_in", [C, 1])
        wT = tmp("wT", [P, 3, 2, 2, C])
        folded = tmp("folded", [P, HEADS, P])
        folded_v = tmp("folded_v", [P, HEADS, C])
        tapT = tmp("tapT", [P, TAPS, 2, P])
        tap = tmp("tap", [P, TAPS, C])
        psT = own.enter_context(nc.psum_tensor("psT_w", [P, 6, C], F32))
        psA = [own.enter_context(nc.psum_tensor(f"psA_w{r}", [P, 512], F32)) for r in range(4)]
        psB = own.enter_context(nc.psum_tensor("psB_w", [P, 2, 512], F32))
        loads, local_in, w_turned, wT_ready = sem("conv_w_loads"), sem("conv_local_loads"), sem("conv_w_turned"), sem("conv_wT_ready")
        heads_done, taps_done, tap_free = sem("head_products_done"), sem("taps_done"), sem("tap_free")
        weff_done, weff_copied = sem("weff_done"), sem("weff_copied")
        act_did, dve_did = sem("conv_w_act"), sem("conv_w_dve")
        n_loads = 7

        with nc.Block() as block:
            @block.sync
            def _(eng):
                for dst, src in ((wq, a["L0_conv_w_q"]), (wk, a["L0_conv_w_k"]), (wv, a["L0_conv_w_v"])):
                    eng.dma_start(dst[:, :], src.rearrange("a b c n -> (a b c) n")).then_inc(loads, 16)
                eng.dma_start(wout[:, :, :], a["L0_conv_w_out"].rearrange("a b (k p) n -> p (a b k) n", p=P)).then_inc(loads, 16)
                for k in range(2):
                    eng.dma_start(b_local[:, k:k + 1], a["L0_conv_b_local"][k * P:(k + 1) * P].rearrange("(p o) -> p o", o=1)).then_inc(loads, 16)
                eng.dma_start(b_out[:, :], a["L0_conv_b_out"].rearrange("(p o) -> p o", o=1)).then_inc(loads, 16)
                local = a["L0_conv_w_local"].rearrange("u v (k p) n -> k p (u v) n", p=P)
                for k in range(2):
                    eng.dma_start(wlocal[:, k], local[k]).then_inc(local_in, 16)
                src = a["x"].rearrange("b (nx r) (ny c) e -> ny r c (b nx) e", nx=2, ny=2)
                for ny in range(2):
                    for r in range(WIN):
                        p0 = ny * WTOK + r * WIN
                        eng.dma_start(s.gn_x[p0:p0 + WIN, :, :], src[ny, r]).then_inc(s.gn_x_in, 16)

            @block.tensor
            def _(eng):
                eng.wait_ge(loads, 16 * n_loads)
                for i, w in enumerate((wq, wk, wv)):
                    for k in range(2):
                        last = eng.transpose(psT[:, 2 * i + k, :], w[:, k * P:(k + 1) * P], s.ident[0:C, 0:C])
                last.then_inc(w_turned, 1)
                eng.wait_ge(wT_ready, 2)
                for h in range(HEADS):
                    k, r = divmod(h, 4)
                    rows = slice(D * r, D * r + D)
                    q, kk, v = (wT[rows, i, k].rearrange("p a c -> p (a c)") for i in range(3))
                    eng.matmul(psA[r][:, k * P:(k + 1) * P], kk, q, start=True, stop=True)
                    last = eng.matmul(psA[r][:, 2 * P + k * C:2 * P + (k + 1) * C], v, wout[rows, k, :],
                                      start=True, stop=True)
                last.then_inc(heads_done, 1)
                eng.wait_ge(local_in, 16 * 2)
                for t in range(TAPS):
                    if t >= 2:
                        eng.wait_ge(tap_free, t - 1)
                    for blk in range(2):
                        for k in range(2):
                            last = eng.matmul(psB[:, t % 2, blk * P:(blk + 1) * P], wlocal[:, k, t, blk * P:(blk + 1) * P],
                                              wT[:, 2, k].rearrange("p a c -> p (a c)"),
                                              start=(k == 0), stop=(k == 1))
                    last.then_inc(taps_done, 1)
                eng.wait_ge(tap_free, TAPS)
                for t in range(TAPS):
                    for blk in range(2):
                        last = eng.matmul(psB[:, t // 8, (t % 8) * C:(t % 8 + 1) * C], tapT[:, t, blk, :], wout[:, blk, :],
                                          start=(blk == 0), stop=(blk == 1))
                last.then_inc(weff_done, 1)
                for k in range(2):
                    last = eng.matmul(psB[0:C, 1, 256:257], wout[:, k, :], b_local[:, k:k + 1], start=(k == 0), stop=(k == 1))
                last.then_inc(weff_done, 1)

            @block.scalar
            def _(eng):
                eng.wait_ge(w_turned, 1)
                turned = psT[:, :, :].rearrange("p (i k) c -> p i k c", k=2)
                for twice in range(2):
                    eng.activation(wT[:, :, :, twice, :], turned, ACT.Copy).then_inc(wT_ready, 1)
                mine = Steps(eng, act_did)
                eng.wait_ge(heads_done, 1)
                for h in range(HEADS):
                    k, r = divmod(h, 4)
                    mine.did(eng.activation(folded[:, h, :], psA[r][:, k * P:(k + 1) * P], ACT.Copy, scale=D ** -0.5))
                    mine.did(eng.activation(folded_v[:, h, :], psA[r][:, 2 * P + k * C:2 * P + (k + 1) * C], ACT.Copy))
                mine.settle()
                mine.did(eng.activation(s.score_w[0][:, :, :], folded[:, :, :], ACT.Copy))
                mine.did(eng.activation(s.value_w[0][:, :], folded_v[:, :, :].rearrange("p h c -> p (h c)"), ACT.Copy))
                eng.wait_ge(weff_copied, 2)
                mine.did(eng.activation(s.tap_w[:, :, 0, :], tap[:, :, :], ACT.Copy))

            @block.vector
            def _(eng):
                for t in range(TAPS):
                    eng.wait_ge(taps_done, t + 1)
                    eng.tensor_copy(tapT[:, t], psB[:, t % 2, 0:2 * P].rearrange("p (b e) -> p b e", b=2)).then_inc(tap_free, 1)
                eng.memset(s.conv_bias[:, :], 0.0).then_inc(dve_did, 1)
                eng.wait_ge(act_did, 2 * HEADS + 2)
                eng.tensor_tensor(s.score_w[1][:, :, :], folded[:, :, :], s.score_w[0][:, :, :].bitcast(F32), ALU.subtract).then_inc(dve_did, 1)
                eng.tensor_tensor(s.value_w[1][:, :], folded_v[:, :, :].rearrange("p h c -> p (h c)"), s.value_w[0][:, :].bitcast(F32), ALU.subtract).then_inc(dve_did, 1)
                eng.wait_ge(weff_done, 2)
                eng.wait_ge(dve_did, 3)
                eng.tensor_tensor(s.conv_bias[0:C, :], psB[0:C, 1, 256:257], b_out[:, :], ALU.add).then_inc(dve_did, 1)
                eng.tensor_copy(tap[:, 0:8, :], psB[:, 0, :].rearrange("p (t c) -> p t c", c=C)).then_inc(weff_copied, 1)
                eng.tensor_copy(tap[:, 8, :], psB[:, 1, 0:C]).then_inc(weff_copied, 1)
                eng.wait_ge(act_did, 2 * HEADS + 3)
                eng.tensor_tensor(s.tap_w[:, :, 1, :], tap[:, :, :], s.tap_w[:, :, 0, :].bitcast(F32), ALU.subtract).then_inc(dve_did, 1)


def group_norm(nc, s, sem):
    with ExitStack() as own:
        def tmp(name, shape, dt=F32):
            return own.enter_context(nc.sbuf_tensor(name, shape, dt))

        x, x_in = s.gn_x, s.gn_x_in
        sq = tmp("gn_sq", [P, TILES, C])
        groups = C // 2
        mean = tmp("gn_mean", [P, BATCH, groups])
        var = tmp("gn_var", [P, BATCH, groups])
        rstd = tmp("gn_rstd", [P, BATCH, groups])
        fix = tmp("gn_fix", [P, BATCH, groups])
        PARTS = 4
        per = BATCH // PARTS
        ps = own.enter_context(nc.psum_tensor("gn_ps", [P, 2, PARTS, 512], F32))
        sums, squares, roots = sem("gn_sums"), sem("gn_squares"), sem("gn_roots")
        centered, var_ready, normed, hi_ready, dve_did = (sem("gn_centered"), sem("gn_var_ready"), sem("gn_normed"),
                                                          sem("gn_hi_ready"), sem("gn_dve"))
        lo_ready = sem("gn_lo_ready")

        def half(t, h):
            return t[:, h::2, :].rearrange("p b (g e) -> p b g e", e=2)

        def spread(t):
            return t[:, :, :].unsqueeze(3).to_broadcast([P, BATCH, groups, 2])

        with nc.Block() as block:
            @block.tensor
            def _(eng):
                eng.wait_ge(x_in, 16 * 2 * WIN)
                for k, t in enumerate((x, sq)):
                    for q in range(PARTS):
                        if k == 1:
                            eng.wait_ge(squares, 1)
                        for h in range(2):
                            first = 2 * q * per + h
                            last = eng.matmul(ps[:, k, q, :], s.mean_of_group[:, :], t[:, first:2 * (q + 1) * per:2, :],
                                              start=(h == 0), stop=(h == 1))
                        last.then_inc(sums, 1)

            @block.scalar
            def _(eng):
                eng.wait_ge(centered, 2)
                eng.activation(sq[:, :, :], x[:, :, :], ACT.Square).then_inc(squares, 1)
                eng.wait_ge(var_ready, 1)
                eng.activation(fix[:, :, :], var[:, :, :], ACT.Sqrt).then_inc(roots, 1)
                eng.wait_ge(normed, 2)
                eng.activation(s.xhl[:, :, 0:C].bitcast(F32R), sq[:, :, :], ACT.Copy).then_inc(hi_ready, 1)

            @block.vector
            def _(eng):
                mine = Steps(eng, dve_did)
                for q in range(PARTS):
                    eng.wait_ge(sums, q + 1)
                    mine.did(eng.tensor_reduce(mean[:, q * per:(q + 1) * per, :],
                                               ps[:, 0, q, :].rearrange("p (b g e) -> p b g e", g=groups, e=2), AX.X, ALU.add))
                eng.wait_ge(sums, PARTS)
                mine.settle()
                for h in range(2):
                    eng.tensor_tensor(half(x, h), half(x, h), spread(mean), ALU.subtract).then_inc(centered, 1)
                for q in range(PARTS):
                    eng.wait_ge(sums, PARTS + q + 1)
                    mine.did(eng.tensor_reduce(var[:, q * per:(q + 1) * per, :],
                                               ps[:, 1, q, :].rearrange("p (b g e) -> p b g e", g=groups, e=2), AX.X, ALU.add))
                mine.settle()
                eng.tensor_scalar(var[:, :, :], var[:, :, :], 1e-5, None, ALU.add).then_inc(var_ready, 1)
                eng.wait_ge(roots, 1)
                mine.then(eng.reciprocal(rstd[:, :, :], fix[:, :, :]))
                newton(eng, mine, rstd[:, :, :], var[:, :, :], fix[:, :, :])
                for h in range(2):
                    eng.tensor_tensor(half(sq, h), half(x, h), spread(rstd), ALU.mult).then_inc(normed, 1)
                eng.wait_ge(hi_ready, 1)
                eng.wait_ge(normed, 2)
                eng.tensor_tensor(s.xhl[:, :, C:2 * C], sq[:, :, :], s.xhl[:, :, 0:C], ALU.subtract).then_inc(lo_ready, 1)


def newton(eng, mine, y, v, t):
    mine.then(eng.tensor_tensor(t, y, y, ALU.mult))
    mine.then(eng.tensor_tensor(t, t, v, ALU.mult))
    mine.then(eng.tensor_scalar(t, t, -0.5, 1.5, ALU.mult, ALU.add))
    mine.then(eng.tensor_tensor(y, y, t, ALU.mult))


def conv_attention(nc, s, a, sem):
    with ExitStack() as own:
        def tmp(name, shape, dt=F32):
            return own.enter_context(nc.sbuf_tensor(name, shape, dt))

        W2 = 2
        staged = [tmp(f"staged{i}", [P, 2, P]) for i in range(W2)]
        xw = [tmp(f"xw{i}", [P, 4, 2, WTOK], F32R) for i in range(W2)]
        xp = [tmp(f"xp{i}", [P, PADDED, PADDED], F32R) for i in range(W2)]
        y = tmp("score_side", [P, HEADS, L])
        v = [tmp(f"values{i}", [P, 2, 4, 2, C]) for i in range(W2)]
        shifted = [tmp(f"shifted{i}", [P, HEADS, WTOK]) for i in range(W2)]
        probs = [tmp(f"probs{i}", [P, HEADS, WTOK]) for i in range(W2)]
        probsT = [tmp(f"probsT{i}", [P, 4, P]) for i in range(W2)]
        mx = [tmp(f"win_max{i}", [P, HEADS]) for i in range(W2)]
        den = [tmp(f"win_den{i}", [P, HEADS]) for i in range(W2)]
        rden = [tmp(f"win_rden{i}", [P, HEADS]) for i in range(W2)]

        def bank(name):
            return own.enter_context(nc.psum_tensor(name, [P, 512], F32))

        ps_x, ps_o = bank("ps_x"), bank("ps_o")
        ps_a = [bank(f"ps_a{i}") for i in range(4)]
        ps_s = [bank("ps_s0"), bank("ps_s1")]

        staged_n, turned_n, xw_n, xp_n = sem("staged_n"), sem("turned_n"), sem("xw_n"), sem("xp_n")
        conv_n, convc_n = sem("conv_done_n"), sem("conv_copied_n")
        y_n, ya_n, yd_n = sem("y_done_n"), sem("y_copied_act_n"), sem("y_copied_dve_n")
        v_n, va_n, vd_n = sem("v_done_n"), sem("v_copied_act_n"), sem("v_copied_dve_n")
        s_n, sub_n, exp_n, rden_n, prob_n = sem("scores_n"), sem("shifted_n"), sem("exp_n"), sem("rden_n"), sem("prob_n")
        pt_n, ptc_n, o_n, added_n = sem("probs_turned_n"), sem("probsT_n"), sem("out_n"), sem("added_n")
        max_n, den_n, zero_n = sem("win_max_n"), sem("win_den_n"), sem("border_zero")

        def images(eng, body):
            body(0, 0)
            body(1, 1)
            with eng.Fori(1, BATCH // 2 - 1) as i:
                for par in range(2):
                    body(2 * i + par, par)
            body(BATCH - 2, 0)
            body(BATCH - 1, 1)

        def there(n):
            return sym(n) or n < BATCH

        with nc.Block() as block:
            @block.sync
            def _(eng):
                x = a["x"].rearrange("b (h4 r) c e -> b (h4 r c) e", r=1).rearrange("b (g q) e -> q b g e", q=4)
                for q in range(4):
                    eng.dma_start(s.x1[q * BATCH:(q + 1) * BATCH, :, :], x[q]).then_inc(s.x1_in, 16)

            @block.gpsimd
            def _(eng):
                for i in range(W2):
                    eng.memset(xp[i][:, :, :].bitcast(F32), 0.0).then_inc(zero_n, 1)

                def stage(n, par):
                    wait(eng, turned_n, n - 1)
                    eng.tensor_copy(staged[par][:, :, :], s.xhl[:, bass.ds(2 * n, 2), :]).then_inc(staged_n, 1)

                def body(n, par):
                    if there(n + 2):
                        stage(n + 2, par)
                    for t in range(2):
                        eng.wait_ge(rden_n, 2 * n + t + 1)
                        wait(eng, pt_n, 2 * n + t - 1)
                        eng.tensor_tensor(probs[t][:, :, :], shifted[t][:, :, :],
                                          rden[t][:, :].unsqueeze(2).to_broadcast([P, HEADS, WTOK]), ALU.mult).then_inc(prob_n, 1)

                stage(0, 0)
                stage(1, 1)
                images(eng, body)

            @block.tensor
            def _(eng):
                def turn(n, par):
                    eng.wait_ge(staged_n, n + 1)
                    wait(eng, convc_n, n)
                    for t in range(2):
                        last = eng.transpose(ps_x[:, t * P:(t + 1) * P], staged[par][:, t, :], s.ident[:, :])
                    last.then_inc(turned_n, 1)

                def right_side(n, par):
                    eng.wait_ge(xw_n, n + 1)
                    for g in range(4):
                        wait(eng, va_n, 4 * n - 3 + g)
                        wait(eng, vd_n, 4 * n - 3 + g)
                        for e in range(2):
                            for k in range(2):
                                last = eng.matmul(ps_a[g][:, e * L:(e + 1) * L], s.score_w[k][:, 2 * g + e, :],
                                                  xw[par][:, :, 0, :], start=(k == 0), stop=(k == 1))
                        last.then_inc(y_n, 1)

                def values(n, par, windows):
                    for w in windows:
                        eng.wait_ge((ya_n, yd_n)[w % 2], 2 * n + w // 2 + 1)
                        both = xw[par][:, w].rearrange("p a j -> p (a j)")
                        for k in range(2):
                            last = eng.matmul(ps_a[w][:, :], both, s.value_w[k][:, :], start=(k == 0), stop=(k == 1))
                        last.then_inc(v_n, 1)

                def convolution(n, par):
                    eng.wait_ge(xp_n, n + 1)
                    for tap in range(TAPS):
                        u, w = divmod(tap, 3)
                        last = eng.matmul(ps_x[:, 0:L].rearrange("p (r c) -> p r c", r=SIDE),
                                          s.tap_w[:, tap].rearrange("p k c -> p (k c)"),
                                          xp[par][:, u:u + SIDE, w:w + SIDE], start=(tap == 0), stop=(tap == TAPS - 1))
                    last.then_inc(conv_n, 1)

                def scores(n, par):
                    eng.wait_ge(ya_n, 2 * n + 2)
                    eng.wait_ge(yd_n, 2 * n + 2)
                    for t in range(2):
                        wait(eng, ptc_n, 2 * n + t - 1)
                        for w in range(2):
                            cols = slice((2 * t + w) * WTOK, (2 * t + w + 1) * WTOK)
                            last = eng.matmul(ps_s[t][w * WTOK:(w + 1) * WTOK, :], xw[par][:, 2 * t + w, 0, :].bitcast(F32),
                                              y[:, :, cols], start=True, stop=True)
                        last.then_inc(s_n, 1)

                def turn_probs(n, t):
                    eng.wait_ge(prob_n, 2 * n + t + 1)
                    for g in range(4):
                        last = eng.transpose(ps_s[t][:, g * P:(g + 1) * P],
                                             probs[t][:, 2 * g:2 * g + 2, :].rearrange("p h j -> p (h j)"), s.ident[:, :])
                    last.then_inc(pt_n, 1)

                def output(n, par, t):
                    eng.wait_ge(ptc_n, 2 * n + t + 1)
                    if t == 0:
                        eng.wait_ge(va_n, 4 * n + 4)
                        eng.wait_ge(vd_n, 4 * n + 4)
                        wait(eng, added_n, n)
                    for g in range(4):
                        last = eng.matmul(ps_o[:, t * P:(t + 1) * P], v[par][:, t, g].rearrange("p w c -> p (w c)"),
                                          probsT[t][:, g, :], start=(g == 0), stop=(g == 3))
                    last.then_inc(o_n, 1)

                def body(n, par):
                    scores(n, par)
                    if there(n + 1):
                        right_side(n + 1, 1 - par)
                        values(n + 1, 1 - par, range(3))
                        convolution(n + 1, 1 - par)
                        values(n + 1, 1 - par, [3])
                    turn_probs(n, 0)
                    if there(n + 2):
                        turn(n + 2, par)
                    turn_probs(n, 1)
                    output(n, par, 0)
                    output(n, par, 1)

                eng.wait_ge(zero_n, W2)
                turn(0, 0)
                right_side(0, 0)
                values(0, 0, range(3))
                convolution(0, 0)
                values(0, 0, [3])
                turn(1, 1)
                images(eng, body)

            @block.scalar
            def _(eng):
                def windows(n, par):
                    eng.wait_ge(turned_n, n + 1)
                    eng.activation(xw[par][:, :, :, :], ps_x[:, 0:L].rearrange("p (w j) -> p w j", w=4).unsqueeze(2).to_broadcast([P, 4, 2, WTOK]),
                                   ACT.Copy).then_inc(xw_n, 1)

                def right_side(n):
                    wait(eng, s_n, 2 * n)
                    for g in (0, 2):
                        eng.wait_ge(y_n, 4 * n + g + 1)
                        eng.activation(y[:, 2 * g:2 * g + 2, :], ps_a[g][:, :].rearrange("p (e l) -> p e l", e=2),
                                       ACT.Copy).then_inc(ya_n, 1)

                def values(n, par, windows):
                    if 0 in windows:
                        wait(eng, o_n, 2 * (n - 1))
                    for w in windows:
                        eng.wait_ge(v_n, 4 * n + w + 1)
                        eng.activation(v[par][0:WTOK, w // 2, :, w % 2, :],
                                       ps_a[w][0:WTOK, :].rearrange("p (g e c) -> p g e c", e=2, c=C)[:, :, 0, :],
                                       ACT.Copy).then_inc(va_n, 1)

                def convolution(n):
                    eng.wait_ge(conv_n, n + 1)
                    eng.activation(s.conv[:, bass.ds(n * L, L)], ps_x[:, 0:L], ACT.Identity, bias=s.conv_bias[:, 0:1]).then_inc(convc_n, 1)

                def turned_probs(n, t):
                    eng.wait_ge(pt_n, 2 * n + t + 1)
                    wait(eng, o_n, 2 * n + t - 1)
                    eng.activation(probsT[t][:, :, :], ps_s[t][:, :].rearrange("p (g i) -> p g i", g=4), ACT.Copy).then_inc(ptc_n, 1)

                def exp(n, t):
                    eng.wait_ge(sub_n, 2 * n + t + 1)
                    eng.activation(shifted[t][:, :, :], shifted[t][:, :, :], ACT.Exp).then_inc(exp_n, 1)

                def body(n, par):
                    exp(n, 0)
                    if there(n + 1):
                        right_side(n + 1)
                    exp(n, 1)
                    if there(n + 1):
                        values(n + 1, 1 - par, range(3))
                        convolution(n + 1)
                        values(n + 1, 1 - par, [3])
                    turned_probs(n, 0)
                    if there(n + 2):
                        windows(n + 2, par)
                    turned_probs(n, 1)

                windows(0, 0)
                right_side(0)
                values(0, 0, range(3))
                convolution(0)
                values(0, 0, [3])
                windows(1, 1)
                images(eng, body)

            @block.vector
            def _(eng):
                def padded(n, par):
                    eng.wait_ge(xw_n, n + 1)
                    wait(eng, conv_n, n - 1)
                    for nx in range(2):
                        for ny in range(2):
                            w = 2 * nx + ny
                            last = eng.tensor_copy(xp[par][:, 1 + nx * WIN:1 + (nx + 1) * WIN, 1 + ny * WIN:1 + (ny + 1) * WIN],
                                                   xw[par][:, w, 0, :].bitcast(F32).rearrange("p (r c) -> p r c", r=WIN))
                    last.then_inc(xp_n, 1)

                def right_side(n, g):
                    if g == 1:
                        wait(eng, s_n, 2 * n)
                    eng.wait_ge(y_n, 4 * n + g + 1)
                    eng.tensor_copy(y[:, 2 * g:2 * g + 2, :], ps_a[g][:, :].rearrange("p (e l) -> p e l", e=2)).then_inc(yd_n, 1)

                def values(n, par, w):
                    if w == 0:
                        wait(eng, o_n, 2 * (n - 1))
                    eng.wait_ge(v_n, 4 * n + w + 1)
                    eng.tensor_copy(v[par][WTOK:P, w // 2, :, w % 2, :],
                                    ps_a[w][WTOK:P, :].rearrange("p (g e c) -> p g e c", e=2, c=C)[:, :, 1, :]).then_inc(vd_n, 1)

                def scores(t):
                    return ps_s[t][:, :].rearrange("p (h j) -> p h j", h=HEADS)

                def maximum(n, t):
                    eng.wait_ge(s_n, 2 * n + t + 1)
                    eng.tensor_reduce(mx[t][:, :], scores(t), AX.X, ALU.max).then_inc(max_n, 1)

                def shift(n, t):
                    k = 2 * n + t
                    eng.wait_ge(max_n, k + 1)
                    wait(eng, prob_n, k - 1)
                    eng.tensor_tensor(shifted[t][:, :, :], scores(t),
                                      mx[t][:, :].unsqueeze(2).to_broadcast([P, HEADS, WTOK]), ALU.subtract).then_inc(sub_n, 1)

                def sums(n, t):
                    eng.wait_ge(exp_n, 2 * n + t + 1)
                    eng.tensor_reduce(den[t][:, :], shifted[t][:, :, :], AX.X, ALU.add).then_inc(den_n, 1)

                def inverse(n, t):
                    eng.wait_ge(den_n, 2 * n + t + 1)
                    eng.reciprocal(rden[t][:, :], den[t][:, :]).then_inc(rden_n, 1)

                def add(n):
                    eng.wait_ge(convc_n, n + 1)
                    eng.wait_ge(o_n, 2 * n + 2)
                    for t in range(2):
                        for w in range(2):
                            rows = slice(w * C, (w + 1) * C)
                            own_part = s.conv[rows, bass.ds(n * L + t * WIN * SIDE, WIN * SIDE)].rearrange(
                                "p (r c) -> p r c", c=SIDE)[:, :, w * WIN:(w + 1) * WIN]
                            last = eng.tensor_tensor(own_part, own_part,
                                                     ps_o[rows, t * P + w * WTOK:t * P + (w + 1) * WTOK].rearrange("p (r c) -> p r c", r=WIN),
                                                     ALU.add)
                    last.then_inc(added_n, 1)

                def body(n, par):
                    more = there(n + 1)
                    if more:
                        padded(n + 1, 1 - par)
                    maximum(n, 0)
                    shift(n, 0)
                    maximum(n, 1)
                    if more:
                        right_side(n + 1, 1)
                    shift(n, 1)
                    sums(n, 0)
                    if more:
                        right_side(n + 1, 3)
                    inverse(n, 0)
                    if more:
                        values(n + 1, 1 - par, 0)
                    sums(n, 1)
                    inverse(n, 1)
                    if more:
                        for w in range(1, 4):
                            values(n + 1, 1 - par, w)
                    if sym(n) or n > 0:
                        add(n - 1)

                padded(0, 0)
                right_side(0, 1)
                right_side(0, 3)
                for w in range(4):
                    values(0, 0, w)
                images(eng, body)
                add(BATCH - 1)


def axial_weights(nc, s, a, sem):
    with ExitStack() as own:
        def tmp(name, shape, dt=F32):
            return own.enter_context(nc.sbuf_tensor(name, shape, dt))

        raw = tmp("proj_raw", [P, 4, HC])
        loads, kept, scaled, split_n = sem("proj_loads"), sem("kept_loads"), sem("proj_scaled"), sem("proj_split")
        with nc.Block() as block:
            @block.sync
            def _(eng):
                for i, n in enumerate(("q", "k", "g", "v")):
                    for half in range(2):
                        eng.dma_start(raw[half * C:(half + 1) * C, i, :], a[f"L1_attn_W{n}"]).then_inc(loads, 16)
                eng.dma_start(s.wo[:, :, :], a["L1_attn_Wo"].rearrange("(k p) n -> p k n", p=P)).then_inc(kept, 16)
                eng.dma_start(s.bo[:, :], a["L1_attn_bo"].partition_broadcast(P)).then_inc(kept, 16)
                for k in range(2):
                    eng.dma_start(s.bg[:, k:k + 1], a["L1_attn_bg"][k * P:(k + 1) * P].rearrange("(p o) -> p o", o=1)).then_inc(kept, 16)
                eng.dma_start(s.gamma[:, :], a["L1_attn_gamma"].partition_broadcast(P)).then_inc(kept, 16)
                eng.dma_start(s.beta[:, :], a["L1_attn_beta"].partition_broadcast(P)).then_inc(kept, 16)
                eng.wait_ge(kept, 16 * 6)
                eng.wait_ge(s.x1_in, 16 * 4)

            @block.scalar
            def _(eng):
                eng.wait_ge(scaled, 1)
                eng.activation(s.proj[0][:, :, :], raw[:, :, :], ACT.Copy).then_inc(split_n, 1)

            @block.vector
            def _(eng):
                eng.wait_ge(loads, 16 * 8)
                eng.tensor_scalar(raw[:, 0, :], raw[:, 0, :], D ** -0.5 * L ** -0.5, None, ALU.mult).then_inc(scaled, 1)
                eng.wait_ge(split_n, 1)
                eng.tensor_tensor(s.proj[1][:, :, :], raw[:, :, :], s.proj[0][:, :, :].bitcast(F32), ALU.subtract).then_inc(split_n, 1)


GROUP = 4
GTOK = GROUP * P
GROUPS = TILES // GROUP
PAIR = 2 * GROUP
PAIRS = GROUPS // 2
QUARTERS = 4
QTILES = TILES // QUARTERS


def sym(n):
    return not isinstance(n, int)


def wait(eng, semaphore, n):
    if sym(n) or n > 0:
        eng.wait_ge(semaphore, n)


def by_groups(eng, body):
    for g in range(2):
        body(g, g)
    with eng.Fori(1, GROUPS // 2) as i:
        for par in range(2):
            body(2 * i + par, par)


def ln_center(eng, mine, b, center_n):
    mine.then(eng.tensor_reduce(b.sum[:, :], b.x[:, :, :], AX.X, ALU.add))
    mine.then(eng.tensor_scalar(b.sum[:, :], b.sum[:, :], 1.0 / C, None, ALU.mult))
    eng.tensor_tensor(b.xc[:, :, :], b.x[:, :, :], b.sum[:, :].unsqueeze(2).to_broadcast([P, PAIR, C]), ALU.subtract).then_inc(center_n, 1)


def ln_variance(eng, mine, b, sq_n, sq_wait, var_n):
    eng.wait_ge(sq_n, sq_wait)
    mine.then(eng.tensor_reduce(b.var[:, :], b.sq[:, :, :], AX.X, ALU.add))
    eps = 1e-5
    eng.tensor_scalar(b.var[:, :], b.var[:, :], (1 + eps) / C, eps * eps, ALU.mult, ALU.add).then_inc(var_n, 1)


def ln_scale(eng, mine, b, roots_n, root_wait, center_n):
    eng.wait_ge(roots_n, root_wait)
    mine.then(eng.reciprocal(b.rstd[:, :], b.root[:, :]))
    newton(eng, mine, b.rstd[:, :], b.var[:, :], b.root[:, :])
    eng.wait_ge(center_n, root_wait)
    mine.then(eng.tensor_tensor(b.xc[:, :, :], b.xc[:, :, :], b.rstd[:, :].unsqueeze(2).to_broadcast([P, PAIR, C]), ALU.mult))


LN_STEPS = 9


class NormBuffers:

    def __init__(self, tmp, name):
        self.x = tmp(f"{name}_x", [P, PAIR, C])
        self.sum, self.var = tmp(f"{name}_sum", [P, PAIR]), tmp(f"{name}_var", [P, PAIR])
        self.rstd, self.root = tmp(f"{name}_rstd", [P, PAIR]), tmp(f"{name}_root", [P, PAIR])
        self.xc, self.sq = tmp(f"{name}_xc", [P, PAIR, C]), tmp(f"{name}_sq", [P, PAIR, C])
        self.hl = tmp(f"{name}_hl", [P, PAIR, P])


def axial_scores(nc, s, sem):
    with ExitStack() as own:
        def tmp(name, shape, dt=F32):
            return own.enter_context(nc.sbuf_tensor(name, shape, dt))

        b = NormBuffers(tmp, "ax")
        staged = [tmp(f"ax_staged{i}", [P, 4 * PAIR, BATCH]) for i in range(2)]
        qk = [tmp(f"ax_qk{i}", [P, 4, GROUP, BATCH, 8]) for i in range(2)]
        qkl = [tmp(f"ax_qkl{i}", [P, 4, 4, BATCH, 8]) for i in range(2)]
        zero = tmp("ax_zero", [P, 2 * P])
        att = tmp("ax_att", [P, 2, BATCH])
        attT = tmp("ax_attT", [P, 2, BATCH])
        top = tmp("ax_top", [P, 2])
        den = tmp("ax_den", [P, 2])

        def bank(name):
            return own.enter_context(nc.psum_tensor(name, [P, 512], F32))

        ps_f, ps_a = bank("ax_ps_f"), bank("ax_ps_a")
        ps_x = [bank(f"ax_ps_x{i}") for i in range(2)]
        ps_qk = [bank(f"ax_ps_qk{i}") for i in range(4)]
        staged_n, f_n, res_n, center_n, sq_n, var_n, root_n = (sem("ax_staged_n"), sem("ax_f_n"), sem("ax_res_n"), sem("ax_center_n"),
                                                               sem("ax_sq_n"), sem("ax_var_n"), sem("ax_root_n"))
        z_n, hi_n, lo_n, x_n, xt_n, dve_n = sem("ax_z_n"), sem("ax_hi_n"), sem("ax_lo_n"), sem("ax_x_n"), sem("ax_xt_n"), sem("ax_dve_n")
        qk_n, q_c, k_c, moved_n, att_n, zero_n = (sem("ax_qk_n"), sem("ax_q_copied"), sem("ax_k_copied"),
                                                  [sem(f"ax_moved{i}") for i in range(2)], sem("ax_att_n"), sem("ax_zero_n"))
        top_n, exp_n, kept_n = sem("ax_top_n"), sem("ax_exp_n"), sem("ax_kept_n")
        MOVES = 4 * GROUP

        def rounds(eng, body):
            for m in range(4):
                body(m, m % 2, m // 2, True, m > 0)
            with eng.Fori(2, PAIRS // 2) as i:
                for u in range(2):
                    body(2 * i + u, u, i, True, True)
            body(PAIRS, 0, PAIRS // 2, False, True)

        with nc.Block() as block:
            @block.gpsimd
            def _(eng):
                eng.memset(zero[:, :], 0.0).then_inc(zero_n, 1)
                eng.memset(s.att_w[:, :, :], 0.0).then_inc(zero_n, 1)
                eng.wait_ge(zero_n, 2)
                by_position = s.conv[:, :].rearrange("p (s l) -> p l s", l=L)

                def keep(m):
                    eng.wait_ge(res_n, m + 1)
                    eng.tensor_copy(s.x1[:, bass.ds(m * PAIR, PAIR), :], b.x[:, :, :]).then_inc(kept_n, 1)

                def body(m, par, half, norms, projects):
                    if norms:
                        wait(eng, f_n, m - 1)
                        eng.tensor_copy(staged[par][:, :, :], by_position[:, bass.ds(4 * PAIR * m, 4 * PAIR), :]).then_inc(staged_n, 1)
                    if projects:
                        keep(m - 1)
                rounds(eng, body)
                eng.wait_ge(kept_n, PAIRS)

            @block.sync
            def _(eng):
                def body(p, pb):
                    eng.wait_ge(q_c, 4 * p + 4)
                    eng.wait_ge(k_c, 4 * p + 4)
                    for h in range(4):
                        for t in range(GROUP):
                            eng.dma_start(qkl[pb][t * D:(t + 1) * D, :, h, :, :].rearrange("p k s l -> p k (s l)"),
                                          qk[pb][h * D:(h + 1) * D, :, t, :, :].rearrange("p k s l -> p k (s l)")).then_inc(moved_n[pb], 16)
                body(0, 0)
                body(1, 1)
                with eng.Fori(1, PAIRS // 2) as i:
                    for pb in range(2):
                        body(2 * i + pb, pb)

            @block.tensor
            def _(eng):
                eng.wait_ge(zero_n, 2)
                eng.matmul(ps_a[:, 0:2 * P], zero[:, 0:P], zero[:, :], start=True, stop=False, skip_group_check=True)

                def turn_conv(m, par):
                    eng.wait_ge(staged_n, m + 1)
                    wait(eng, res_n, m)
                    for t in range(PAIR):
                        last = eng.matmul(ps_f[:, t * C:(t + 1) * C], staged[par][:, 4 * t:4 * t + 4, :].rearrange("p l s -> p (l s)"),
                                          s.fold[:, :], start=True, stop=True)
                    last.then_inc(f_n, 1)

                def turn_x(p):
                    eng.wait_ge(lo_n, p + 1)
                    eng.wait_ge(hi_n, p + 1)
                    for j in range(2):
                        for t in range(GROUP):
                            last = eng.transpose(ps_x[j][:, t * P:(t + 1) * P], b.hl[:, j * GROUP + t, :], s.ident[:, :])
                        last.then_inc(x_n, 1)

                def project(g):
                    eng.wait_ge(xt_n, g + 1)
                    wait(eng, q_c, 2 * g)
                    wait(eng, k_c, 2 * g)
                    for m in range(4):
                        for k in range(2):
                            last = eng.matmul(ps_qk[m][:, :], s.proj[k][:, m // 2, (m % 2) * P:(m % 2 + 1) * P],
                                              s.xt[:, bass.ds(g * GTOK, GTOK)], start=(k == 0), stop=(k == 1))
                        last.then_inc(qk_n, 1)

                def scores(half, pb):
                    eng.wait_ge(moved_n[pb], 16 * MOVES * (half + 1))
                    for l in range(8):
                        for k in range(2):
                            last = eng.matmul(ps_a[:, k * P:(k + 1) * P], qkl[pb][:, k].rearrange("p h s l -> p (h s) l")[:, :, l],
                                              qkl[pb][:, 2 + k].rearrange("p h s l -> p (h s) l")[:, :, l],
                                              start=False, stop=False, skip_group_check=True)
                    last.then_inc(att_n, 1)

                def body(m, par, half, norms, projects):
                    if norms:
                        turn_conv(m, par)
                    if projects:
                        turn_x(m - 1)
                        project(2 * m - 2)
                    if sym(m) or m >= 3:
                        scores(half - 2 + par, 1 - par)
                    if projects:
                        project(2 * m - 1)
                rounds(eng, body)
                for pb in range(2):
                    scores(PAIRS // 2 - 1, pb)
                eng.matmul(ps_a[:, 0:2 * P], zero[:, 0:P], zero[:, :], start=False, stop=True, skip_group_check=True).then_inc(att_n, 1)

            def to_moved(pb, j, m):
                return qk[pb][:, m, :, :, 4 * j:4 * j + 4].rearrange("p t s l -> p t l s")

            def projected(m):
                return ps_qk[m][:, :].rearrange("p (t l s) -> p t l s", t=GROUP, l=4)

            @block.scalar
            def _(eng):
                def copy_q(p, pb, half, j):
                    if j == 0:
                        wait(eng, moved_n[pb], 16 * MOVES * half)
                    for m in range(2):
                        eng.wait_ge(qk_n, 8 * p + 4 * j + m + 1)
                        eng.activation(to_moved(pb, j, m), projected(m), ACT.Copy).then_inc(q_c, 1)

                def body(m, par, half, norms, projects):
                    if projects:
                        for j in range(2):
                            eng.wait_ge(x_n, 2 * m - 1 + j)
                            eng.activation(s.xt[:, bass.ds((2 * m - 2 + j) * GTOK, GTOK)], ps_x[j][:, :], ACT.Copy).then_inc(xt_n, 1)
                    if norms:
                        eng.wait_ge(center_n, m + 1)
                        eng.activation(b.sq[:, :, :], b.xc[:, :, :], ACT.Square).then_inc(sq_n, 1)
                    if projects:
                        copy_q(m - 1, 1 - par, half - 1 + par, 0)
                    if norms:
                        eng.wait_ge(var_n, m + 1)
                        eng.activation(b.root[:, :], b.var[:, :], ACT.Sqrt).then_inc(root_n, 1)
                    if projects:
                        copy_q(m - 1, 1 - par, half - 1 + par, 1)
                    if norms:
                        eng.wait_ge(z_n, m + 1)
                        wait(eng, x_n, 2 * m)
                        eng.activation(b.hl[:, :, 0:C].bitcast(F32R), b.xc[:, :, :], ACT.Copy).then_inc(hi_n, 1)
                rounds(eng, body)
                eng.wait_ge(top_n, 1)
                eng.activation(att[:, :, :], att[:, :, :], ACT.Exp).then_inc(exp_n, 1)

            @block.vector
            def _(eng):
                mine = Steps(eng, dve_n, LN_STEPS + 1)

                def copy_k(p, pb, half, j, m):
                    if j == 0 and m == 0:
                        wait(eng, moved_n[pb], 16 * MOVES * half)
                    eng.wait_ge(qk_n, 8 * p + 4 * j + m + 3)
                    eng.tensor_copy(to_moved(pb, j, 2 + m), projected(2 + m)).then_inc(k_c, 1)

                def body(m, par, half, norms, projects):
                    def copy(j, k):
                        if projects:
                            copy_k(m - 1, 1 - par, half - 1 + par, j, k)

                    if norms:
                        mine.round(m)
                        eng.wait_ge(f_n, m + 1)
                        wait(eng, kept_n, m)
                        eng.tensor_tensor(b.x[:, :, :], s.x1[:, bass.ds(m * PAIR, PAIR), :],
                                          ps_f[:, :].rearrange("p (t c) -> p t c", t=PAIR), ALU.add).then_inc(res_n, 1)
                        wait(eng, lo_n, m)
                        eng.wait_ge(res_n, m + 1)
                        ln_center(eng, mine, b, center_n)
                    copy(0, 0)
                    if norms:
                        ln_variance(eng, mine, b, sq_n, m + 1, var_n)
                    copy(0, 1)
                    if norms:
                        ln_scale(eng, mine, b, root_n, m + 1, center_n)
                    copy(1, 0)
                    wide = [P, PAIR, C]
                    if norms:
                        mine.then(eng.tensor_tensor(b.xc[:, :, :], b.xc[:, :, :], s.gamma[:, :].unsqueeze(1).to_broadcast(wide), ALU.mult))
                        eng.tensor_tensor(b.xc[:, :, :], b.xc[:, :, :], s.beta[:, :].unsqueeze(1).to_broadcast(wide), ALU.add).then_inc(z_n, 1)
                    copy(1, 1)
                    if norms:
                        eng.wait_ge(hi_n, m + 1)
                        eng.wait_ge(z_n, m + 1)
                        eng.tensor_tensor(b.hl[:, :, C:2 * C], b.xc[:, :, :], b.hl[:, :, 0:C], ALU.subtract).then_inc(lo_n, 1)
                rounds(eng, body)
                mine = Steps(eng, sem("ax_softmax_dve"))
                eng.wait_ge(att_n, PAIRS + 1)
                for h in range(4):
                    rows = slice(h * BATCH, (h + 1) * BATCH)
                    mine.did(eng.tensor_copy(att[rows, :, :], ps_a[rows, 0:2 * P].rearrange("p (k n) -> p k n", k=2)[:, :, rows]))
                mine.settle()
                mine.then(eng.tensor_reduce(top[:, :], att[:, :, :], AX.X, ALU.max))
                eng.tensor_tensor(att[:, :, :], att[:, :, :], top[:, :].unsqueeze(2).to_broadcast([P, 2, BATCH]), ALU.subtract).then_inc(top_n, 1)
                eng.wait_ge(exp_n, 1)
                mine.then(eng.tensor_reduce(den[:, :], att[:, :, :], AX.X, ALU.add))
                mine.then(eng.reciprocal(top[:, :], den[:, :]))
                mine.then(eng.tensor_tensor(att[:, :, :], att[:, :, :], top[:, :].unsqueeze(2).to_broadcast([P, 2, BATCH]), ALU.mult))
                mine.then(eng.transpose(attT[:, :, :].rearrange("p k s -> p (k s)"), att[:, :, :].rearrange("p k s -> p (k s)")))
                for h in range(4):
                    for q in range(4):
                        rows = slice(q * BATCH, (q + 1) * BATCH)
                        mine.did(eng.tensor_copy(s.att_w[rows, h::4, rows], attT[h * BATCH:(h + 1) * BATCH, :, :]))
                mine.settle()


def axial_values(nc, s, sem):
    with ExitStack() as own:
        def tmp(name, shape, dt=F32):
            return own.enter_context(nc.sbuf_tensor(name, shape, dt))

        xs = [tmp(f"av_x{i}", [P, GTOK], F32R) for i in range(2)]
        v = [tmp(f"av_v{i}", [P, GROUP, HC]) for i in range(2)]
        gate = [tmp(f"av_gate{i}", [P, 2, GTOK]) for i in range(2)]
        o = [tmp(f"av_o{i}", [P, GROUP, HC]) for i in range(2)]
        og = [tmp(f"av_og{i}", [P, 2, GTOK]) for i in range(2)]
        biased = tmp("av_biased", [P, GROUP, C])

        def bank(name):
            return own.enter_context(nc.psum_tensor(name, [P, 512], F32))

        ps_v, ps_o, ps_t = ([bank(f"av_ps_{n}{i}") for i in range(2)] for n in "vot")
        ps_r = bank("av_ps_r")
        xs_n, v_n, v_c, g_n, g_c, o_n, o_c = (sem(f"av_{n}") for n in ("x_staged", "v_done", "v_copied", "g_done", "g_copied", "o_done", "o_copied"))
        t_n, og_n, r_n, biased_n, res_n = (sem(f"av_{n}") for n in ("turned", "gated", "projected", "biased", "residual"))

        def rounds(eng, body):
            body(0, 0, True, False)
            body(1, 1, True, True)
            with eng.Fori(1, GROUPS // 2) as i:
                for par in range(2):
                    body(2 * i + par, par, True, True)
            body(GROUPS, 0, False, True)

        with nc.Block() as block:
            @block.gpsimd
            def _(eng):
                def body(g, par):
                    wait(eng, g_n, 2 * (g - par))
                    eng.tensor_copy(xs[par][:, :], s.xt[:, bass.ds(g * GTOK, GTOK)].bitcast(F32)).then_inc(xs_n, 1)
                by_groups(eng, body)

            @block.tensor
            def _(eng):
                def values(g, par):
                    eng.wait_ge(xs_n, g + 1)
                    wait(eng, g_c, 2 * g)
                    for t in range(GROUP):
                        for k in range(2):
                            last = eng.matmul(ps_v[t // 2][:, (t % 2) * HC:(t % 2 + 1) * HC], xs[par][:, t * P:(t + 1) * P],
                                              s.proj[k][:, 3, :], start=(k == 0), stop=(k == 1))
                        if t % 2:
                            last.then_inc(v_n, 1)

                def gates(g, par):
                    for m in range(2):
                        eng.wait_ge(v_c, 2 * g + m + 1)
                        for k in range(2):
                            last = eng.matmul(ps_v[m][:, :], s.proj[k][:, 2, m * P:(m + 1) * P], xs[par][:, :],
                                              start=(k == 0), stop=(k == 1))
                        last.then_inc(g_n, 1)

                def attend(g, par):
                    for h in range(HEADS):
                        if h % 4 == 0:
                            wait(eng, o_c, 2 * g - 1 + h // 4)
                        last = eng.matmul(ps_o[h // 4][:, (h % 4) * P:(h % 4 + 1) * P].rearrange("p (t c) -> p t c", t=GROUP),
                                          s.att_w[:, h, :], v[par][:, :, h * D:(h + 1) * D], start=True, stop=True)
                        if h % 4 == 3:
                            last.then_inc(o_n, 1)

                def turn(g, par):
                    for m in range(2):
                        eng.wait_ge(o_c, 2 * g + m + 1)
                        wait(eng, og_n, 2 * g - 1 + m)
                        for t in range(GROUP):
                            last = eng.transpose(ps_t[m][:, t * P:(t + 1) * P], o[par][:, t, m * P:(m + 1) * P], s.ident[:, :])
                        last.then_inc(t_n, 1)

                def project(g, par):
                    eng.wait_ge(og_n, 2 * g + 2)
                    wait(eng, biased_n, g)
                    for t in range(GROUP):
                        for m in range(2):
                            last = eng.matmul(ps_r[:, t * C:(t + 1) * C], og[par][:, m, t * P:(t + 1) * P], s.wo[:, m, :],
                                              start=(m == 0), stop=(m == 1))
                    last.then_inc(r_n, 1)

                def body(m, par, this, before):
                    if this:
                        values(m, par)
                    if before:
                        turn(m - 1, 1 - par)
                    if this:
                        gates(m, par)
                        attend(m, par)
                    if before:
                        project(m - 1, 1 - par)
                rounds(eng, body)

            @block.scalar
            def _(eng):
                def body(g, par, this, before):
                    if not this:
                        return
                    wait(eng, og_n, 2 * (g - par))
                    for m in range(2):
                        eng.wait_ge(g_n, 2 * g + m + 1)
                        eng.activation(gate[par][:, m, :], ps_v[m][:, :], ACT.Sigmoid, bias=s.bg[:, m:m + 1]).then_inc(g_c, 1)
                    wait(eng, t_n, 2 * (g - par))
                    for m in range(2):
                        eng.wait_ge(o_n, 2 * g + m + 1)
                        eng.activation(o[par][:, :, m * P:(m + 1) * P].rearrange("p t (h c) -> p h t c", c=D),
                                       ps_o[m][:, :].rearrange("p (h t c) -> p h t c", h=4, t=GROUP), ACT.Copy).then_inc(o_c, 1)
                rounds(eng, body)

            @block.vector
            def _(eng):
                def body(g, par, this, before):
                    if this:
                        for m in range(2):
                            eng.wait_ge(v_n, 2 * g + m + 1)
                            if m == 0:
                                wait(eng, o_n, 2 * (g - par))
                            eng.tensor_copy(v[par][:, 2 * m:2 * m + 2, :], ps_v[m][:, :].rearrange("p (t n) -> p t n", t=2)).then_inc(v_c, 1)
                    if before:
                        for m in range(2):
                            eng.wait_ge(t_n, 2 * g + m - 1)
                            eng.wait_ge(g_c, 2 * g + m - 1)
                            eng.tensor_tensor(og[1 - par][:, m, :], ps_t[m][:, :], gate[1 - par][:, m, :], ALU.mult).then_inc(og_n, 1)
                        eng.wait_ge(r_n, g)
                        wait(eng, res_n, g - 1)
                        eng.tensor_tensor(biased[:, :, :], ps_r[:, 0:GROUP * C].rearrange("p (t c) -> p t c", c=C),
                                          s.bo[:, :].unsqueeze(1).to_broadcast([P, GROUP, C]), ALU.add).then_inc(biased_n, 1)
                        eng.wait_ge(biased_n, g)
                        tiles = s.x1[:, bass.ds((g - 1) * GROUP, GROUP), :]
                        eng.tensor_tensor(tiles, tiles, biased[:, :, :], ALU.add).then_inc(res_n, 1)
                rounds(eng, body)


EXPERTS, HID = 8, 682
HCHUNK, HCHUNKS = 114, 6
HPAD = HCHUNK * HCHUNKS
SLOT = 512
FTILES = 2 * TOK // SLOT + EXPERTS - 1
SLOTS = FTILES * SLOT
EXPERT_ROWS = TOK // SLOT
R = SLOT // P
ROW = C + 2


def expert_weights(nc, s, a, sem):
    with ExitStack() as own:
        def tmp(name, shape, dt=F32):
            return own.enter_context(nc.sbuf_tensor(name, shape, dt))

        w13 = [tmp(f"w13_in{i}", [HCHUNK, 2, HCHUNKS, 2, C]) for i in range(2)]
        w2 = [tmp(f"w2_in{i}", [C, HPAD]) for i in range(2)]
        ps = [own.enter_context(nc.psum_tensor(f"ew_ps{i}", [P, 512], F32)) for i in range(6)]
        zeroed, in_n, turned, hi_n, lo_n, w2_n = (sem(f"ew_{n}") for n in ("zeroed", "loads", "turned", "hi", "lo", "w2"))
        in_n, sent, w2hi_n = [in_n, sem("ew_loads_odd")], sem("ew_tokens_sent"), sem("ew_w2_hi")
        LOADS = 2 * 2 * 2 + 1
        HALF = HCHUNKS // 2

        with nc.Block() as block:
            @block.gpsimd
            def _(eng):
                for i in range(2):
                    eng.memset(w13[i][:, :, HCHUNKS - 1], 0.0).then_inc(zeroed, 1)
                    eng.memset(w2[i][:, HID:HPAD], 0.0).then_inc(zeroed, 1)
                for t in range(TILES):
                    for k in range(2):
                        eng.indirect_dma_start(s.slot_x[:, :], bass.IndirectOffsetOnAxis(s.slot[k][:, t:t + 1], 0),
                                               s.rows[k][:, t, :], None).then_inc(sent, 16)
                eng.wait_ge(sent, 16 * 2 * TILES)

            @block.sync
            def _(eng):
                eng.wait_ge(zeroed, 4)
                whole = (HCHUNKS - 1) * HCHUNK
                for e in range(EXPERTS):
                    i = e % 2
                    if e >= 2:
                        eng.wait_ge(turned, 5 * (e - 1))
                    for m, name in enumerate(("w1", "w3")):
                        w = a[f"L1_ffn_{name}"][e]
                        for twice in range(2):
                            eng.dma_start(w13[i][:, m, 0:HCHUNKS - 1, twice, :],
                                          w[0:whole, :].rearrange("(k p) c -> p k c", p=HCHUNK)).then_inc(in_n[i], 16)
                            eng.dma_start(w13[i][0:HID - whole, m, HCHUNKS - 1, twice, :], w[whole:HID, :]).then_inc(in_n[i], 16)
                    eng.dma_start(w2[i][:, 0:HID], a["L1_ffn_w2"][e]).then_inc(in_n[i], 16)

            @block.tensor
            def _(eng):
                for e in range(EXPERTS):
                    i = e % 2
                    eng.wait_ge(in_n[i], 16 * LOADS * (e // 2 + 1))
                    for part in range(4):
                        m, half = divmod(part, 2)
                        if e >= 1:
                            eng.wait_ge(lo_n, 4 * (e - 1) + part + 1)
                        for k in range(HALF):
                            last = eng.transpose(ps[part][:, k * HCHUNK:(k + 1) * HCHUNK],
                                                 w13[i][:, m, half * HALF + k].rearrange("p a c -> p (a c)"), s.ident[0:HCHUNK, 0:HCHUNK])
                        last.then_inc(turned, 1)
                    if e >= 2:
                        eng.wait_ge(w2_n, e - 1)
                    for k in range(HCHUNKS):
                        last = eng.transpose(ps[4 + i][0:HCHUNK, k * C:(k + 1) * C], w2[i][:, k * HCHUNK:(k + 1) * HCHUNK], s.ident[0:C, 0:C])
                    last.then_inc(turned, 1)

            def halves(w, e, m, half):
                return w[:, e, m, half * HALF * HCHUNK:(half + 1) * HALF * HCHUNK]

            @block.scalar
            def _(eng):
                for e in range(EXPERTS):
                    for part in range(4):
                        eng.wait_ge(turned, 5 * e + part + 1)
                        eng.activation(halves(s.w13[0], e, *divmod(part, 2)), ps[part][:, 0:HALF * HCHUNK], ACT.Copy).then_inc(hi_n, 1)
                    eng.wait_ge(turned, 5 * e + 5)
                    eng.activation(s.w2[:, e, :, 0, :], ps[4 + e % 2][0:HCHUNK, 0:HCHUNKS * C].rearrange("p (k c) -> p k c", c=C),
                                   ACT.Copy).then_inc(w2hi_n, 1)

            @block.vector
            def _(eng):
                for e in range(EXPERTS):
                    for part in range(4):
                        eng.wait_ge(hi_n, 4 * e + part + 1)
                        eng.tensor_tensor(halves(s.w13[1], e, *divmod(part, 2)), ps[part][:, 0:HALF * HCHUNK],
                                          halves(s.w13[0], e, *divmod(part, 2)).bitcast(F32), ALU.subtract).then_inc(lo_n, 1)
                    eng.wait_ge(w2hi_n, e + 1)
                    eng.tensor_tensor(s.w2[:, e, :, 1, :], ps[4 + e % 2][0:HCHUNK, 0:HCHUNKS * C].rearrange("p (k c) -> p k c", c=C),
                                      s.w2[:, e, :, 0, :].bitcast(F32), ALU.subtract).then_inc(w2_n, 1)


def route(nc, s, a, sem):
    with ExitStack() as own:
        def tmp(name, shape, dt=F32):
            return own.enter_context(nc.sbuf_tensor(name, shape, dt))

        mean, var, rstd, root = (tmp(f"rt_{n}", [P, TILES]) for n in ("mean", "var", "rstd", "root_of_var"))
        sq = [tmp(f"rt_sq{i}", [P, QTILES, C]) for i in range(2)]
        hl = [tmp(f"rt_hl{i}", [P, QTILES, P]) for i in range(2)]
        xt = [tmp(f"rt_xt{i}", [P, GTOK]) for i in range(2)]
        probs, work = tmp("rt_probs", [P, TILES, EXPERTS]), tmp("rt_work", [P, TILES, EXPERTS])
        pick = [tmp(f"rt_pick{k}", [P, TILES, EXPERTS]) for k in range(2)]
        number = tmp("rt_number", [P, EXPERTS])
        best = [tmp(f"rt_best{k}", [P, TILES]) for k in range(2)]
        small = tmp("rt_small", [P, TILES])
        before, ones = tmp("rt_before", [P, P]), tmp("rt_ones", [P, P])
        total, ahead = tmp("rt_total", [P, EXPERTS, TILES]), tmp("rt_ahead", [P, EXPERTS, TILES])
        one_row = tmp("rt_one_row", [P, TILES])
        step = tmp("rt_step", [P, EXPERT_ROWS])
        over = tmp("rt_over", [P, EXPERTS, EXPERT_ROWS])
        count, end, start = tmp("rt_count", [P, EXPERTS]), tmp("rt_end", [P, EXPERTS]), tmp("rt_start", [P, EXPERTS])
        slot_f = tmp("rt_slot_f", [P, TILES])
        tile_no = tmp("rt_tile_no", [P, FTILES])
        past = tmp("rt_past", [P, FTILES, EXPERTS])
        owner = tmp("rt_owner", [P, FTILES])

        def bank(name):
            return own.enter_context(nc.psum_tensor(name, [P, 512], F32))

        ps_x, ps_l, ps_p, ps_c = [bank(f"rt_ps_x{i}") for i in range(2)], bank("rt_ps_l"), bank("rt_ps_p"), bank("rt_ps_c")
        center_n, sq_n, var_n, root_n, z_n, hi_n, lo_n, x_n, xt_n, l_n, twin_n = (
            sem(f"rt_{n}") for n in ("center", "sq", "var", "root", "z", "hi", "lo", "x", "xt", "logit", "second_rows"))
        const_n, max_n, exp_n, picked_n, ranked_n, slots_n, zero_n = (
            sem(f"rt_{n}") for n in ("const", "max", "exp", "picked", "ranked", "slots", "zero_slots"))
        rw_n = sem("rt_router_loads")
        filled_n, ids_n = sem("rt_filled"), sem("rt_ids")
        blank = tmp("rt_blank", [P, R, ROW])

        def quarter(q):
            return slice(q * QTILES, (q + 1) * QTILES)

        with nc.Block() as block:
            @block.sync
            def _(eng):
                for half in range(2):
                    eng.dma_start(s.router[half * C:(half + 1) * C, :], a["L1_ffn_router_w"].rearrange("e c -> c e"),
                                  allow_slow_non_contiguous=True).then_inc(rw_n, 16)
                eng.wait_ge(filled_n, 2)
                eng.dma_start(s.slot_x[:, :].rearrange("(k p r) c -> p k (r c)", p=P, r=R),
                              blank[:, :, :].rearrange("p r c -> p (r c)").unsqueeze(1).to_broadcast([P, FTILES, R * ROW])).then_inc(zero_n, 16)
                rows = s.summed[0:TOK, :].rearrange("(b g q) e -> q b g e", b=BATCH, q=4)
                for q in range(4):
                    eng.dma_start(rows[q], s.x1[q * BATCH:(q + 1) * BATCH, :, :]).then_inc(zero_n, 16)
                eng.dma_start(s.summed[TOK:TOK + SLOT, :].rearrange("(p r) c -> p r c", p=P), blank[:, :, 0:C]).then_inc(zero_n, 16)
                eng.wait_ge(zero_n, 16 * 6)

            @block.gpsimd
            def _(eng):
                eng.memset(blank[:, :, :], 0.0).then_inc(filled_n, 1)
                eng.wait_ge(filled_n, 1)
                for q in range(4):
                    wait(eng, ids_n, q)
                    eng.iota(s.rows[0][q * BATCH:(q + 1) * BATCH, :, C + 1].bitcast(mybir.dt.int32), pattern=[[4, TILES]], base=q,
                             channel_multiplier=L).then_inc(ids_n, 1)
                eng.wait_ge(ids_n, 4)
                eng.tensor_copy(s.rows[1][:, :, C + 1].bitcast(mybir.dt.int32), s.rows[0][:, :, C + 1].bitcast(mybir.dt.int32)).then_inc(ids_n, 1)
                eng.wait_ge(filled_n, 1)
                eng.iota(blank[:, :, C + 1].bitcast(mybir.dt.int32), pattern=[[1, R]], base=TOK, channel_multiplier=R).then_inc(filled_n, 1)
                eng.memset(ones[:, :], 1.0).then_inc(const_n, 1)
                eng.memset(one_row[:, :], 1.0).then_inc(const_n, 1)
                eng.wait_ge(const_n, 2)
                eng.affine_select(out=before[:, :], in_=ones[:, :], compare_op=ALU.is_gt, fill=0.0, base=0,
                                  pattern=[[1, P]], channel_multiplier=-1).then_inc(const_n, 1)
                for t, n, by in ((number, EXPERTS, 1), (step, EXPERT_ROWS, SLOT), (tile_no, FTILES, 1)):
                    eng.iota(t[:, :], pattern=[[by, n]], base=0, channel_multiplier=0,
                             allow_small_or_imprecise_dtypes=True).then_inc(const_n, 1)
                eng.wait_ge(ids_n, 5)

            @block.tensor
            def _(eng):
                eng.wait_ge(rw_n, 32)

                def logits(g):
                    eng.wait_ge(xt_n, g + 1)
                    for t in range(GROUP):
                        tile = g * GROUP + t
                        last = eng.matmul(ps_l[:, tile * EXPERTS:(tile + 1) * EXPERTS], xt[g % 2][:, t * P:(t + 1) * P], s.router[:, :],
                                          start=True, stop=True)
                    last.then_inc(l_n, 1)

                for g in range(GROUPS):
                    q, place = divmod(g, QTILES // GROUP)
                    if place == 0:
                        eng.wait_ge(hi_n, q + 1)
                        eng.wait_ge(lo_n, q + 1)
                    wait(eng, xt_n, g - 1)
                    for t in range(GROUP):
                        last = eng.transpose(ps_x[g % 2][:, t * P:(t + 1) * P], hl[q % 2][:, place * GROUP + t, :], s.ident[:, :])
                    last.then_inc(x_n, 1)
                    if g > 0:
                        logits(g - 1)
                logits(GROUPS - 1)
                eng.wait_ge(const_n, 3)
                eng.wait_ge(picked_n, 1)
                chosen = work[:, :, :].rearrange("p t e -> p (t e)")
                eng.matmul(ps_p[:, :], before[:, :], chosen, start=True, stop=True)
                eng.matmul(ps_c[:, :], ones[:, :], chosen, start=True, stop=True).then_inc(ranked_n, 1)

            @block.scalar
            def _(eng):
                def square(q):
                    wait(eng, var_n, q - 1)
                    eng.wait_ge(center_n, q + 1)
                    eng.activation(sq[q % 2][:, :, :], s.rows[0][:, quarter(q), 0:C], ACT.Square).then_inc(sq_n, 1)

                square(0)
                square(1)

                def across(g):
                    eng.wait_ge(x_n, g + 1)
                    wait(eng, l_n, g - 1)
                    eng.activation(xt[g % 2][:, :], ps_x[g % 2][:, :], ACT.Copy).then_inc(xt_n, 1)

                BY_QUARTER = QTILES // GROUP
                for q in range(QUARTERS):
                    if q > 0:
                        across((q - 1) * BY_QUARTER)
                    eng.wait_ge(var_n, q + 1)
                    eng.activation(root[:, quarter(q)], var[:, quarter(q)], ACT.Sqrt).then_inc(root_n, 1)
                    if q + 2 < QUARTERS:
                        square(q + 2)
                    if q > 0:
                        across((q - 1) * BY_QUARTER + 1)
                    eng.wait_ge(z_n, q + 1)
                    wait(eng, x_n, (q - 1) * BY_QUARTER)
                    eng.activation(hl[q % 2][:, :, 0:C].bitcast(F32R), s.rows[0][:, quarter(q), 0:C], ACT.Copy).then_inc(hi_n, 1)
                    eng.activation(s.rows[1][:, quarter(q), 0:C], s.rows[0][:, quarter(q), 0:C], ACT.Copy).then_inc(twin_n, 1)
                    if q > 0:
                        for g in range((q - 1) * BY_QUARTER + 2, q * BY_QUARTER):
                            across(g)
                for g in range((QUARTERS - 1) * BY_QUARTER, GROUPS):
                    across(g)
                eng.wait_ge(twin_n, QUARTERS)
                eng.wait_ge(max_n, 1)
                eng.activation(work[:, :, :], work[:, :, :], ACT.Exp).then_inc(exp_n, 1)

            @block.vector
            def _(eng):
                mine = Steps(eng, sem("rt_norm_dve"))

                def over_channels(t, q):
                    return t[:, quarter(q)].unsqueeze(2).to_broadcast([P, QTILES, C])

                def center(q):
                    x, m = s.x1[:, quarter(q), :], mean[:, quarter(q)]
                    mine.then(eng.tensor_reduce(m, x, AX.X, ALU.add))
                    mine.then(eng.tensor_scalar(m, m, 1.0 / C, None, ALU.mult))
                    eng.tensor_tensor(s.rows[0][:, quarter(q), 0:C], x, over_channels(mean, q), ALU.subtract).then_inc(center_n, 1)

                center(0)
                center(1)
                for q in range(QUARTERS):
                    v, r, t = var[:, quarter(q)], rstd[:, quarter(q)], root[:, quarter(q)]
                    eng.wait_ge(sq_n, q + 1)
                    mine.then(eng.tensor_reduce(v, sq[q % 2][:, :, :], AX.X, ALU.add))
                    eng.tensor_scalar(v, v, 1.0 / C, 1e-5, ALU.mult, ALU.add).then_inc(var_n, 1)
                    if q + 2 < QUARTERS:
                        center(q + 2)
                    eng.wait_ge(root_n, q + 1)
                    mine.then(eng.reciprocal(r, t))
                    newton(eng, mine, r, v, t)
                    eng.tensor_tensor(s.rows[0][:, quarter(q), 0:C], s.rows[0][:, quarter(q), 0:C], over_channels(rstd, q),
                                      ALU.mult).then_inc(z_n, 1)
                    eng.wait_ge(hi_n, q + 1)
                    eng.tensor_tensor(hl[q % 2][:, :, C:2 * C], s.rows[0][:, quarter(q), 0:C], hl[q % 2][:, :, 0:C],
                                      ALU.subtract).then_inc(lo_n, 1)
                logits = ps_l[:, :].rearrange("p (t e) -> p t e", e=EXPERTS)
                wide = [P, TILES, EXPERTS]
                mine = Steps(eng, sem("rt_pick_dve"))

                def over_experts(t):
                    return t[:, :].unsqueeze(2).to_broadcast(wide)

                def over_tokens(t):
                    return t[:, :].unsqueeze(1).to_broadcast(wide)

                eng.wait_ge(l_n, GROUPS)
                eng.wait_ge(const_n, 6)
                mine.then(eng.tensor_reduce(small[:, :], logits, AX.X, ALU.max))
                eng.tensor_tensor(work[:, :, :], logits, over_experts(small), ALU.subtract).then_inc(max_n, 1)
                eng.wait_ge(exp_n, 1)
                mine.then(eng.tensor_reduce(small[:, :], work[:, :, :], AX.X, ALU.add))
                mine.then(eng.reciprocal(small[:, :], small[:, :]))
                mine.then(eng.tensor_tensor(probs[:, :, :], work[:, :, :], over_experts(small), ALU.mult))
                for k in range(2):
                    mine.then(eng.tensor_reduce(best[k][:, :], probs[:, :, :], AX.X, ALU.max))
                    mine.then(eng.tensor_tensor(work[:, :, :], probs[:, :, :], over_experts(best[k]), ALU.is_lt))
                    mine.then(eng.tensor_scalar(work[:, :, :], work[:, :, :], float(EXPERTS), None, ALU.mult))
                    mine.then(eng.tensor_tensor(work[:, :, :], work[:, :, :], over_tokens(number), ALU.add))
                    mine.then(eng.tensor_reduce(small[:, :], work[:, :, :], AX.X, ALU.min))
                    mine.then(eng.tensor_tensor(pick[k][:, :, :], over_tokens(number), over_experts(small), ALU.is_equal))
                    if k == 0:
                        mine.then(eng.tensor_scalar(work[:, :, :], pick[0][:, :, :], 2.0, None, ALU.mult))
                        mine.then(eng.tensor_tensor(probs[:, :, :], probs[:, :, :], work[:, :, :], ALU.subtract))
                eng.tensor_tensor(work[:, :, :], pick[0][:, :, :], pick[1][:, :, :], ALU.add).then_inc(picked_n, 1)
                mine.then(eng.tensor_tensor(small[:, :], best[0][:, :], best[1][:, :], ALU.add))
                mine.then(eng.tensor_scalar(small[:, :], small[:, :], 1e-9, None, ALU.add))
                mine.then(eng.reciprocal(small[:, :], small[:, :]))
                for k in range(2):
                    mine.did(eng.tensor_tensor(s.rows[k][:, :, C], best[k][:, :], small[:, :], ALU.mult))
                eng.wait_ge(ranked_n, 1)
                mine.then(eng.tensor_copy(total[:, :, :], ps_c[:, :].rearrange("p (t e) -> p e t", e=EXPERTS)))
                for e in range(EXPERTS):
                    mine.did(eng.tensor_tensor_scan(ahead[:, e, :], one_row[:, :], total[:, e, :], 0.0, ALU.mult, ALU.add))
                mine.settle()
                mine.then(eng.tensor_tensor(over[:, :, :], ahead[:, :, TILES - 1:TILES].to_broadcast([P, EXPERTS, EXPERT_ROWS]),
                                            step[:, :].unsqueeze(1).to_broadcast([P, EXPERTS, EXPERT_ROWS]), ALU.is_gt))
                mine.then(eng.tensor_reduce(count[:, :], over[:, :, :], AX.X, ALU.add))
                mine.then(eng.tensor_tensor_scan(end[:, :], one_row[:, 0:EXPERTS], count[:, :], 0.0, ALU.mult, ALU.add))
                mine.then(eng.tensor_tensor(start[:, :], end[:, :], count[:, :], ALU.subtract))
                mine.then(eng.tensor_scalar(start[:, :], start[:, :], float(SLOT), None, ALU.mult))
                mine.then(eng.tensor_tensor(ahead[:, :, :], ahead[:, :, :], total[:, :, :], ALU.subtract))
                mine.then(eng.tensor_tensor(ahead[:, :, :], ahead[:, :, :], start[:, :].unsqueeze(2).to_broadcast([P, EXPERTS, TILES]), ALU.add))
                mine.then(eng.tensor_tensor(probs[:, :, :], ps_p[:, :].rearrange("p (t e) -> p t e", e=EXPERTS),
                                            ahead[:, :, :].rearrange("p e t -> p t e"), ALU.add))
                for k in range(2):
                    mine.then(eng.tensor_tensor(work[:, :, :], probs[:, :, :], pick[k][:, :, :], ALU.mult))
                    mine.then(eng.tensor_reduce(slot_f[:, :], work[:, :, :], AX.X, ALU.add))
                    eng.tensor_copy(s.slot[k][:, :], slot_f[:, :]).then_inc(slots_n, 1)
                    eng.wait_ge(slots_n, k + 1)
                mine.then(eng.tensor_tensor(past[:, :, :], tile_no[:, :].unsqueeze(2).to_broadcast([P, FTILES, EXPERTS]),
                                            end[:, :].unsqueeze(1).to_broadcast([P, FTILES, EXPERTS]), ALU.is_ge))
                mine.then(eng.tensor_reduce(owner[:, :], past[:, :, :], AX.X, ALU.add))
                mine.then(eng.tensor_scalar(owner[:, :], owner[:, :], float(EXPERTS - 1), None, ALU.min))
                mine.then(eng.tensor_copy(s.owner[:, :], owner[:, :]))


def experts(nc, s, sem):
    with ExitStack() as own:
        def tmp(name, shape, dt=F32):
            return own.enter_context(nc.sbuf_tensor(name, shape, dt))

        I32, U32 = mybir.dt.int32, mybir.dt.uint32
        x = [tmp(f"ex_x{i}", [P, R, ROW]) for i in range(4)]
        gate = [tmp(f"ex_gate{i}", [P, R]) for i in range(4)]
        number = [tmp(f"ex_number{i}", [P, R], I32) for i in range(4)]
        hl = tmp("ex_hl", [P, R, P])
        xt = [tmp(f"ex_xt{i}", [P, SLOT], F32R) for i in range(2)]
        w13 = [[tmp(f"ex_w13_{i}{k}", [P, 2, HPAD], F32R) for k in range(2)] for i in range(2)]
        w2 = [tmp(f"ex_w2_{i}", [HCHUNK, HCHUNKS, 2 * C], F32R) for i in range(2)]
        act = [tmp(f"ex_act{i}", [HCHUNK, SLOT]) for i in range(2)]
        hf = [tmp(f"ex_hf{i}", [HCHUNK, SLOT]) for i in range(3)]
        h = [tmp(f"ex_h{k}", [HCHUNK, HCHUNKS, SLOT], F32R) for k in range(2)]
        y = tmp("ex_y", [P, SLOT])
        out = [tmp(f"ex_out{i}", [P, R, C]) for i in range(2)]

        def bank(name):
            return own.enter_context(nc.psum_tensor(name, [P, 512], F32))

        ps_x, ps_o = bank("ex_ps_x"), bank("ex_ps_o")
        ps_y, ps_1, ps_3 = ([bank(f"ex_ps_{n}{i}") for i in range(2)] for n in "y13")
        x_in = [sem(f"ex_x_in{i}") for i in range(4)]
        hi_n, lo_n, x_n, xt_n, w13_n, w2_n, h1_n, h3_n, act_n, h_n, hhi_n, y_n, yc_n, o_n, oc_n = (
            sem(f"ex_{n}") for n in ("hi", "lo", "x", "xt", "w13", "w2", "h1", "h3", "act", "h", "h_hi", "y", "y_copied", "o", "o_copied"))
        hlo_v, hlo_p = sem("ex_h_lo_vector"), sem("ex_h_lo_gpsimd")
        BY_GPSIMD = (0, HCHUNKS - 1)
        BY_VECTOR = tuple(c for c in range(HCHUNKS) if c not in BY_GPSIMD)

        def wait_lower(eng, k, c):
            if c in BY_GPSIMD:
                wait(eng, hlo_p, len(BY_GPSIMD) * k + BY_GPSIMD.index(c) + 1)
            else:
                wait(eng, hlo_v, len(BY_VECTOR) * k + BY_VECTOR.index(c) + 1)

        added = sem("ex_added")
        slot_x = s.slot_x[:, :].rearrange("(k p r) c -> k p r c", p=P, r=R)
        LAST = FTILES - 1
        ROUNDS = (FTILES - 4 - 1) // 4

        def run(eng, body, rounds=ROUNDS):
            for k in range(4):
                body(k, k, 0)
            with eng.Fori(1, rounds + 1) as i:
                for u in range(4):
                    body(4 * i + u, u, i)
            for k in range(4 + 4 * rounds, FTILES):
                body(k, k % 4, k // 4)

        def after(k, n):
            return sym(k) or k >= n

        def before_last(k):
            return sym(k) or k < LAST

        with nc.Block() as block:
            @block.sync
            def _(eng):
                def load(k, buf):
                    eng.dma_start(x[buf][:, :, :], slot_x[bass.ds(k, 1)].rearrange("o p r c -> (o p) r c")).then_inc(x_in[buf], 16)

                def body(k, buf, quarter):
                    if sym(k) or k + 4 <= LAST:
                        eng.wait_ge(lo_n, k + 1)
                        load(k + 4, buf)
                for k in range(4):
                    load(k, k)
                run(eng, body, ROUNDS - 1)

            @block.gpsimd
            def _(eng):
                def h_lower(k, c):
                    eng.wait_ge(hhi_n, HCHUNKS * k + c + 1)
                    eng.tensor_tensor(h[1][:, c, :], hf[c % 3][:, :], h[0][:, c, :].bitcast(F32), ALU.subtract).then_inc(hlo_p, 1)

                def wait_result(k):
                    wait(eng, added, 16 * R * k)
                    eng.wait_ge(oc_n, k + 1)

                def scatter(k, buf):
                    for j in range(R):
                        eng.indirect_dma_start(s.summed[:, :], bass.IndirectOffsetOnAxis(number[buf][:, j:j + 1].bitcast(U32), 0),
                                               out[buf % 2][:, j, :], None, compute_op=ALU.add).then_inc(added, 16)

                def body(k, buf, quarter):
                    if after(k, 1):
                        h_lower(k - 1, HCHUNKS - 1)
                    if after(k, 2):
                        wait_result(k - 2)
                    h_lower(k, 0)
                    if after(k, 2):
                        scatter(k - 2, (buf - 2) % 4)
                run(eng, body)
                h_lower(LAST, HCHUNKS - 1)
                for k in (LAST - 1, LAST):
                    wait_result(k)
                    scatter(k, k % 4)
                eng.wait_ge(added, 16 * R * FTILES)

            @block.tensor
            def _(eng):
                def turn_in(k):
                    eng.wait_ge(hi_n, k + 1)
                    eng.wait_ge(lo_n, k + 1)
                    wait(eng, xt_n, k)
                    for r in range(R):
                        last = eng.transpose(ps_x[:, r * P:(r + 1) * P], hl[:, r, :], s.ident[:, :])
                    last.then_inc(x_n, 1)

                def turn_out(k):
                    eng.wait_ge(yc_n, k + 1)
                    wait(eng, oc_n, k)
                    for r in range(R):
                        last = eng.matmul(ps_o[:, r * C:(r + 1) * C], y[:, r * P:(r + 1) * P], s.fold[:, :], start=True, stop=True)
                    last.then_inc(o_n, 1)

                def hidden(k, par, c):
                    if c == 0:
                        eng.wait_ge(xt_n, k + 1)
                    for m, (ps, done, free) in enumerate(((ps_1, h1_n, act_n), (ps_3, h3_n, h_n))):
                        if c == 0:
                            eng.wait_ge(w13_n, 4 * k + 2 * m + 2)
                        wait(eng, free, HCHUNKS * k + c - 1)
                        for j in range(2):
                            last = eng.matmul(ps[c % 2][0:HCHUNK, :], w13[par][j][:, m, c * HCHUNK:(c + 1) * HCHUNK], xt[par][:, :],
                                              start=(j == 0), stop=(j == 1))
                        last.then_inc(done, 1)

                def product(k, par, c):
                    if c == 0:
                        eng.wait_ge(w2_n, k + 1)
                        wait(eng, yc_n, k - 1)
                    wait_lower(eng, k, c)
                    for j in range(2):
                        last = eng.matmul(ps_y[par][:, :], w2[par][:, c, :], h[j][:, c, :], start=(c == 0 and j == 0),
                                          stop=(c == HCHUNKS - 1 and j == 1))
                    if c == HCHUNKS - 1:
                        last.then_inc(y_n, 1)

                def body(k, buf, quarter):
                    par = buf % 2
                    for c in range(HCHUNKS):
                        if after(k, 1):
                            product(k - 1, 1 - par, c)
                        hidden(k, par, c)
                        if c == 1 and after(k, 2):
                            turn_out(k - 2)
                        if c == 4 and before_last(k):
                            turn_in(k + 1)
                turn_in(0)
                run(eng, body)
                turn_out(LAST - 1)
                for c in range(HCHUNKS):
                    product(LAST, LAST % 2, c)
                turn_out(LAST)

            @block.scalar
            def _(eng):
                def upper(k, buf, quarter):
                    eng.wait_ge(x_in[buf], 16 * (quarter + 1))
                    wait(eng, x_n, k)
                    eng.activation(hl[:, :, 0:C].bitcast(F32R), x[buf][:, :, 0:C], ACT.Copy).then_inc(hi_n, 1)

                def across(k, par):
                    eng.wait_ge(x_n, k + 1)
                    eng.activation(xt[par][:, :], ps_x[:, :], ACT.Copy).then_inc(xt_n, 1)

                def weights(k, par):
                    e = eng.value_load(s.owner[0:1, bass.ds(k, 1)], min_val=0, max_val=EXPERTS - 1)
                    eng.activation(w2[par][:, :, :], s.w2[:, bass.ds(e, 1)].rearrange("p o k a c -> p (o k) (a c)").bitcast(F32),
                                   ACT.Copy).then_inc(w2_n, 1)

                def h_upper(k, c):
                    eng.wait_ge(h_n, HCHUNKS * k + c + 1)
                    eng.activation(h[0][:, c, :], hf[c % 3][:, :], ACT.Copy).then_inc(hhi_n, 1)

                def copy_y(k, par):
                    eng.wait_ge(y_n, k + 1)
                    wait(eng, o_n, k)
                    eng.activation(y[:, :], ps_y[par][:, :], ACT.Copy).then_inc(yc_n, 1)

                def body(k, buf, quarter):
                    par = buf % 2
                    for c in range(HCHUNKS):
                        if c == HCHUNKS - 1 and before_last(k):
                            across(k + 1, 1 - par)
                        eng.wait_ge(h1_n, HCHUNKS * k + c + 1)
                        wait(eng, h_n, HCHUNKS * k + c - 1)
                        eng.activation(act[c % 2][:, :], ps_1[c % 2][0:HCHUNK, :], ACT.Silu).then_inc(act_n, 1)
                        if c >= 1:
                            h_upper(k, c - 1)
                        elif after(k, 1):
                            h_upper(k - 1, HCHUNKS - 1)
                        if c == 3:
                            weights(k, par)
                        if c == 1 and before_last(k):
                            upper(k + 1, (buf + 1) % 4, quarter + (buf + 1) // 4)
                    if after(k, 1):
                        copy_y(k - 1, 1 - par)
                upper(0, 0, 0)
                across(0, 0)
                run(eng, body)
                h_upper(LAST, HCHUNKS - 1)
                copy_y(LAST, LAST % 2)

            @block.vector
            def _(eng):
                def weights(k, par, parts):
                    for j, m in parts:
                        eng.tensor_scalar(w13[par][j][:, m, :], s.w13[j][:, bass.ds(e_of[0], 1), m, :].rearrange("p o n -> p (o n)").bitcast(F32),
                                          1.0, None, ALU.mult).then_inc(w13_n, 1)

                def lower(k, buf):
                    wait(eng, added, 16 * R * (k - 3))
                    eng.wait_ge(hi_n, k + 1)
                    eng.tensor_copy(gate[buf][:, :], x[buf][:, :, C])
                    eng.tensor_copy(number[buf][:, :], x[buf][:, :, C + 1].bitcast(I32))
                    wait(eng, x_n, k)
                    eng.tensor_tensor(hl[:, :, C:2 * C], x[buf][:, :, 0:C], hl[:, :, 0:C], ALU.subtract).then_inc(lo_n, 1)

                def h_lower(k, c):
                    eng.wait_ge(hhi_n, HCHUNKS * k + c + 1)
                    eng.tensor_tensor(h[1][:, c, :], hf[c % 3][:, :], h[0][:, c, :].bitcast(F32), ALU.subtract).then_inc(hlo_v, 1)

                def result(k, buf):
                    eng.wait_ge(o_n, k + 1)
                    wait(eng, added, 16 * R * (k - 1))
                    eng.tensor_tensor(out[buf % 2][:, :, :], ps_o[:, 0:R * C].rearrange("p (r c) -> p r c", c=C),
                                      gate[buf][:, :].unsqueeze(2).to_broadcast([P, R, C]), ALU.mult).then_inc(oc_n, 1)

                PARTS = [(j, m) for m in range(2) for j in range(2)]
                e_of = [eng.value_load(s.owner[0:1, 0:1], min_val=0, max_val=EXPERTS - 1)]
                weights(0, 0, PARTS)
                lower(0, 0)

                def body(k, buf, quarter):
                    if before_last(k):
                        e_of[0] = eng.value_load(s.owner[0:1, bass.ds(k + 1, 1)], min_val=0, max_val=EXPERTS - 1)
                    for c in range(HCHUNKS):
                        eng.wait_ge(act_n, HCHUNKS * k + c + 1)
                        eng.wait_ge(h3_n, HCHUNKS * k + c + 1)
                        if c >= 3:
                            wait_lower(eng, k, c - 3)
                        elif after(k, 1):
                            wait_lower(eng, k - 1, c + 3)
                        eng.tensor_tensor(hf[c % 3][:, :], act[c % 2][:, :], ps_3[c % 2][0:HCHUNK, :], ALU.mult).then_inc(h_n, 1)
                        if c - 1 in BY_VECTOR:
                            h_lower(k, c - 1)
                        if before_last(k) and c in (0, 1, 3, 4):
                            weights(k + 1, (buf + 1) % 2, [PARTS[(0, 1, 3, 4).index(c)]])
                        if c == 1 and after(k, 2):
                            result(k - 2, (buf - 2) % 4)
                        if c == 2 and before_last(k):
                            lower(k + 1, (buf + 1) % 4)
                run(eng, body)
                result(LAST - 1, (LAST - 1) % 4)
                result(LAST, LAST % 4)


def finish(nc, s, out, sem):
    copied = sem("output_copied")
    with nc.Block() as block:
        @block.sync
        def _(eng):
            eng.dma_start(out.rearrange("b r c e -> (b r c) e"), s.summed[0:TOK, :]).then_inc(copied, 16)
            eng.wait_ge(copied, 16)


def hybrid_block(nc, a, out):
    with ExitStack() as ctx:
        def sem(name):
            return ctx.enter_context(nc.semaphore(name))

        s = allocate(nc, ctx)
        constants(nc, s, sem)
        with ExitStack() as upto_layer2:
            def sb(name, shape, dt=F32):
                return upto_layer2.enter_context(nc.sbuf_tensor(name, shape, dt))

            s.conv = sb("conv_out", [P, TOK])
            with ExitStack() as layer1:
                s.xhl = layer1.enter_context(nc.sbuf_tensor("gn_hl", [P, TILES, P], F32))
                s.gn_x, s.gn_x_in = layer1.enter_context(nc.sbuf_tensor("gn_x", [P, TILES, C], F32)), sem("gn_x_in")
                s.x1_in = sem("residual_in")
                conv_weights(nc, layer1, s, a, sem)
                group_norm(nc, s, sem)
                conv_attention(nc, s, a, sem)
            s.xt = sb("norm_T", [P, TOK], F32R)
            s.proj = [sb(f"proj{k}", [P, 4, HC], F32R) for k in range(2)]
            s.wo, s.bo, s.bg = sb("wo_sb", [P, 2, C]), sb("bo_sb", [P, C]), sb("bg_sb", [P, 2])
            s.gamma, s.beta = sb("gamma_sb", [P, C]), sb("beta_sb", [P, C])
            s.att_w = sb("att_w", [P, HEADS, P])
            axial_weights(nc, s, a, sem)
            axial_scores(nc, s, sem)
            axial_values(nc, s, sem)

        def sb(name, shape, dt=F32):
            return ctx.enter_context(nc.sbuf_tensor(name, shape, dt))

        s.slot = [sb(f"slot{k}", [P, TILES], mybir.dt.uint32) for k in range(2)]
        s.owner = sb("owner", [P, FTILES], mybir.dt.int32)
        s.router = sb("router", [P, EXPERTS])
        s.w13 = [sb(f"w13_{k}", [P, EXPERTS, 2, HPAD], F32R) for k in range(2)]
        s.w2 = sb("w2_sb", [HCHUNK, EXPERTS, HCHUNKS, 2, C], F32R)
        s.slot_x = nc.dram_tensor("slot_x", [SLOTS, ROW], F32, kind="Internal").ap()
        s.summed = nc.dram_tensor("summed", [TOK + SLOT, C], F32, kind="Internal").ap()
        with ExitStack() as dispatch:
            s.rows = [dispatch.enter_context(nc.sbuf_tensor(f"rows{k}", [P, TILES, ROW], F32)) for k in range(2)]
            route(nc, s, a, sem)
            expert_weights(nc, s, a, sem)
        experts(nc, s, sem)
        finish(nc, s, out, sem)


_INS = ['x', 'L0_conv_w_q', 'L0_conv_w_k', 'L0_conv_w_v', 'L0_conv_w_local', 'L0_conv_b_local', 'L0_conv_w_out',
        'L0_conv_b_out', 'L1_attn_gamma', 'L1_attn_beta', 'L1_attn_Wq', 'L1_attn_Wk', 'L1_attn_Wv', 'L1_attn_Wg',
        'L1_attn_bg', 'L1_attn_Wo', 'L1_attn_bo', 'L1_ffn_router_w', 'L1_ffn_w1', 'L1_ffn_w2', 'L1_ffn_w3']
_OUTS = [((BATCH, SIDE, SIDE, C), 'float32')]


def kernel(**inputs):
    import numpy as _np
    import concourse.bacc as _bacc
    from concourse import mybir as _mybir
    from concourse.bass_utils import run_bass_kernel_spmd as _run

    nc = _bacc.Bacc("TRN2", target_bir_lowering=False, num_devices=1)
    arrays, args = {}, {}
    for name in _INS:
        arr = _np.ascontiguousarray(inputs[name])
        arrays[f"in_{name}_dram"] = arr
        args[name] = nc.dram_tensor(f"in_{name}_dram", arr.shape, _mybir.dt.from_np(arr.dtype), kind="ExternalInput").ap()
    shape, dtype = _OUTS[0]
    out = nc.dram_tensor("out_0_dram", shape, _mybir.dt.from_np(_np.dtype(dtype)), kind="ExternalOutput").ap()
    hybrid_block(nc, args, out)
    r = _run(nc, [arrays], core_ids=[0])
    return r.results[0]["out_0_dram"]
```
